# Optimizing a Trainium2 kernel written in Bass

```python
import numpy as np
import jax
import jax.numpy as jnp

def _softmax(x, axis=-1):
    return jax.nn.softmax(x, axis=axis)

def _gelu(x):
    return jax.nn.gelu(x, approximate=True)

def _silu(x):
    return jax.nn.silu(x)

def _sigmoid(x):
    return jax.nn.sigmoid(x)

def _layernorm(x, axis=-1, eps=1e-05):
    m = jnp.mean(x, axis=axis, keepdims=True)
    v = jnp.var(x, axis=axis, keepdims=True)
    return (x - m) / jnp.sqrt(v + eps)

def _scatter_add(tgt, idx, src, axis=0):
    return tgt.at[idx].add(src)

def _segment_sum(src, seg, n):
    return jax.ops.segment_sum(src, seg, n)
kernel_name = 'mk_xattn_ffn_d2_seqx_r4_804a04'

def setup_inputs(seed: int=0):
    np.random.seed(seed)
    _w = jnp.asarray

    def _rec_inputs():
        import jax
        import jax.numpy as jnp
        _rk = jax.random.key(seed)
        x = -0.0002928 + 1 * jax.random.normal(jax.random.fold_in(_rk, 1), (4, 512, 256), jnp.float32)
        _lenS = 512 - jax.random.randint(jax.random.fold_in(_rk, 7), (4,), 0, max(1, 512 // 4) + 1, jnp.int32)
        _lenS2 = 512 - jax.random.randint(jax.random.fold_in(_rk, 8), (4,), 0, max(1, 512 // 4) + 1, jnp.int32)
        _ctx_1024P = jax.random.normal(jax.random.fold_in(_rk, 11), (4, 16, 256), jnp.float32)
        _ctx_1024c = jax.random.dirichlet(jax.random.fold_in(_rk, 511), 0.3 * jnp.ones((16,), jnp.float32), (4, 512))
        _ctx_1024t = jnp.einsum('bsk,bkd->bsd', _ctx_1024c, _ctx_1024P)
        _ctx_1024t = _ctx_1024t * jax.lax.rsqrt(jnp.mean(jnp.square(_ctx_1024t)) + 1e-12) * 0.953939
        ctx_1024 = -1.39393e-06 + 0.999914 * (_ctx_1024t + 0.3 * jax.random.normal(jax.random.fold_in(_rk, 611), (4, 512, 256), jnp.float32))
        _validS = jnp.arange(512)[None, :] < _lenS[:, None]
        _validS2 = jnp.arange(512)[None, :] < _lenS2[:, None]
        _causal = jnp.tril(jnp.ones((512, 512), dtype=bool))
        mask_Bx16xSxS2_ff0 = jnp.where(jnp.ones((4, 16, 512, 512), dtype=bool), 0.0, -1000000000.0).astype(jnp.float32)
        return (x, ctx_1024, mask_Bx16xSxS2_ff0)
    x, ctx_1024, mask_Bx16xSxS2_ff0 = _rec_inputs()

    def _L0_xattn_setup():
        import jax, jax.numpy as jnp
        import numpy as np
        B, S, D = (2, 512, 256)
        H = 16
        DH = D // H
        LAMBDA_INIT = 0.8
        EPS = 1e-05
        SCALE = 1.0 / np.sqrt(DH)
        key = jax.random.key(seed)
        ks = jax.random.split(key, 13)
        inp = {'query': jax.random.normal(ks[0], (B, S, D), jnp.float32), 'key': jax.random.normal(ks[1], (B, S, D), jnp.float32), 'value': jax.random.normal(ks[2], (B, S, D), jnp.float32), 'attn_mask': jnp.zeros((B, H, S, S), jnp.float32), 'W_q': jax.random.normal(ks[3], (D, 2 * DH * H), jnp.float32) * 0.02, 'W_k': jax.random.normal(ks[4], (D, 2 * DH * H), jnp.float32) * 0.02, 'W_v': jax.random.normal(ks[5], (D, DH * H), jnp.float32) * 0.02, 'W_o': jax.random.normal(ks[6], (DH * H, D), jnp.float32) * 0.02, 'lambda_q1': jax.random.normal(ks[7], (H, DH), jnp.float32) * 0.1, 'lambda_k1': jax.random.normal(ks[8], (H, DH), jnp.float32) * 0.1, 'lambda_q2': jax.random.normal(ks[9], (H, DH), jnp.float32) * 0.1, 'lambda_k2': jax.random.normal(ks[10], (H, DH), jnp.float32) * 0.1, 'rms_scale': jnp.ones((DH,), jnp.float32)}
        return inp
    _L0_xattn_all = _L0_xattn_setup()
    _L0_xattn_in = {k: v for k, v in _L0_xattn_all.items() if k in ('W_q', 'W_k', 'W_v', 'W_o', 'lambda_q1', 'lambda_k1', 'lambda_q2', 'lambda_k2', 'rms_scale')}
    del _L0_xattn_all

    def _L0_ffn_setup():
        import jax, jax.numpy as jnp
        import numpy as np
        D_MODEL = 256
        D_FF = 1024
        N_EXPERTS = 8
        INIT_SCALE = 0.1

        def _trunc_normal(key, shape, std):
            return std * jax.random.truncated_normal(key, -2.0, 2.0, shape, dtype=jnp.float32)
        key = jax.random.key(seed)
        ks = jax.random.split(key, 5)
        x = jax.random.normal(ks[0], (4, 256, D_MODEL), dtype=jnp.float32)
        router_W = _trunc_normal(ks[1], (D_MODEL, N_EXPERTS), INIT_SCALE / np.sqrt(D_MODEL))
        router_b = jnp.zeros((N_EXPERTS,), dtype=jnp.float32)
        W1 = _trunc_normal(ks[2], (N_EXPERTS, D_MODEL, D_FF), INIT_SCALE / np.sqrt(D_MODEL))
        b1 = jnp.zeros((N_EXPERTS, D_FF), dtype=jnp.float32)
        W2 = _trunc_normal(ks[3], (N_EXPERTS, D_FF, D_MODEL), INIT_SCALE / np.sqrt(D_FF))
        b2 = jnp.zeros((N_EXPERTS, D_MODEL), dtype=jnp.float32)
        return {'x': x, 'router_W': router_W, 'router_b': router_b, 'W1': W1, 'b1': b1, 'W2': W2, 'b2': b2}
    _L0_ffn_all = _L0_ffn_setup()
    _L0_ffn_in = {k: v for k, v in _L0_ffn_all.items() if k in ('router_W', 'router_b', 'W1', 'b1', 'W2', 'b2')}
    del _L0_ffn_all

    def _L1_xattn_setup():
        import jax, jax.numpy as jnp
        import numpy as np
        DIM = 256
        H = 16
        D = 64
        INNER = H * D
        EPS = 1e-05

        def layernorm(x, w, b):
            mu = jnp.mean(x, axis=-1, keepdims=True)
            var = jnp.var(x, axis=-1, keepdims=True)
            return (x - mu) * jax.lax.rsqrt(var + EPS) * w + b
        key = jax.random.key(seed)
        ks = jax.random.split(key, 8)
        B, N, S = (4, 64, 2048)
        s = 1.0 / np.sqrt(DIM)
        return {'latents': jax.random.normal(ks[0], (B, N, DIM), jnp.float32), 'context': jax.random.normal(ks[1], (B, S, DIM), jnp.float32), 'ln_l_w': jnp.ones((DIM,), jnp.float32), 'ln_l_b': jnp.zeros((DIM,), jnp.float32), 'ln_c_w': jnp.ones((DIM,), jnp.float32), 'ln_c_b': jnp.zeros((DIM,), jnp.float32), 'Wq': jax.random.normal(ks[2], (DIM, INNER), jnp.float32) * s, 'Wkv': jax.random.normal(ks[3], (DIM, 2 * INNER), jnp.float32) * s, 'Wo': jax.random.normal(ks[4], (INNER, DIM), jnp.float32) * (1.0 / np.sqrt(INNER)), 'bo': jnp.zeros((DIM,), jnp.float32)}
    _L1_xattn_all = _L1_xattn_setup()
    _L1_xattn_in = {k: v for k, v in _L1_xattn_all.items() if k in ('ln_l_w', 'ln_l_b', 'ln_c_w', 'ln_c_b', 'Wq', 'Wkv', 'Wo', 'bo')}
    del _L1_xattn_all

    def _L1_ffn_setup():
        import jax, jax.numpy as jnp
        import numpy as np
        B, S, D_MODEL, D_HIDDEN = (4, 512, 256, 1024)

        def act_quant(x):
            scale = 127.0 / jnp.clip(jnp.max(jnp.abs(x), axis=-1, keepdims=True), 1e-05)
            return jnp.clip(jnp.round(x * scale), -128, 127) / scale

        def weight_quant(w):
            scale = 1.0 / jnp.clip(jnp.mean(jnp.abs(w)), 1e-05)
            return jnp.clip(jnp.round(w * scale), -1, 1) / scale

        def bit_linear(x, w):
            xq = x + jax.lax.stop_gradient(act_quant(x) - x)
            wq = w + jax.lax.stop_gradient(weight_quant(w) - w)
            return jnp.einsum('bsd,hd->bsh', xq, wq)

        def depthwise_conv1d(x_bcl, w, b):
            y = jax.lax.conv_general_dilated(x_bcl, w, window_strides=(1,), padding=[(1, 1)], dimension_numbers=('NCH', 'OIH', 'NCH'), feature_group_count=x_bcl.shape[1])
            return y + b[None, :, None]
        key = jax.random.key(seed)
        ks = jax.random.split(key, 5)
        lim1 = 1.0 / np.sqrt(D_MODEL)
        lim2 = 1.0 / np.sqrt(D_HIDDEN)
        limc = 1.0 / np.sqrt(3.0)
        return {'x': jax.random.normal(ks[0], (B, S, D_MODEL), dtype=jnp.float32), 'w1': jax.random.uniform(ks[1], (D_HIDDEN, D_MODEL), jnp.float32, -lim1, lim1), 'conv_w': jax.random.uniform(ks[2], (D_HIDDEN, 1, 3), jnp.float32, -limc, limc), 'conv_b': jax.random.uniform(ks[3], (D_HIDDEN,), jnp.float32, -limc, limc), 'w2': jax.random.uniform(ks[4], (D_MODEL, D_HIDDEN), jnp.float32, -lim2, lim2)}
    _L1_ffn_all = _L1_ffn_setup()
    _L1_ffn_in = {k: v for k, v in _L1_ffn_all.items() if k in ('w1', 'conv_w', 'conv_b', 'w2')}
    del _L1_ffn_all
    return {'x': x, 'ctx_1024': ctx_1024, 'mask_Bx16xSxS2_ff0': mask_Bx16xSxS2_ff0, 'L0_xattn_W_q': _L0_xattn_in['W_q'], 'L0_xattn_W_k': _L0_xattn_in['W_k'], 'L0_xattn_W_v': _L0_xattn_in['W_v'], 'L0_xattn_W_o': _L0_xattn_in['W_o'], 'L0_xattn_lambda_q1': _L0_xattn_in['lambda_q1'], 'L0_xattn_lambda_k1': _L0_xattn_in['lambda_k1'], 'L0_xattn_lambda_q2': _L0_xattn_in['lambda_q2'], 'L0_xattn_lambda_k2': _L0_xattn_in['lambda_k2'], 'L0_xattn_rms_scale': _L0_xattn_in['rms_scale'], 'L0_ffn_router_W': _L0_ffn_in['router_W'], 'L0_ffn_router_b': _L0_ffn_in['router_b'], 'L0_ffn_W1': _L0_ffn_in['W1'], 'L0_ffn_b1': _L0_ffn_in['b1'], 'L0_ffn_W2': _L0_ffn_in['W2'], 'L0_ffn_b2': _L0_ffn_in['b2'], 'L1_xattn_ln_l_w': _L1_xattn_in['ln_l_w'], 'L1_xattn_ln_l_b': _L1_xattn_in['ln_l_b'], 'L1_xattn_ln_c_w': _L1_xattn_in['ln_c_w'], 'L1_xattn_ln_c_b': _L1_xattn_in['ln_c_b'], 'L1_xattn_Wq': _L1_xattn_in['Wq'], 'L1_xattn_Wkv': _L1_xattn_in['Wkv'], 'L1_xattn_Wo': _L1_xattn_in['Wo'], 'L1_xattn_bo': _L1_xattn_in['bo'], 'L1_ffn_w1': _L1_ffn_in['w1'], 'L1_ffn_conv_w': _L1_ffn_in['conv_w'], 'L1_ffn_conv_b': _L1_ffn_in['conv_b'], 'L1_ffn_w2': _L1_ffn_in['w2']}

def reference(x, ctx_1024, mask_Bx16xSxS2_ff0, L0_xattn_W_q, L0_xattn_W_k, L0_xattn_W_v, L0_xattn_W_o, L0_xattn_lambda_q1, L0_xattn_lambda_k1, L0_xattn_lambda_q2, L0_xattn_lambda_k2, L0_xattn_rms_scale, L0_ffn_router_W, L0_ffn_router_b, L0_ffn_W1, L0_ffn_b1, L0_ffn_W2, L0_ffn_b2, L1_xattn_ln_l_w, L1_xattn_ln_l_b, L1_xattn_ln_c_w, L1_xattn_ln_c_b, L1_xattn_Wq, L1_xattn_Wkv, L1_xattn_Wo, L1_xattn_bo, L1_ffn_w1, L1_ffn_conv_w, L1_ffn_conv_b, L1_ffn_w2):
    import jax
    import jax.numpy as jnp

    def _L0_xattn_ref(query, key, value, attn_mask, W_q, W_k, W_v, W_o, lambda_q1, lambda_k1, lambda_q2, lambda_k2, rms_scale):
        import jax, jax.numpy as jnp
        import numpy as np
        B, S, D = (2, 512, 256)
        H = 16
        DH = D // H
        LAMBDA_INIT = 0.8
        EPS = 1e-05
        SCALE = 1.0 / np.sqrt(DH)
        b, s, _ = value.shape
        q = (query @ W_q).reshape(b, s, H, 2 * DH).transpose(0, 2, 1, 3)
        k = (key @ W_k).reshape(b, s, H, 2 * DH).transpose(0, 2, 1, 3)
        v = (value @ W_v).reshape(b, s, H, DH).transpose(0, 2, 1, 3)
        q1, q2 = (q[..., :DH], q[..., DH:])
        k1, k2 = (k[..., :DH], k[..., DH:])
        lam = jnp.exp(jnp.sum(lambda_q1 * lambda_k1, -1)) - jnp.exp(jnp.sum(lambda_q2 * lambda_k2, -1)) + LAMBDA_INIT
        lam = lam[None, :, None, None]
        s1 = jnp.einsum('bhqd,bhkd->bhqk', q1, k1) * SCALE + attn_mask
        s2 = jnp.einsum('bhqd,bhkd->bhqk', q2, k2) * SCALE + attn_mask
        attn = jax.nn.softmax(s1, axis=-1) - lam * jax.nn.softmax(s2, axis=-1)
        out = jnp.einsum('bhqk,bhkd->bhqd', attn, v)
        rms = jnp.sqrt(jnp.mean(out * out, axis=-1, keepdims=True) + EPS)
        out = out / rms * rms_scale
        out = out * (1.0 - LAMBDA_INIT)
        out = out.transpose(0, 2, 1, 3).reshape(b, s, H * DH)
        return out @ W_o

    def _L0_ffn_ref(x, router_W, router_b, W1, b1, W2, b2):
        import jax, jax.numpy as jnp
        import numpy as np
        D_MODEL = 256
        D_FF = 1024
        N_EXPERTS = 8
        INIT_SCALE = 0.1

        def _trunc_normal(key, shape, std):
            return std * jax.random.truncated_normal(key, -2.0, 2.0, shape, dtype=jnp.float32)
        logits = jnp.einsum('bsd,de->bse', x.astype(jnp.float32), router_W) + router_b
        probs = jax.nn.softmax(logits, axis=-1)
        top1 = jnp.argmax(probs, axis=-1)
        mask = jax.nn.one_hot(top1, N_EXPERTS, dtype=x.dtype)
        gates = mask * probs.astype(x.dtype)
        h = jax.nn.relu(jnp.einsum('bsd,edf->besf', x, W1) + b1[:, None, :])
        y = jnp.einsum('besf,efd->besd', h, W2) + b2[:, None, :]
        out = jnp.einsum('bse,besd->bsd', gates, y)
        return out

    def _L1_xattn_ref(latents, context, ln_l_w, ln_l_b, ln_c_w, ln_c_b, Wq, Wkv, Wo, bo):
        import jax, jax.numpy as jnp
        import numpy as np
        DIM = 256
        H = 16
        D = 64
        INNER = H * D
        EPS = 1e-05

        def layernorm(x, w, b):
            mu = jnp.mean(x, axis=-1, keepdims=True)
            var = jnp.var(x, axis=-1, keepdims=True)
            return (x - mu) * jax.lax.rsqrt(var + EPS) * w + b
        b, n, _ = latents.shape
        s = context.shape[1]
        lat = layernorm(latents, ln_l_w, ln_l_b)
        ctx = layernorm(context, ln_c_w, ln_c_b)
        q = (lat @ Wq).reshape(b, n, H, D).transpose(0, 2, 1, 3)
        kv = ctx @ Wkv
        k, v = jnp.split(kv, 2, axis=-1)
        k = k.reshape(b, s, H, D).transpose(0, 2, 1, 3)
        v = v.reshape(b, s, H, D).transpose(0, 2, 1, 3)
        scale = D ** (-0.5)
        attn = jnp.einsum('bhnd,bhsd->bhns', q, k) * scale
        attn = jnp.clip(attn, -11.0, 11.0)
        attn = jax.nn.softmax(attn, axis=-1)
        out = jnp.einsum('bhns,bhsd->bhnd', attn, v)
        out = out.transpose(0, 2, 1, 3).reshape(b, n, INNER)
        return out @ Wo + bo

    def _L1_ffn_ref(x, w1, conv_w, conv_b, w2):
        import jax, jax.numpy as jnp
        import numpy as np
        B, S, D_MODEL, D_HIDDEN = (4, 512, 256, 1024)

        def act_quant(x):
            scale = 127.0 / jnp.clip(jnp.max(jnp.abs(x), axis=-1, keepdims=True), 1e-05)
            return jnp.clip(jnp.round(x * scale), -128, 127) / scale

        def weight_quant(w):
            scale = 1.0 / jnp.clip(jnp.mean(jnp.abs(w)), 1e-05)
            return jnp.clip(jnp.round(w * scale), -1, 1) / scale

        def bit_linear(x, w):
            xq = x + jax.lax.stop_gradient(act_quant(x) - x)
            wq = w + jax.lax.stop_gradient(weight_quant(w) - w)
            return jnp.einsum('bsd,hd->bsh', xq, wq)

        def depthwise_conv1d(x_bcl, w, b):
            y = jax.lax.conv_general_dilated(x_bcl, w, window_strides=(1,), padding=[(1, 1)], dimension_numbers=('NCH', 'OIH', 'NCH'), feature_group_count=x_bcl.shape[1])
            return y + b[None, :, None]
        h = bit_linear(x, w1)
        h = depthwise_conv1d(h.transpose(0, 2, 1), conv_w, conv_b)
        h = h.transpose(0, 2, 1)
        h = jax.nn.silu(h)
        return bit_linear(h, w2)
    x = x + _L0_xattn_ref(_layernorm(x, axis=-1), ctx_1024, ctx_1024, mask_Bx16xSxS2_ff0, L0_xattn_W_q, L0_xattn_W_k, L0_xattn_W_v, L0_xattn_W_o, L0_xattn_lambda_q1, L0_xattn_lambda_k1, L0_xattn_lambda_q2, L0_xattn_lambda_k2, L0_xattn_rms_scale)
    x = x + _L0_ffn_ref(_layernorm(x, axis=-1), L0_ffn_router_W, L0_ffn_router_b, L0_ffn_W1, L0_ffn_b1, L0_ffn_W2, L0_ffn_b2)
    x = x + _L1_xattn_ref(_layernorm(x, axis=-1), ctx_1024, L1_xattn_ln_l_w, L1_xattn_ln_l_b, L1_xattn_ln_c_w, L1_xattn_ln_c_b, L1_xattn_Wq, L1_xattn_Wkv, L1_xattn_Wo, L1_xattn_bo)
    x = x + _L1_ffn_ref(_layernorm(x, axis=-1), L1_ffn_w1, L1_ffn_conv_w, L1_ffn_conv_b, L1_ffn_w2)
    return x

_drawn_inputs = setup_inputs


def setup_inputs(seed=0):
    import zlib

    import numpy as np

    out = dict(_drawn_inputs(seed))
    spreads = {'L0_xattn_rms_scale': (1.0, 0.6),
     'L0_ffn_router_b': (0.0, 0.586),
     'L0_ffn_b1': (0.0, 0.8),
     'L0_ffn_b2': (0.0, 0.592),
     'L1_xattn_ln_l_w': (1.0, 0.2),
     'L1_xattn_ln_l_b': (0.0, 0.516),
     'L1_xattn_ln_c_w': (1.0, 0.2),
     'L1_xattn_ln_c_b': (0.0, 0.1),
     'L1_xattn_bo': (0.0, 0.1)}
    factors = {'L0_xattn_W_q': 3.519,
     'L0_xattn_W_k': 3.495,
     'L0_xattn_lambda_q1': 8.0,
     'L0_xattn_lambda_k1': 8.0,
     'L0_xattn_lambda_q2': 8.0,
     'L0_xattn_lambda_k2': 8.0,
     'L0_ffn_router_W': 5.455,
     'L0_ffn_W1': 8.0,
     'L0_ffn_W2': 8.0}
    for name, (base, spread) in spreads.items():
        noise = np.random.default_rng([zlib.crc32(name.encode()), seed]).standard_normal(out[name].shape)
        drawn = base * np.exp(spread * noise) if base else spread * noise
        out[name] = jnp.asarray(drawn.astype(out[name].dtype))
    for name, factor in factors.items():
        out[name] = (out[name] * factor).astype(out[name].dtype)
    return out
```

```python
from contextlib import ExitStack

import numpy as np

import concourse.bass as bass
from concourse import mybir

F32 = mybir.dt.float32
BF16 = mybir.dt.bfloat16
I32 = mybir.dt.int32
ALU = mybir.AluOpType
ACT = mybir.ActivationFunctionType
AX = mybir.AxisListType

P = 128
BATCH, SEQ, DIM = 4, 512, 256
TOK_TILES = SEQ // P
ALL_TILES = BATCH * TOK_TILES
DK = DIM // P
EPS = 1e-5

DH = 16
HEADS = 16
MAPS = 2
FEATS = HEADS * MAPS * DH
FEAT_TILES = FEATS // P
MAPS_PER_TILE = P // DH
LAMBDA_INIT = 0.8


class Steps:

    def __init__(self, eng, sem):
        self.eng, self.sem, self.base, self.n = eng, sem, 0, 0
        self.turn = self.per_turn = None

    def loop(self, turn, per_turn):
        self.base, self.n, self.turn, self.per_turn = self.base + self.n, 0, turn, per_turn

    def end_loop(self, turns):
        assert self.n == self.per_turn, f"{self.sem} counts {self.n} per turn, not {self.per_turn}"
        self.base, self.n, self.turn = self.base + turns * self.per_turn, 0, None

    def done(self, instruction):
        instruction.then_inc(self.sem, 1)
        self.n += 1
        return self.n

    def wait(self, n=None):
        n = self.n if n is None else n
        at = self.base + n
        self.eng.wait_ge(self.sem, at if self.turn is None else self.turn * self.per_turn + at)


def flat(ap):
    return ap.rearrange("p a n -> p (a n)")


def diff_attention(nc, ctx_outer, T, A):
    with ExitStack() as ctx:
        def sb(name, shape, dt=F32):
            return ctx.enter_context(nc.sbuf_tensor("a_" + name, shape, dt))

        def sem(name):
            return ctx_outer.enter_context(nc.semaphore("a_" + name))

        psum = [ctx.enter_context(nc.psum_tensor(f"a_bank{i}", [P, 512], F32)) for i in range(8)]
        x_res, ident = T["x_res"], T["ident"]
        SCALE = 1.0 / float(np.sqrt(DH))

        wq = sb("wq", [P, DK, FEATS])
        wk = sb("wk", [P, DK, FEATS])
        wv = sb("wv", [P, DK, DIM])
        wo = sb("wo", [P, DK, DIM])
        ctx_b = sb("ctx_b", [P, TOK_TILES, DIM])
        xnT = sb("xnT", [P, DK, SEQ])
        ctxT = sb("ctxT", [P, DK, SEQ])
        part = sb("part", [P, 4, 3, SEQ], BF16)
        q_packed = sb("q_packed", [96, HEADS * MAPS, SEQ], BF16)
        k_packed = sb("k_packed", [96, HEADS * MAPS, SEQ], BF16)
        mask = sb("mask", [P, 2, TOK_TILES, SEQ])
        prob = sb("prob", [P, 2, TOK_TILES, MAPS, SEQ])
        attn = sb("attn", [P, 2, TOK_TILES, SEQ])
        attnT = sb("attnT", [P, TOK_TILES, SEQ])
        pv_part = sb("pv_part", [P, SEQ])
        v_pad = sb("v_pad", [P, TOK_TILES, HEADS, 32])
        o_heads = sb("o_heads", [P, HEADS, TOK_TILES, DH])
        xn_b = attn[:, 0, 0:2, :].rearrange("p a n -> p (a n)").rearrange("p (q d) -> p q d", d=DIM)
        rest = attn[:, 1, 0:2, :]
        o_norm = rest.rearrange("p a n -> p (a n)").rearrange("p (q h d) -> p q h d", h=HEADS, d=DH)
        oT = xnT
        neg_max = sb("neg_max", [P, HEADS, TOK_TILES, MAPS])
        row_sum = sb("row_sum", [P, HEADS, MAPS, TOK_TILES])
        coef = sb("coef", [P, 2, 2, TOK_TILES])
        small = sb("small", [P, 4, HEADS * TOK_TILES])
        stats = sb("stats", [P, ALL_TILES, 6])
        moments = sb("moments", [P, ALL_TILES, 2])
        rstd = sb("rstd", [P, 2, ALL_TILES])
        lam_in = attnT[:, :, 0:HEADS * DH]
        neg_lam = sb("neg_lam", [P, HEADS])
        rms_col = sb("rms_col", [P, 2])
        scratch = sb("scratch", [P, 8])
        q_parts_d = nc.dram_tensor("a_q_parts", (BATCH, 3, FEATS, SEQ), BF16, kind="Internal").ap()
        k_parts_d = nc.dram_tensor("a_k_parts", (BATCH, 3, FEATS, SEQ), BF16, kind="Internal").ap()

        names = ("x_in w_in lam_loaded rms_loaded stats_ready std_ready lam_prod lam_exp ctx_in mask_in0 mask_in1 "
                 "xn_ready pro_mm pro_act pro_dve split_done scores ttr exp comb turned at_ready pv pv_ev oturned "
                 "oreduced ms_ready rms_ready on_ready on_turned oT_ready wo_mm x_added dve_own act_own pool_own "
                 "vpad_zero parts_written rms_scaled").split()
        S = {n: sem(n) for n in names}
        pack_in = [sem(f"pack_in{f}") for f in range(FEAT_TILES)]

        JOBS = 14
        UNITS = HEADS * TOK_TILES * MAPS
        TURNS = HEADS * TOK_TILES

        def kind_of(j):
            if j < 4:
                return ("turn", j % 2, j // 2)
            if j < 12:
                return ("qk", (j - 4) // 2, (j - 4) % 2)
            return ("v", j - 12, 0)

        with nc.Block() as block:
            @block.sync
            def _(sp):
                sp.dma_start(x_res[:, :, :], A["x"].rearrange("b (q p) d -> p (b q) d", p=P)).then_inc(S["x_in"], 16)
                for w, name in ((wq, "W_q"), (wk, "W_k"), (wv, "W_v"), (wo, "W_o")):
                    sp.dma_start(w[:, :, :], A["L0_xattn_" + name].rearrange("(k p) n -> p k n", p=P)).then_inc(S["w_in"], 16)
                with sp.Fori(0, BATCH) as b:
                    sp.wait_ge(S["pro_act"], b * JOBS)
                    sp.dma_start(ctx_b[:, :, :], A["ctx_1024"][bass.ds(b, 1)].rearrange("a (q p) d -> p (a q) d", p=P)).then_inc(S["ctx_in"], 16)

                    def load_mask(h):
                        if h < 2:
                            sp.wait_ge(S["ttr"], b * UNITS)
                        else:
                            sp.wait_ge(S["ttr"], b * UNITS + 8 * (h - 1))
                        sp.dma_start(mask[:, h % 2, :, :],
                                     A["mask_Bx16xSxS2_ff0"][bass.ds(b, 1), h].rearrange("a (q p) n -> p (a q) n", p=P)
                                     ).then_inc(S[f"mask_in{h % 2}"], 16)

                    load_mask(0)
                    load_mask(1)

                    def write_parts(i):
                        f, isk = i // 2, i % 2
                        sp.wait_ge(S["split_done"], b * 8 + i + 1)
                        dst = (k_parts_d if isk else q_parts_d)[bass.ds(b, 1), :, f * P:(f + 1) * P, :]
                        sp.dma_start(dst.rearrange("a j p n -> p (a j) n"), part[:, i % 4, :, :]).then_inc(S["parts_written"], 16)

                    def read_packed(f):
                        sp.wait_ge(S["parts_written"], b * 128 + 32 * (f + 1))
                        lo = 0
                        for j, reps in enumerate((3, 2, 1)):
                            n = reps * DH
                            src_q = q_parts_d[bass.ds(b, 1), 0:reps, f * P:(f + 1) * P, :]
                            src_k = k_parts_d[bass.ds(b, 1), j, f * P:(f + 1) * P, :]
                            maps = slice(f * MAPS_PER_TILE, (f + 1) * MAPS_PER_TILE)
                            for r in range(reps):
                                sp.dma_start(q_packed[lo + r * DH:lo + (r + 1) * DH, maps, :],
                                             src_q[:, r].rearrange("a (s d) n -> d (a s) n", d=DH)).then_inc(pack_in[f], 16)
                                sp.dma_start(k_packed[lo + r * DH:lo + (r + 1) * DH, maps, :],
                                             src_k.rearrange("a (s d) n -> d (a s) n", d=DH)).then_inc(pack_in[f], 16)
                            lo += n

                    for f in range(FEAT_TILES):
                        write_parts(2 * f)
                        write_parts(2 * f + 1)
                        read_packed(f)
                    for h in range(2, HEADS):
                        load_mask(h)

            @block.gpsimd
            def _(pool):
                own = Steps(pool, S["pool_own"])
                pool.memset(v_pad[:, :, :, :], 0.0).then_inc(S["vpad_zero"], 1)
                for i, n in enumerate(("q1", "k1", "q2", "k2")):
                    pool.dma_start(lam_in[:, i, :], A["L0_xattn_lambda_" + n].rearrange("h d -> (h d)").rearrange("(a n) -> a n", a=1).broadcast_to([P, HEADS * DH])).then_inc(S["lam_loaded"], 16)
                for g in range(P // DH):
                    pool.dma_start(rms_col[g * DH:(g + 1) * DH, 0:1], A["L0_xattn_rms_scale"].rearrange("(d a) -> d a", a=1)).then_inc(S["rms_loaded"], 16)
                with pool.Fori(0, BATCH) as b:
                    own.loop(b, 0)
                    for i in range(8):
                        pool.wait_ge(S["pro_dve"], b * JOBS + 4 + i + 1)
                        pool.tensor_tensor(part[:, i % 4, 2, :], rest[:, i % 2, :], part[:, i % 4, 1, :], ALU.subtract).then_inc(S["split_done"], 1)
                    own.end_loop(BATCH)

            @block.tensor
            def _(pe):
                pe.wait_ge(S["w_in"], 64)
                pe.wait_ge(T["ident_ready"], T["ident_count"])
                with pe.Fori(0, BATCH) as b:
                    def prologue(j):
                        kind, a, c = kind_of(j)
                        bank = psum[j % 4]
                        if j < 4:
                            pe.wait_ge(S["ttr"], b * UNITS)
                        else:
                            pe.wait_ge(S["pro_act"], b * JOBS + j - 3)
                            pe.wait_ge(S["pro_dve"], b * JOBS + j - 3)
                        if kind == "turn":
                            if j == 0:
                                pe.wait_ge(S["xn_ready"], b + 1)
                            if j == 2:
                                pe.wait_ge(S["ctx_in"], b * 16 + 16)
                            src = ctx_b if c else xn_b
                            for q in range(TOK_TILES):
                                mm = pe.transpose(bank[:, q * P:(q + 1) * P], src[:, q, a * P:(a + 1) * P], ident[:, :])
                        elif kind == "qk":
                            if j == 4:
                                pe.wait_ge(S["pro_act"], b * JOBS + 4)
                                pe.wait_ge(S["pro_dve"], b * JOBS + 4)
                            w, src = (wk, ctxT) if c else (wq, xnT)
                            for k in range(DK):
                                mm = pe.matmul(bank[:, :], w[:, k, a * P:(a + 1) * P], src[:, k, :], start=k == 0, stop=k == DK - 1)
                        else:
                            for t in range(2):
                                for k in range(DK):
                                    mm = pe.matmul(bank[:, t * DIM:(t + 1) * DIM], ctxT[:, k, (2 * a + t) * P:(2 * a + t + 1) * P],
                                                   wv[:, k, :], start=k == 0, stop=k == DK - 1)
                        mm.then_inc(S["pro_mm"], 1)

                    for j in range(JOBS):
                        prologue(j)

                    def scores(h, q):
                        if h % 4 == 0 and q == 0:
                            pe.wait_ge(pack_in[h // 4], b * 192 + 192)
                        for m in range(MAPS):
                            n = (h * TOK_TILES + q) * MAPS + m
                            if n < 4:
                                if n == 0:
                                    pe.wait_ge(S["pro_act"], b * JOBS + JOBS)
                                    pe.wait_ge(S["pro_dve"], b * JOBS + JOBS)
                            else:
                                pe.wait_ge(S["ttr"], b * UNITS + n - 3)
                            hm = h * MAPS + m
                            pe.matmul(psum[n % 4][:, :], q_packed[:, hm, q * P:(q + 1) * P], k_packed[:, hm, :],
                                      start=True, stop=True).then_inc(S["scores"], 1)

                    def turn(h, k):
                        n = h * TOK_TILES + k
                        if k == 0:
                            pe.wait_ge(S["comb"], b * TURNS + TOK_TILES * (h + 1))
                        if n >= 2:
                            pe.wait_ge(S["at_ready"], b * TURNS + n - 1)
                        for q in range(TOK_TILES):
                            mm = pe.transpose(psum[4 + n % 2][:, q * P:(q + 1) * P], attn[:, h % 2, q, k * P:(k + 1) * P], ident[:, :])
                        mm.then_inc(S["turned"], 1)

                    def values(h):
                        pe.wait_ge(S["at_ready"], b * TURNS + TOK_TILES * (h + 1))
                        if h:
                            pe.wait_ge(S["pv_ev"], b * HEADS + h)
                        for k in range(TOK_TILES):
                            mm = pe.matmul(psum[6][32 * k:32 * (k + 1), :], v_pad[:, k, h, :], attnT[:, k, :], start=True, stop=True)
                        mm.then_inc(S["pv"], 1)

                    def turn_out(h):
                        pe.wait_ge(S["pv_ev"], b * HEADS + h + 1)
                        if h:
                            pe.wait_ge(S["oreduced"], b * HEADS + h)
                        for q in range(TOK_TILES):
                            mm = pe.transpose(psum[7][:, q * P:(q + 1) * P], pv_part[:, q * P:(q + 1) * P], ident[:, :])
                        mm.then_inc(S["oturned"], 1)

                    for h in range(HEADS + 4):
                        for q in range(TOK_TILES):
                            if h < HEADS:
                                scores(h, q)
                            if q == 0 and 4 <= h:
                                turn_out(h - 4)
                            if q == 0 and 3 <= h < HEADS + 3:
                                values(h - 3)
                            if 2 <= h < HEADS + 2:
                                turn(h - 2, q)

                    for k in range(DK):
                        if k == 0:
                            pe.wait_ge(S["on_ready"], b + 1)
                        for q in range(TOK_TILES):
                            mm = pe.transpose(psum[4 + k][:, q * P:(q + 1) * P], o_norm[:, q, 8 * k:8 * (k + 1), :].rearrange("p h d -> p (h d)"), ident[:, :])
                        mm.then_inc(S["on_turned"], 1)
                    pe.wait_ge(S["oT_ready"], (b + 1) * DK)
                    for q in range(TOK_TILES):
                        for k in range(DK):
                            mm = pe.matmul(psum[6 + q // 2][:, (q % 2) * DIM:(q % 2 + 1) * DIM], oT[:, k, q * P:(q + 1) * P], wo[:, k, :],
                                           start=k == 0, stop=k == DK - 1)
                        mm.then_inc(S["wo_mm"], 1)

            @block.scalar
            def _(act):
                own = Steps(act, S["act_own"])
                act.wait_ge(S["stats_ready"], 1)
                act.activation(rstd[:, 0, :], moments[:, :, 1], ACT.Sqrt, bias=T["eps"][:, :]).then_inc(S["std_ready"], 1)
                act.wait_ge(S["lam_prod"], 1)
                act.activation(small[:, 1, 0:2 * HEADS], small[:, 0, 0:2 * HEADS], ACT.Exp).then_inc(S["lam_exp"], 1)
                with act.Fori(0, BATCH) as b:
                    own.loop(b, 0)
                    for j in range(JOBS):
                        kind, a, c = kind_of(j)
                        bank = psum[j % 4]
                        act.wait_ge(S["pro_mm"], b * JOBS + j + 1)
                        if kind == "turn":
                            act.copy((ctxT if c else xnT)[:, a, 0:256], bank[:, 0:256]).then_inc(S["pro_act"], 1)
                        elif kind == "qk":
                            i = j - 4
                            if i >= 4:
                                act.wait_ge(S["parts_written"], b * 128 + 16 * (2 * ((i - 4) // 2) + 2))
                            else:
                                act.wait_ge(S["parts_written"], b * 128)
                            act.activation(part[:, i % 4, 0, :], bank[:, :], ACT.Copy, scale=1.0 if c else SCALE).then_inc(S["pro_act"], 1)
                        else:
                            act.copy(v_pad[:, 2 * a, :, 0:DH], bank[:, 0:DIM].rearrange("p (h d) -> p h d", d=DH)).then_inc(S["pro_act"], 1)

                    def exps(h, q):
                        for m in range(MAPS):
                            n = (h * TOK_TILES + q) * MAPS + m
                            act.wait_ge(S["ttr"], b * UNITS + n + 1)
                            tile = prob[:, h % 2, q, m, :]
                            act.activation(tile, tile, ACT.Exp, bias=neg_max[:, h, q, m:m + 1], scale=-1.0,
                                           accum_out=row_sum[:, h, m, q:q + 1]).then_inc(S["exp"], 1)

                    def copy_turned(h, k):
                        n = h * TOK_TILES + k
                        if k == 0 and h:
                            act.wait_ge(S["pv"], b * HEADS + h)
                        act.wait_ge(S["turned"], b * TURNS + n + 1)
                        act.copy(attnT[:, k, :], psum[4 + n % 2][:, :]).then_inc(S["at_ready"], 1)

                    def copy_values(h):
                        if h:
                            act.wait_ge(S["oturned"], b * HEADS + h)
                        act.wait_ge(S["pv"], b * HEADS + h + 1)
                        act.copy(pv_part[:, :], psum[6][:, :]).then_inc(S["pv_ev"], 1)

                    for h in range(HEADS + 3):
                        for q in range(TOK_TILES):
                            if h < HEADS:
                                exps(h, q)
                            if q == 0 and 3 <= h:
                                copy_values(h - 3)
                            if 2 <= h < HEADS + 2:
                                copy_turned(h - 2, q)
                    act.wait_ge(S["ms_ready"], b + 1)
                    act.activation(small[:, 2, :], small[:, 1, :], ACT.Sqrt, bias=T["eps"][:, :], scale=1.0 / DH).then_inc(S["rms_ready"], 1)
                    if True:
                        act.wait_ge(S["rms_scaled"], 1)
                    for k in range(DK):
                        act.wait_ge(S["on_turned"], b * DK + k + 1)
                        act.activation(oT[:, k, :], psum[4 + k][:, :], ACT.Copy, scale=rms_col[:, 1:2]).then_inc(S["oT_ready"], 1)
                    own.end_loop(BATCH)

            @block.vector
            def _(dve):
                own = Steps(dve, S["dve_own"])
                dve.wait_ge(S["x_in"], 16)
                for t in range(ALL_TILES):
                    s = dve.bn_stats(stats[:, t, :], x_res[:, t, :])
                own.done(s)
                own.wait()
                for t in range(ALL_TILES):
                    s = dve.bn_aggr(moments[:, t, :], stats[:, t, :])
                s.then_inc(S["stats_ready"], 1)
                dve.wait_ge(S["lam_loaded"], 64)
                for i in range(2):
                    own.done(dve.tensor_tensor(lam_in[:, 2 * i, :], lam_in[:, 2 * i, :], lam_in[:, 2 * i + 1, :], ALU.mult))
                own.wait()
                for i in range(2):
                    s = dve.tensor_reduce(small[:, 0, i * HEADS:(i + 1) * HEADS], lam_in[:, 2 * i, :].rearrange("p (h d) -> p h d", d=DH), AX.X, ALU.add)
                s.then_inc(S["lam_prod"], 1)
                dve.wait_ge(S["lam_exp"], 1)
                dve.scalar_tensor_tensor(out=neg_lam[:, :], in0=small[:, 1, HEADS:2 * HEADS], scalar=-LAMBDA_INIT, in1=small[:, 1, 0:HEADS],
                                         op0=ALU.add, op1=ALU.subtract)
                dve.wait_ge(S["rms_loaded"], 128)
                dve.tensor_scalar(rms_col[:, 1:2], rms_col[:, 0:1], 1.0 - LAMBDA_INIT, None, ALU.mult).then_inc(S["rms_scaled"], 1)
                dve.wait_ge(S["std_ready"], 1)
                own.done(dve.reciprocal(rstd[:, 1, :], rstd[:, 0, :]))
                own.wait()
                dve.wait_ge(S["vpad_zero"], 1)
                PER = 14
                with dve.Fori(0, BATCH) as b:
                    own.loop(b, DVE_A)
                    dve.wait_ge(S["pro_mm"], b * JOBS)
                    mom = moments[:, :, :].rearrange("p (b q) c -> p b (q c)", b=BATCH)
                    rs = rstd[:, 1, :].rearrange("p (b q) -> p b q", b=BATCH)
                    own.done(dve.tensor_copy(small[:, 3, 0:8], mom[:, bass.ds(b, 1), :].rearrange("p a n -> p (a n)")))
                    own.done(dve.tensor_copy(small[:, 3, 8:12], rs[:, bass.ds(b, 1), :].rearrange("p a n -> p (a n)")))
                    own.wait()
                    xv = x_res[:, :, :].rearrange("p (b q) d -> p b (q d)", b=BATCH)
                    for q in range(TOK_TILES):
                        s = dve.tensor_scalar(xn_b[:, q, :], flat(xv[:, bass.ds(b, 1), q * DIM:(q + 1) * DIM]),
                                              small[:, 3, 2 * q:2 * q + 1], small[:, 3, 8 + q:9 + q], ALU.subtract, ALU.mult)
                    s.then_inc(S["xn_ready"], 1)
                    for j in range(JOBS):
                        kind, a, c = kind_of(j)
                        bank = psum[j % 4]
                        dve.wait_ge(S["pro_act"], b * JOBS + j + 1)
                        if kind == "turn":
                            dve.tensor_copy((ctxT if c else xnT)[:, a, 256:512], bank[:, 256:512]).then_inc(S["pro_dve"], 1)
                        elif kind == "qk":
                            i = j - 4
                            if i >= 2:
                                dve.wait_ge(S["split_done"], b * 8 + i - 1)
                            own.done(dve.scalar_tensor_tensor(out=rest[:, i % 2, :], in0=bank[:, :], scalar=1.0 if c else SCALE,
                                                              in1=part[:, i % 4, 0, :], op0=ALU.mult, op1=ALU.subtract))
                            own.wait()
                            dve.tensor_copy(part[:, i % 4, 1, :], rest[:, i % 2, :]).then_inc(S["pro_dve"], 1)
                        else:
                            dve.tensor_copy(v_pad[:, 2 * a + 1, :, 0:DH], bank[:, DIM:2 * DIM].rearrange("p (h d) -> p h d", d=DH)).then_inc(S["pro_dve"], 1)

                    def ready(h, q):
                        if q == 0:
                            dve.wait_ge(S[f"mask_in{h % 2}"], b * 128 + 16 * (h // 2 + 1))
                        dve.wait_ge(S["scores"], b * UNITS + (h * TOK_TILES + q + 1) * MAPS)

                    def add_mask(h, q):
                        for m in range(MAPS):
                            n = (h * TOK_TILES + q) * MAPS + m
                            dve.tensor_tensor_reduce(prob[:, h % 2, q, m, :], psum[n % 4][:, :], mask[:, h % 2, q, :], -1.0, 3.0e38,
                                                     ALU.add, ALU.min, neg_max[:, h, q, m:m + 1]).then_inc(S["ttr"], 1)

                    def coefficients(h):
                        dve.wait_ge(S["exp"], b * UNITS + 8 * (h + 1))
                        own.done(dve.reciprocal(coef[:, h % 2, 0, :], row_sum[:, h, 1, :]))
                        own.wait()
                        own.done(dve.scalar_tensor_tensor(out=coef[:, h % 2, 1, :], in0=row_sum[:, h, 0, :], scalar=neg_lam[:, h:h + 1],
                                                          in1=coef[:, h % 2, 0, :], op0=ALU.mult, op1=ALU.mult))
                        own.wait()

                    def combine(h, q):
                        if q == 0 and h >= 2:
                            dve.wait_ge(S["turned"], b * TURNS + TOK_TILES * (h - 1))
                        dve.scalar_tensor_tensor(out=attn[:, h % 2, q, :], in0=prob[:, h % 2, q, 1, :], scalar=coef[:, h % 2, 1, q:q + 1],
                                                 in1=prob[:, h % 2, q, 0, :], op0=ALU.mult, op1=ALU.add).then_inc(S["comb"], 1)

                    def gather_out(h):
                        dve.wait_ge(S["oturned"], b * HEADS + h + 1)
                        dve.tensor_reduce(o_heads[:, h, :, :], psum[7][:, :].rearrange("p (q g d) -> p q d g", q=TOK_TILES, g=4)[:, :, 0:DH, :],
                                          AX.X, ALU.add).then_inc(S["oreduced"], 1)

                    for h in range(HEADS + 4):
                        for q in range(TOK_TILES):
                            g, p = (h - 1, q - 1) if q else (h - 2, TOK_TILES - 1)
                            if h < HEADS:
                                if h >= 2 and q == 0:
                                    dve.wait_ge(S["comb"], b * TURNS + TOK_TILES * (h - 1) - 1)
                                ready(h, q)
                            if 0 <= g < HEADS:
                                combine(g, p)
                            elif h < HEADS:
                                dve.memset(scratch[:, 4 * h + q:4 * h + q + 1], 0.0)
                            if h < HEADS:
                                add_mask(h, q)
                            if q == 0 and 1 <= h <= HEADS:
                                coefficients(h - 1)
                        if h >= 4:
                            gather_out(h - 4)
                    dve.wait_ge(S["oreduced"], (b + 1) * HEADS)
                    own.done(dve.reciprocal(small[:, 0, :].rearrange("p (h q) -> p h q", q=TOK_TILES), row_sum[:, :, 0, :]))
                    own.wait()
                    r4 = lambda k: small[:, k, :].rearrange("p (n a) -> p n a", a=1).broadcast_to([P, HEADS * TOK_TILES, DH])
                    oh = o_heads[:, :, :, :].rearrange("p h q d -> p (h q) d")
                    on = o_norm.rearrange("p q h d -> p (q h) d")
                    own.done(dve.tensor_tensor(oh, oh, r4(0), ALU.mult))
                    own.wait()
                    own.done(dve.tensor_tensor(on, oh, oh, ALU.mult))
                    own.wait()
                    dve.tensor_reduce(small[:, 1, :], on, AX.X, ALU.add).then_inc(S["ms_ready"], 1)
                    dve.wait_ge(S["rms_ready"], b + 1)
                    own.done(dve.reciprocal(small[:, 0, :], small[:, 2, :]))
                    own.wait()
                    dve.tensor_tensor(o_norm.rearrange("p q h d -> p h q d"), o_heads[:, :, :, :],
                                      small[:, 0, :].rearrange("p (h q a) -> p h q a", q=TOK_TILES, a=1).broadcast_to([P, HEADS, TOK_TILES, DH]),
                                      ALU.mult).then_inc(S["on_ready"], 1)
                    for q in range(TOK_TILES):
                        dve.wait_ge(S["wo_mm"], b * TOK_TILES + 2 * (q // 2) + 2)
                        xq = flat(xv[:, bass.ds(b, 1), q * DIM:(q + 1) * DIM])
                        s = dve.tensor_tensor(xq, psum[6 + q // 2][:, (q % 2) * DIM:(q % 2 + 1) * DIM], xq, ALU.add)
                    s.then_inc(S["x_added"], 1)
                    own.end_loop(BATCH)


DVE_A = 2 + 8 + 2 * HEADS + 4


EXPERTS = 8
FF = 1024
FF_TILES = FF // P
SLOT_TILES = 24


def layernorm_all(dve, own, sem_stats, sem_std, std_at, x_res, stats, moments, rstd, out):
    for t in range(ALL_TILES):
        s = dve.bn_stats(stats[:, t, :], x_res[:, t, :])
    own.done(s)
    own.wait()
    for t in range(ALL_TILES):
        s = dve.bn_aggr(moments[:, t, :], stats[:, t, :])
    s.then_inc(sem_stats, 1)
    dve.wait_ge(sem_std, std_at)
    own.done(dve.reciprocal(rstd[:, 1, :], rstd[:, 0, :]))
    own.wait()
    for t in range(ALL_TILES):
        s = dve.tensor_scalar(out[:, t, :], x_res[:, t, :], moments[:, t, 0:1], rstd[:, 1, t:t + 1], ALU.subtract, ALU.mult)
    return s


def experts(nc, ctx_outer, T, A):
    with ExitStack() as ctx:
        def sb(name, shape, dt=F32):
            return ctx.enter_context(nc.sbuf_tensor("b_" + name, shape, dt))

        def sem(name):
            return ctx_outer.enter_context(nc.semaphore("b_" + name))

        psum = [ctx.enter_context(nc.psum_tensor(f"b_bank{i}", [P, 512], F32)) for i in range(8)]
        x_res, ident = T["x_res"], T["ident"]
        stats = sb("stats", [P, ALL_TILES, 6])
        moments = sb("moments", [P, ALL_TILES, 2])
        rstd = sb("rstd", [P, 2, ALL_TILES])
        xn = sb("xn", [P, ALL_TILES, DIM])
        xnT = sb("xnT", [P, BATCH, DK, SEQ])
        router = sb("router", [P, DK, EXPERTS])
        router_b = sb("router_b", [P, EXPERTS])
        logits = sb("logits", [P, ALL_TILES, EXPERTS])
        expd = sb("expd", [P, ALL_TILES, EXPERTS])
        pick = sb("pick", [P, ALL_TILES, EXPERTS])
        onehot = sb("onehot", [P, ALL_TILES, EXPERTS])
        onehot_b = sb("onehot_b", [P, ALL_TILES, EXPERTS], BF16)
        col = sb("col", [P, 6, ALL_TILES])
        gate = sb("gate", [P, ALL_TILES])
        first_w = sb("first_w", [P, EXPERTS])
        before = sb("before", [P, P], BF16)
        ones_b = sb("ones_b", [P, P], BF16)
        totals = sb("totals", [P, ALL_TILES, EXPERTS])
        cum = sb("cum", [P, 2, ALL_TILES, EXPERTS])
        where = sb("where", [P, ALL_TILES, EXPERTS])
        count_i = sb("count_i", [P, 2, EXPERTS], I32)
        need = sb("need", [P, 4, EXPERTS])
        slot_f = sb("slot_f", [P, ALL_TILES])
        slot = sb("slot", [P, ALL_TILES], I32)
        tile_no = sb("tile_no", [P, SLOT_TILES])
        past = sb("past", [P, SLOT_TILES, EXPERTS])
        owner_f = sb("owner_f", [P, SLOT_TILES])
        owner = sb("owner", [P, SLOT_TILES], I32)
        zero = sb("zero", [P, SLOT_TILES, DIM])
        b1_rows = sb("b1_rows", [EXPERTS * FF_TILES, P])
        b1T = sb("b1T", [P, EXPERTS * FF_TILES])
        b2_all = sb("b2_all", [P, EXPERTS, DIM])
        w1 = sb("w1", [P, 2, DK, FF])
        w2 = sb("w2", [P, 2, FF_TILES, DIM])
        x_slots = sb("x_slots", [P, 2, DIM])
        x_slotsT = sb("x_slotsT", [P, 2, DK, P])
        hiddenT = sb("hiddenT", [P, 2, FF_TILES, P])
        b1_t = sb("b1_t", [P, 2, FF_TILES])
        y_slots = sb("y_slots", [P, 2, DIM])
        y_tok = sb("y_tok", [P, 4, DIM])
        x_slots_d = nc.dram_tensor("b_x_sorted", (SLOT_TILES * P, DIM), F32, kind="Internal").ap()
        y_slots_d = nc.dram_tensor("b_y_sorted", (SLOT_TILES * P, DIM), F32, kind="Internal").ap()

        names = ("w_in b1_in b1_turned b1_ready zeroed zero_out stats_ready std_ready xn_ready turned turn_act turn_dve "
                 "logit_mm shifted exp_done onehot_ready masks_ready ranks totals_mm slot_ready owner_ready scattered "
                 "w1_in0 w1_in1 w2_in0 w2_in1 xs_in0 xs_in1 xs_turned xsT_ready b1_picked h_mm0 h_mm1 "
                 "relu_act relu_dve y_mm y_ready y_out0 y_out1 gathered combined dve_own pool_own iota_done").split()
        S = {n: sem(n) for n in names}
        gathered = [sem(f"gathered{i}") for i in range(4)]
        EB, NTILE = EXPERTS, ALL_TILES

        with nc.Block() as block:
            @block.sync
            def _(sp):
                sp.dma_start(router[:, :, :], A["L0_ffn_router_W"].rearrange("(k p) e -> p k e", p=P)).then_inc(S["w_in"], 16)
                sp.dma_start(router_b[:, :], A["L0_ffn_router_b"].rearrange("(a e) -> a e", a=1).broadcast_to([P, EXPERTS])).then_inc(S["w_in"], 16)
                sp.dma_start(b1_rows[:, :], A["L0_ffn_b1"].rearrange("e (f p) -> (e f) p", p=P)).then_inc(S["b1_in"], 16)
                sp.dma_start(b2_all[:, :, :], A["L0_ffn_b2"].rearrange("(a e) d -> a e d", a=1).broadcast_to([P, EXPERTS, DIM])).then_inc(S["b1_in"], 16)
                sp.wait_ge(S["zeroed"], 1)
                sp.dma_start(x_slots_d.rearrange("(t p) d -> p t d", p=P), zero[:, :, :]).then_inc(S["zero_out"], 16)
                sp.wait_ge(S["owner_ready"], 1)
                with sp.Fori(0, SLOT_TILES // 2) as i:
                    for r in range(2):
                        e = sp.value_load(owner[0:1, bass.ds(2 * i + r, 1)], min_val=0, max_val=EXPERTS - 1)
                        sp.wait_ge(S[f"h_mm{r}"], i)
                        sp.dma_start(w1[:, r, :, :], A["L0_ffn_W1"][bass.ds(e, 1)].rearrange("a (k p) f -> p (a k) f", p=P)).then_inc(S[f"w1_in{r}"], 16)
                        sp.wait_ge(S["y_mm"], 2 * i + (r if r else 0))
                        sp.dma_start(w2[:, r, :, :], A["L0_ffn_W2"][bass.ds(e, 1)].rearrange("a (k p) d -> p (a k) d", p=P)).then_inc(S[f"w2_in{r}"], 16)

            @block.gpsimd
            def _(pool):
                own = Steps(pool, S["pool_own"])
                pool.memset(zero[:, :, :], 0.0).then_inc(S["zeroed"], 1)
                pool.memset(ones_b[:, :], 1.0)
                own.done(pool.memset(before[:, :], 1.0))
                own.wait()
                pool.affine_select(out=before[:, :], in_=before[:, :], compare_op=ALU.is_gt, fill=0.0, base=0,
                                   pattern=[[1, P]], channel_multiplier=-1).then_inc(S["masks_ready"], 1)
                pool.iota(first_w[:, :], pattern=[[-1, EXPERTS]], base=EXPERTS, channel_multiplier=0,
                          allow_small_or_imprecise_dtypes=True).then_inc(S["iota_done"], 1)
                pool.iota(tile_no[:, :], pattern=[[1, SLOT_TILES]], base=0, channel_multiplier=0,
                          allow_small_or_imprecise_dtypes=True).then_inc(S["iota_done"], 1)
                pool.wait_ge(S["slot_ready"], 1)
                pool.wait_ge(S["xn_ready"], 1)
                pool.wait_ge(S["zero_out"], 16)
                for t in range(ALL_TILES):
                    pool.indirect_dma_start(x_slots_d, bass.IndirectOffsetOnAxis(slot[:, t:t + 1], 0), xn[:, t, :], None).then_inc(S["scattered"], 16)
                pool.wait_ge(S["scattered"], 16 * ALL_TILES)
                with pool.Fori(0, SLOT_TILES // 2) as i:
                    for r in range(2):
                        pool.wait_ge(S["xs_turned"], 2 * i + (r if r else 0))
                        pool.dma_start(x_slots[:, r, :], x_slots_d.rearrange("(i r p) d -> i r p d", r=2, p=P)[bass.ds(i, 1), r].rearrange("a p d -> p (a d)")).then_inc(S[f"xs_in{r}"], 16)
                pool.wait_ge(S["y_out0"], 16 * (SLOT_TILES // 2))
                pool.wait_ge(S["y_out1"], 16 * (SLOT_TILES // 2))
                for t in range(ALL_TILES):
                    if t >= 4:
                        pool.wait_ge(S["combined"], t - 3)
                    pool.indirect_dma_start(y_tok[:, t % 4, :], None, y_slots_d, bass.IndirectOffsetOnAxis(slot[:, t:t + 1], 0)).then_inc(gathered[t % 4], 16)

            @block.tensor
            def _(pe):
                pe.wait_ge(S["b1_in"], 32)
                pe.transpose(psum[7][:, 0:EXPERTS * FF_TILES], b1_rows[:, :], ident[0:EXPERTS * FF_TILES, 0:EXPERTS * FF_TILES]).then_inc(S["b1_turned"], 1)
                pe.wait_ge(S["w_in"], 32)
                pe.wait_ge(S["xn_ready"], 1)
                for b in range(BATCH):
                    for k in range(DK):
                        n = b * DK + k
                        if n >= 4:
                            pe.wait_ge((S["turn_dve"] if k else S["turn_act"]), b - 1)
                        for q in range(TOK_TILES):
                            mm = pe.transpose(psum[n % 4][:, q * P:(q + 1) * P], xn[:, b * TOK_TILES + q, k * P:(k + 1) * P], ident[:, :])
                        mm.then_inc(S["turned"], 1)
                for b in range(BATCH):
                    pe.wait_ge(S["turn_act"], b + 1)
                    pe.wait_ge(S["turn_dve"], b + 1)
                    for q in range(TOK_TILES):
                        for k in range(DK):
                            t = b * TOK_TILES + q
                            mm = pe.matmul(psum[4][:, t * EB:(t + 1) * EB], xnT[:, b, k, q * P:(q + 1) * P], router[:, k, :], start=k == 0, stop=k == DK - 1)
                mm.then_inc(S["logit_mm"], 1)
                pe.wait_ge(S["masks_ready"], 1)
                pe.wait_ge(S["onehot_ready"], 1)
                pe.matmul(psum[5][:, 0:NTILE * EB], ones_b[:, :], onehot_b[:, :, :].rearrange("p t e -> p (t e)"), start=True, stop=True).then_inc(S["totals_mm"], 1)
                pe.matmul(psum[6][:, 0:NTILE * EB], before[:, :], onehot_b[:, :, :].rearrange("p t e -> p (t e)"), start=True, stop=True).then_inc(S["ranks"], 1)
                with pe.Fori(0, SLOT_TILES // 2) as i:
                    def turn(r):
                        pe.wait_ge(S[f"xs_in{r}"], i * 16 + 16)
                        pe.wait_ge(S["xsT_ready"], 2 * i + r if r else 2 * i)
                        for k in range(DK):
                            mm = pe.transpose(psum[0][:, k * P:(k + 1) * P], x_slots[:, r, k * P:(k + 1) * P], ident[:, :])
                        mm.then_inc(S["xs_turned"], 1)

                    def hidden(r):
                        pe.wait_ge(S["xsT_ready"], 2 * i + r + 1)
                        pe.wait_ge(S[f"w1_in{r}"], i * 16 + 16)
                        pe.wait_ge(S["relu_act"], 2 * i)
                        pe.wait_ge(S["relu_dve"], 2 * i)
                        for f in range(FF_TILES):
                            for k in range(DK):
                                mm = pe.matmul(psum[2 + 2 * r + f // 4][:, (f % 4) * P:(f % 4 + 1) * P], w1[:, r, k, f * P:(f + 1) * P],
                                               x_slotsT[:, r, k, :], start=k == 0, stop=k == DK - 1)
                        mm.then_inc(S[f"h_mm{r}"], 1)

                    def down(r):
                        pe.wait_ge(S["relu_act"], 2 * i + r + 1)
                        pe.wait_ge(S["relu_dve"], 2 * i + r + 1)
                        pe.wait_ge(S[f"w2_in{r}"], i * 16 + 16)
                        pe.wait_ge(S["y_ready"], 2 * i)
                        for f in range(FF_TILES):
                            mm = pe.matmul(psum[6 + r][:, 0:DIM], hiddenT[:, r, f, :], w2[:, r, f, :], start=f == 0, stop=f == FF_TILES - 1)
                        mm.then_inc(S["y_mm"], 1)

                    turn(0)
                    turn(1)
                    hidden(0)
                    hidden(1)
                    down(0)
                    down(1)

            @block.scalar
            def _(act):
                act.wait_ge(S["b1_turned"], 1)
                act.copy(b1T[:, :], psum[7][:, 0:EXPERTS * FF_TILES]).then_inc(S["b1_ready"], 1)
                act.wait_ge(S["stats_ready"], 1)
                act.activation(rstd[:, 0, :], moments[:, :, 1], ACT.Sqrt, bias=T["eps"][:, :]).then_inc(S["std_ready"], 1)
                for b in range(BATCH):
                    act.wait_ge(S["turned"], b * DK + 1)
                    act.copy(xnT[:, b, 0, :], psum[(b * DK) % 4][:, :]).then_inc(S["turn_act"], 1)
                act.wait_ge(S["shifted"], 1)
                act.activation(expd[:, :, :], logits[:, :, :], ACT.Exp).then_inc(S["exp_done"], 1)
                with act.Fori(0, SLOT_TILES // 2) as i:
                    def turned(r):
                        act.wait_ge(S["xs_turned"], 2 * i + r + 1)
                        act.copy(x_slotsT[:, r, :, :].rearrange("p k n -> p (k n)"), psum[0][:, 0:2 * P]).then_inc(S["xsT_ready"], 1)

                    def relu(r):
                        act.wait_ge(S["b1_picked"], 2 * i + r + 1)
                        act.wait_ge(S[f"h_mm{r}"], i + 1)
                        act.wait_ge(S["y_mm"], 2 * i)
                        for f in range(4):
                            s = act.activation(hiddenT[:, r, f, :], psum[2 + 2 * r][:, f * P:(f + 1) * P], ACT.Relu, bias=b1_t[:, r, f:f + 1])
                        s.then_inc(S["relu_act"], 1)

                    turned(0)
                    turned(1)
                    relu(0)
                    relu(1)
                    for r in range(2):
                        act.wait_ge(S["y_ready"], 2 * i + r + 1)
                        act.dma_start(y_slots_d.rearrange("(i r p) d -> i r p d", r=2, p=P)[bass.ds(i, 1), r].rearrange("a p d -> p (a d)"),
                                      y_slots[:, r, :]).then_inc(S[f"y_out{r}"], 16)

            @block.vector
            def _(dve):
                own = Steps(dve, S["dve_own"])

                def do(instruction):
                    own.done(instruction)
                    own.wait()

                s = layernorm_all(dve, own, S["stats_ready"], S["std_ready"], 1, x_res, stats, moments, rstd, xn)
                s.then_inc(S["xn_ready"], 1)
                for b in range(BATCH):
                    dve.wait_ge(S["turned"], b * DK + 2)
                    dve.tensor_copy(xnT[:, b, 1, :], psum[(b * DK + 1) % 4][:, :]).then_inc(S["turn_dve"], 1)
                wide = lambda ap: ap.rearrange("p (t a) -> p t a", a=1).broadcast_to([P, NTILE, EB])
                every = lambda ap: ap.rearrange("p (a e) -> p a e", a=1).broadcast_to([P, NTILE, EB])
                dve.wait_ge(S["logit_mm"], 1)
                do(dve.tensor_tensor(logits[:, :, :], psum[4][:, 0:NTILE * EB].rearrange("p (t e) -> p t e", e=EB), every(router_b[:, :]), ALU.add))
                do(dve.tensor_reduce(col[:, 0, :], logits[:, :, :], AX.X, ALU.max))
                dve.tensor_tensor(logits[:, :, :], logits[:, :, :], wide(col[:, 0, :]), ALU.subtract).then_inc(S["shifted"], 1)
                dve.wait_ge(S["exp_done"], 1)
                dve.wait_ge(S["iota_done"], 2)
                dve.tensor_reduce(col[:, 1, :], expd[:, :, :], AX.X, ALU.add)
                do(dve.tensor_reduce(col[:, 2, :], expd[:, :, :], AX.X, ALU.max))
                dve.reciprocal(col[:, 3, :], col[:, 1, :])
                do(dve.tensor_tensor(pick[:, :, :], expd[:, :, :], wide(col[:, 2, :]), ALU.is_ge))
                dve.tensor_tensor(gate[:, :], col[:, 2, :], col[:, 3, :], ALU.mult)
                do(dve.tensor_tensor(pick[:, :, :], pick[:, :, :], every(first_w[:, :]), ALU.mult))
                do(dve.tensor_reduce(col[:, 4, :], pick[:, :, :], AX.X, ALU.max))
                do(dve.tensor_tensor(onehot[:, :, :], pick[:, :, :], wide(col[:, 4, :]), ALU.is_equal))
                dve.tensor_copy(onehot_b[:, :, :], onehot[:, :, :]).then_inc(S["onehot_ready"], 1)
                dve.wait_ge(S["totals_mm"], 1)
                flat_ps = psum[5][:, 0:NTILE * EB].rearrange("p (t e) -> p t e", e=EB)
                dve.tensor_copy(totals[:, :, :], flat_ps)
                do(dve.tensor_copy(cum[:, 0, :, :], flat_ps))
                at, step = 0, 1
                while step < NTILE:
                    dve.tensor_copy(cum[:, 1 - at, 0:step, :], cum[:, at, 0:step, :])
                    do(dve.tensor_tensor(cum[:, 1 - at, step:, :], cum[:, at, step:, :], cum[:, at, 0:NTILE - step, :], ALU.add))
                    at, step = 1 - at, 2 * step
                do(dve.tensor_scalar(count_i[:, 0, :], cum[:, at, NTILE - 1, :], float(P - 1), None, ALU.add))
                do(dve.tensor_scalar(count_i[:, 1, :], count_i[:, 0, :], P.bit_length() - 1, None, ALU.arith_shift_right))
                dve.tensor_copy(need[:, 0, :], count_i[:, 1, :])
                do(dve.tensor_copy(need[:, 1, :], count_i[:, 1, :]))
                here, step = 1, 1
                while step < EB:
                    dve.tensor_copy(need[:, 3 - here, 0:step], need[:, here, 0:step])
                    do(dve.tensor_tensor(need[:, 3 - here, step:], need[:, here, step:], need[:, here, 0:EB - step], ALU.add))
                    here, step = 3 - here, 2 * step
                ends = need[:, here, :].rearrange("p (a e) -> p a e", a=1).broadcast_to([P, SLOT_TILES, EB])
                do(dve.tensor_tensor(past[:, :, :], tile_no[:, :].rearrange("p (t a) -> p t a", a=1).broadcast_to([P, SLOT_TILES, EB]), ends, ALU.is_ge))
                do(dve.tensor_reduce(owner_f[:, :], past[:, :, :], AX.X, ALU.add))
                dve.tensor_scalar(owner[:, :], owner_f[:, :], float(EB - 1), None, ALU.min).then_inc(S["owner_ready"], 1)
                do(dve.tensor_tensor(need[:, 3, :], need[:, here, :], need[:, 0, :], ALU.subtract))
                do(dve.tensor_scalar(need[:, 3, :], need[:, 3, :], float(P), None, ALU.mult))
                do(dve.tensor_tensor(where[:, :, :], cum[:, at, :, :], totals[:, :, :], ALU.subtract))
                dve.wait_ge(S["ranks"], 1)
                do(dve.tensor_tensor(where[:, :, :], where[:, :, :], psum[6][:, 0:NTILE * EB].rearrange("p (t e) -> p t e", e=EB), ALU.add))
                do(dve.tensor_tensor(where[:, :, :], where[:, :, :], every(need[:, 3, :]), ALU.add))
                do(dve.tensor_tensor(where[:, :, :], where[:, :, :], onehot[:, :, :], ALU.mult))
                do(dve.tensor_reduce(slot_f[:, :], where[:, :, :], AX.X, ALU.add))
                dve.tensor_copy(slot[:, :], slot_f[:, :]).then_inc(S["slot_ready"], 1)
                dve.wait_ge(S["b1_ready"], 1)
                dve.wait_ge(S["owner_ready"], 1)
                with dve.Fori(0, SLOT_TILES // 2) as i:
                    es = []
                    for r in range(2):
                        e = dve.value_load(owner[0:1, bass.ds(2 * i + r, 1)], min_val=0, max_val=EXPERTS - 1)
                        es.append(e)
                        dve.wait_ge(S["relu_act"], 2 * i)
                        dve.wait_ge(S["relu_dve"], 2 * i)
                        dve.tensor_copy(b1_t[:, r, :], b1T[:, bass.ds(e * FF_TILES, FF_TILES)]).then_inc(S["b1_picked"], 1)
                    for r in range(2):
                        dve.wait_ge(S["b1_picked"], 2 * i + r + 1)
                        dve.wait_ge(S[f"h_mm{r}"], i + 1)
                        dve.wait_ge(S["y_mm"], 2 * i)
                        for f in range(4, 8):
                            s = dve.tensor_scalar(hiddenT[:, r, f, :], psum[3 + 2 * r][:, (f - 4) * P:(f - 3) * P], b1_t[:, r, f:f + 1], 0.0, ALU.add, ALU.max)
                        s.then_inc(S["relu_dve"], 1)
                    for r in range(2):
                        dve.wait_ge(S[f"y_out{r}"], i * 16)
                        dve.wait_ge(S["y_mm"], 2 * i + r + 1)
                        dve.tensor_tensor(y_slots[:, r, :], psum[6 + r][:, 0:DIM], flat(b2_all[:, bass.ds(es[r], 1), :]), ALU.add).then_inc(S["y_ready"], 1)
                for t in range(ALL_TILES):
                    dve.wait_ge(gathered[t % 4], 16 * (t // 4 + 1))
                    dve.scalar_tensor_tensor(out=x_res[:, t, :], in0=y_tok[:, t % 4, :], scalar=gate[:, t:t + 1], in1=x_res[:, t, :],
                                             op0=ALU.mult, op1=ALU.add).then_inc(S["combined"], 1)


HD = 64
INNER = HEADS * HD
PAIRS = HEADS // 2
CLIP = 11.0


def cross_attention(nc, ctx_outer, T, A):
    with ExitStack() as ctx:
        def sb(name, shape, dt=F32):
            return ctx.enter_context(nc.sbuf_tensor("c_" + name, shape, dt))

        def sem(name):
            return ctx_outer.enter_context(nc.semaphore("c_" + name))

        score_ps = ctx.enter_context(nc.psum_tensor("c_scores", [P, 4, 512], F32))
        value_ps = ctx.enter_context(nc.psum_tensor("c_values", [P, 2, 512], F32))
        sum_ps = ctx.enter_context(nc.psum_tensor("c_sums", [P, 2, 512], F32))
        x_res, ident = T["x_res"], T["ident"]
        SCALE = HD ** -0.5
        LOW, HIGH = float(np.exp(-CLIP)), float(np.exp(CLIP))

        wq = sb("wq", [P, DK, INNER])
        wkv = sb("wkv", [P, DK, 2 * INNER])
        wo = sb("wo", [P, PAIRS, DIM])
        bo = sb("bo", [P, DIM])
        ln_col = sb("ln_col", [P, 4, DK])
        z1 = sb("z1", [P, ALL_TILES, DIM])
        stats = sb("stats", [P, ALL_TILES, 6])
        moments = sb("moments", [P, 3, ALL_TILES, 2])
        rstd = sb("rstd", [P, 3, 2, ALL_TILES])
        now = sb("now", [P, 2, 12])
        lat_b = sb("lat_b", [P, TOK_TILES, DIM])
        ctx_raw = sb("ctx_raw", [P, TOK_TILES, DIM])
        latT = sb("latT", [P, DK, SEQ])
        ctxT = sb("ctxT", [P, DK, SEQ])
        q_half = sb("q_half", [P, HEADS, SEQ])
        kT = sb("kT", [P, PAIRS, SEQ])
        v = sb("v", [P, TOK_TILES, INNER])
        ctx_all = v[:, :, :].rearrange("p t n -> p (t n)").rearrange("p (t d) -> p t d", d=DIM)
        prob = sb("prob", [P, 2, TOK_TILES, 2, SEQ])
        key_sum = sb("key_sum", [P, 2, 2, SEQ])
        rinv = key_sum
        oT = sb("oT", [P, PAIRS, SEQ])
        recip = sb("recip", [P, SEQ])
        ones = sb("ones", [P, HD])

        names = ("w_in ctx_all_in ln_in bo_in stats1 stats2 stats3 std1 std2 std3 half_zero ones_ready ctx_in lat_ready "
                 "pro_mm pro_act pro_dve scores exp clipped summed values sums normed wo_mm dve_own pool_own").split()
        S = {n: sem(n) for n in names}

        JOBS = [("lat", 0, "d"), ("lat", 1, "d"), ("ctx", 0, "a"), ("ctx", 1, "a")]
        JOBS += [("q", f, "ad") for f in range(PAIRS)] + [("k", f, "ad"[f % 2]) for f in range(PAIRS)]
        JOBS += [("v", f, "ad"[f % 2]) for f in range(8)]

        def copied(engine, upto):
            return sum(engine in e for _, _, e in JOBS[:upto])

        ACT_JOBS, DVE_JOBS, N_JOBS = copied("a", len(JOBS)), copied("d", len(JOBS)), len(JOBS)
        STEPS = PAIRS * TOK_TILES

        with nc.Block() as block:
            @block.sync
            def _(sp):
                sp.dma_start(ctx_all, A["ctx_1024"].rearrange("b (q p) d -> p (b q) d", p=P)).then_inc(S["ctx_all_in"], 16)
                sp.dma_start(wq[:, :, :], A["L1_xattn_Wq"].rearrange("(k p) n -> p k n", p=P)).then_inc(S["w_in"], 16)
                sp.dma_start(wkv[:, :, :], A["L1_xattn_Wkv"].rearrange("(k p) n -> p k n", p=P)).then_inc(S["w_in"], 16)
                sp.dma_start(wo[:, :, :], A["L1_xattn_Wo"].rearrange("(k p) n -> p k n", p=P)).then_inc(S["w_in"], 16)
                sp.dma_start(bo[:, :], A["L1_xattn_bo"].rearrange("(a n) -> a n", a=1).broadcast_to([P, DIM])).then_inc(S["bo_in"], 16)
                for i, n in enumerate(("ln_l_w", "ln_l_b", "ln_c_w", "ln_c_b")):
                    for k in range(DK):
                        sp.dma_start(ln_col[:, i, k:k + 1], A["L1_xattn_" + n][k * P:(k + 1) * P].rearrange("(p a) -> p a", a=1)).then_inc(S["ln_in"], 16)
                with sp.Fori(0, BATCH) as b:
                    sp.wait_ge(S["pro_mm"], b * N_JOBS)
                    sp.dma_start(ctx_raw[:, :, :], A["ctx_1024"][bass.ds(b, 1)].rearrange("a (q p) d -> p (a q) d", p=P)).then_inc(S["ctx_in"], 16)

            @block.gpsimd
            def _(pool):
                own = Steps(pool, S["pool_own"])
                pool.memset(ones[:, :], 1.0).then_inc(S["ones_ready"], 1)
                pool.memset(q_half[:, :, :], 0.0).then_inc(S["half_zero"], 1)
                with pool.Fori(0, BATCH) as b:
                    own.loop(b, PAIRS * 2)
                    for p in range(PAIRS):
                        acc = key_sum[:, p % 2, :, :]
                        for k in range(1, TOK_TILES):
                            if k > 1:
                                own.wait()
                            elif p >= 2:
                                pool.wait_ge(S["sums"], b * PAIRS + p - 1)
                            else:
                                pool.wait_ge(S["sums"], b * PAIRS)
                            pool.wait_ge(S["clipped"], b * STEPS + p * TOK_TILES + k + 1)
                            first = prob[:, p % 2, 0, :, :] if k == 1 else acc
                            s = pool.tensor_tensor(acc, first, prob[:, p % 2, k, :, :], ALU.add)
                            if k < TOK_TILES - 1:
                                own.done(s)
                        s.then_inc(S["summed"], 1)
                    own.end_loop(BATCH)

            @block.tensor
            def _(pe):
                pe.wait_ge(S["w_in"], 48)
                pe.wait_ge(S["ones_ready"], 1)
                with pe.Fori(0, BATCH) as b:
                    for j, (kind, f, _) in enumerate(JOBS):
                        bank = score_ps[:, j % 4, :]
                        if j >= 4:
                            upto = max(j - 3, 2 if kind == "q" else 4)
                            pe.wait_ge(S["pro_act"], b * ACT_JOBS + copied("a", upto))
                            pe.wait_ge(S["pro_dve"], b * DVE_JOBS + copied("d", upto))
                        else:
                            pe.wait_ge(S["exp"], b * STEPS)
                            pe.wait_ge(S["normed"], b * (PAIRS + 2))
                        if kind in ("lat", "ctx"):
                            if f == 0 and kind == "lat":
                                pe.wait_ge(S["lat_ready"], 2 * b + 1)
                            if f == 0 and kind == "ctx":
                                pe.wait_ge(S["lat_ready"], 2 * b + 2)
                            src = lat_b if kind == "lat" else ctx_raw
                            for q in range(TOK_TILES):
                                mm = pe.transpose(bank[:, q * P:(q + 1) * P], src[:, q, f * P:(f + 1) * P], ident[:, :])
                        elif kind == "q":
                            for k in range(DK):
                                mm = pe.matmul(bank, wq[:, k, f * P:(f + 1) * P], latT[:, k, :], start=k == 0, stop=k == DK - 1)
                        elif kind == "k":
                            for k in range(DK):
                                mm = pe.matmul(bank, wkv[:, k, f * P:(f + 1) * P], ctxT[:, k, :], start=k == 0, stop=k == DK - 1)
                        else:
                            t, half = f // 2, f % 2
                            for k in range(DK):
                                mm = pe.matmul(bank, ctxT[:, k, t * P:(t + 1) * P], wkv[:, k, INNER + half * 512:INNER + (half + 1) * 512],
                                               start=k == 0, stop=k == DK - 1)
                        mm.then_inc(S["pro_mm"], 1)
                    pe.wait_ge(S["pro_act"], (b + 1) * ACT_JOBS)
                    pe.wait_ge(S["pro_dve"], (b + 1) * DVE_JOBS)
                    for p in range(PAIRS + 1):
                        for k in range(TOK_TILES):
                            n = p * TOK_TILES + k
                            if p < PAIRS:
                                if n >= 2:
                                    pe.wait_ge(S["exp"], b * STEPS + n - 1)
                                for m in range(2):
                                    mm = pe.matmul(score_ps[:, 2 * (k % 2) + m, :], kT[:, p, k * P:(k + 1) * P], q_half[:, 2 * p + m, :], start=True, stop=True)
                                mm.then_inc(S["scores"], 1)
                            if p:
                                g = p - 1
                                pe.wait_ge(S["clipped"], b * STEPS + g * TOK_TILES + k + 1)
                                if k == 0 and g >= 2:
                                    pe.wait_ge(S["normed"], b * (PAIRS + 2) + g - 1)
                                for m in range(2):
                                    mm = pe.matmul(value_ps[m * HD:(m + 1) * HD, g % 2, :], v[:, k, (2 * g + m) * HD:(2 * g + m + 1) * HD],
                                                   prob[:, g % 2, k, m, :], start=k == 0, stop=k == TOK_TILES - 1)
                                mm.then_inc(S["values"], 1)
                        if p:
                            pe.wait_ge(S["summed"], b * PAIRS + p)
                            for m in range(2):
                                mm = pe.matmul(sum_ps[m * HD:(m + 1) * HD, (p - 1) % 2, :], ones[:, :], key_sum[:, (p - 1) % 2, m, :], start=True, stop=True)
                            mm.then_inc(S["sums"], 1)
                    pe.wait_ge(S["normed"], b * (PAIRS + 2) + PAIRS)
                    for q in range(TOK_TILES):
                        for k in range(PAIRS):
                            mm = pe.matmul(score_ps[:, q // 2, (q % 2) * DIM:(q % 2 + 1) * DIM], oT[:, k, q * P:(q + 1) * P], wo[:, k, :],
                                           start=k == 0, stop=k == PAIRS - 1)
                        if q % 2:
                            mm.then_inc(S["wo_mm"], 1)

            @block.scalar
            def _(act):
                for i in range(3):
                    act.wait_ge(S[f"stats{i + 1}"], 1)
                    act.activation(rstd[:, i, 0, :], moments[:, i, :, 1], ACT.Sqrt, bias=T["eps"][:, :]).then_inc(S[f"std{i + 1}"], 1)
                act.wait_ge(S["ln_in"], 64 * DK)
                act.wait_ge(S["half_zero"], 1)
                with act.Fori(0, BATCH) as b:
                    for j, (kind, f, engines) in enumerate(JOBS):
                        if "a" not in engines:
                            continue
                        bank = score_ps[:, j % 4, :]
                        act.wait_ge(S["pro_mm"], b * N_JOBS + j + 1)
                        if kind == "ctx":
                            s = act.activation(ctxT[:, f, :], bank, ACT.Identity, scale=ln_col[:, 2, f:f + 1], bias=ln_col[:, 3, f:f + 1])
                        elif kind == "q":
                            s = act.activation(q_half[0:HD, 2 * f, :], bank[0:HD, :], ACT.Copy, scale=SCALE)
                        elif kind == "k":
                            s = act.copy(kT[:, f, :], bank)
                        else:
                            s = act.copy(v[:, f // 2, (f % 2) * 512:(f % 2 + 1) * 512], bank)
                        s.then_inc(S["pro_act"], 1)
                    for p in range(PAIRS):
                        for k in range(TOK_TILES):
                            n = p * TOK_TILES + k
                            if p >= 2:
                                act.wait_ge(S["values"], b * STEPS + n - 2 * TOK_TILES + 1)
                                if k == 0:
                                    act.wait_ge(S["summed"], b * PAIRS + p - 1)
                            act.wait_ge(S["scores"], b * STEPS + n + 1)
                            act.activation(prob[:, p % 2, k, :, :], score_ps[:, 2 * (k % 2):2 * (k % 2) + 2, :], ACT.Exp).then_inc(S["exp"], 1)

            @block.vector
            def _(dve):
                own = Steps(dve, S["dve_own"])

                def stats_of(i, src):
                    for t in range(ALL_TILES):
                        s = dve.bn_stats(stats[:, t, :], src[:, t, :])
                    own.done(s)
                    own.wait()
                    for t in range(ALL_TILES):
                        s = dve.bn_aggr(moments[:, i, t, :], stats[:, t, :])
                    own.done(s)
                    own.wait()
                    dve.tensor_copy(now[:, 0, i:i + 1], moments[:, i, 0, 0:1]).then_inc(S[f"stats{i + 1}"], 1)

                def root_of(i):
                    dve.wait_ge(S[f"std{i + 1}"], 1)
                    own.done(dve.reciprocal(rstd[:, i, 1, :], rstd[:, i, 0, :]))
                    own.wait()

                stats_of(0, x_res)
                root_of(0)
                for t in range(ALL_TILES):
                    s = dve.tensor_scalar(z1[:, t, :], x_res[:, t, :], moments[:, 0, t, 0:1], rstd[:, 0, 1, t:t + 1], ALU.subtract, ALU.mult)
                own.done(s)
                own.wait()
                stats_of(1, z1)
                root_of(1)
                dve.wait_ge(S["ctx_all_in"], 16)
                stats_of(2, ctx_all)
                root_of(2)
                dve.wait_ge(S["bo_in"], 16)
                own.done(dve.tensor_tensor(x_res[:, :, :], x_res[:, :, :], bo[:, :].rearrange("p (a n) -> p a n", a=1).broadcast_to([P, ALL_TILES, DIM]), ALU.add))
                own.wait()
                dve.wait_ge(S["ln_in"], 64 * DK)
                dve.wait_ge(S["half_zero"], 1)
                with dve.Fori(0, BATCH) as b:
                    own.loop(b, 4 + PAIRS)
                    for i in range(2):
                        mom = moments[:, i + 1, :, :].rearrange("p (b q) c -> p b (q c)", b=BATCH)
                        rs = rstd[:, i + 1, 1, :].rearrange("p (b q) -> p b q", b=BATCH)
                        own.done(dve.tensor_copy(now[:, i, 0:8], mom[:, bass.ds(b, 1), :].rearrange("p a n -> p (a n)")))
                        own.done(dve.tensor_copy(now[:, i, 8:12], rs[:, bass.ds(b, 1), :].rearrange("p a n -> p (a n)")))
                    own.wait()
                    zv = z1[:, :, :].rearrange("p (b q) d -> p b (q d)", b=BATCH)
                    for q in range(TOK_TILES):
                        s = dve.tensor_scalar(lat_b[:, q, :], flat(zv[:, bass.ds(b, 1), q * DIM:(q + 1) * DIM]),
                                              now[:, 0, 2 * q:2 * q + 1], now[:, 0, 8 + q:9 + q], ALU.subtract, ALU.mult)
                    s.then_inc(S["lat_ready"], 1)
                    dve.wait_ge(S["ctx_in"], b * 16 + 16)
                    for q in range(TOK_TILES):
                        s = dve.tensor_scalar(ctx_raw[:, q, :], ctx_raw[:, q, :], now[:, 1, 2 * q:2 * q + 1], now[:, 1, 8 + q:9 + q],
                                              ALU.subtract, ALU.mult)
                    s.then_inc(S["lat_ready"], 1)
                    for j, (kind, f, engines) in enumerate(JOBS):
                        if "d" not in engines:
                            continue
                        bank = score_ps[:, j % 4, :]
                        dve.wait_ge(S["pro_mm"], b * N_JOBS + j + 1)
                        if kind == "lat":
                            s = dve.tensor_scalar(latT[:, f, :], bank, ln_col[:, 0, f:f + 1], ln_col[:, 1, f:f + 1], ALU.mult, ALU.add)
                        elif kind == "q":
                            s = dve.tensor_scalar(q_half[HD:P, 2 * f + 1, :], bank[HD:P, :], SCALE, None, ALU.mult)
                        elif kind == "k":
                            s = dve.tensor_copy(kT[:, f, :], bank)
                        else:
                            s = dve.tensor_copy(v[:, f // 2, (f % 2) * 512:(f % 2 + 1) * 512], bank)
                        s.then_inc(S["pro_dve"], 1)

                    def normalise(g):
                        dve.wait_ge(S["sums"], b * PAIRS + g + 1)
                        dve.wait_ge(S["normed"], b * (PAIRS + 2) + g)
                        own.done(dve.reciprocal(recip[:, :], sum_ps[:, g % 2, :]))
                        own.wait()
                        dve.tensor_tensor(oT[:, g, :], value_ps[:, g % 2, :], recip[:, :], ALU.mult).then_inc(S["normed"], 1)

                    for p in range(PAIRS + 2):
                        for k in range(TOK_TILES):
                            if p < PAIRS:
                                dve.wait_ge(S["exp"], b * STEPS + p * TOK_TILES + k + 1)
                                tile = prob[:, p % 2, k, :, :]
                                dve.tensor_scalar(tile, tile, LOW, HIGH, ALU.max, ALU.min).then_inc(S["clipped"], 1)
                            if k == 1 and p >= 2:
                                normalise(p - 2)
                    xv = x_res[:, :, :].rearrange("p (b q) d -> p b (q d)", b=BATCH)
                    for h in range(2):
                        dve.wait_ge(S["wo_mm"], 2 * b + h + 1)
                        xq = flat(xv[:, bass.ds(b, 1), h * 512:(h + 1) * 512])
                        dve.tensor_tensor(xq, score_ps[:, h, :], xq, ALU.add).then_inc(S["normed"], 1)
                    own.end_loop(BATCH)


HID = 1024
HID_TILES = HID // P
ROUND = 1.5 * 2.0 ** 23
QMAX = 127.0
RING = 4


def ternary_ffn(nc, ctx_outer, T, A):
    with ExitStack() as ctx:
        def sb(name, shape, dt=F32):
            return ctx.enter_context(nc.sbuf_tensor("d_" + name, shape, dt))

        def sem(name):
            return ctx_outer.enter_context(nc.semaphore("d_" + name))

        wide_ps = [ctx.enter_context(nc.psum_tensor(f"d_wide{i}", [P, 512], F32)) for i in range(6)]
        bf_ps = [ctx.enter_context(nc.psum_tensor(f"d_bf{i}", [P, 1024], BF16)) for i in range(2)]
        x_res, ident = T["x_res"], T["ident"]

        w_raw = sb("w_raw", [P, 2, 2048])
        w_tern = sb("w_tern", [P, 2, 2048], BF16)
        w1T = sb("w1T", [P, DK, HID], BF16)
        w2T = sb("w2T", [P, HID_TILES, DIM], BF16)
        ident_b = sb("ident_b", [P, P], BF16)
        ones = sb("ones", [P, P])
        tap_rows = sb("tap_rows", [HID_TILES, 4, P])
        tap_raw = sb("tap_raw", [HID_TILES, P * 3])
        taps = sb("taps", [P, 4, HID_TILES])
        w_sum = sb("w_sum", [P, 2])
        w_inv = sb("w_inv", [P, 2])
        w_scale = sb("w_scale", [P, 2])
        stats = sb("stats", [P, ALL_TILES, 6])
        moments = sb("moments", [P, ALL_TILES, 2])
        rstd = sb("rstd", [P, 2, ALL_TILES])
        z = sb("z", [P, ALL_TILES, DIM])
        tok = sb("tok", [P, 4, ALL_TILES])
        spread = sb("spread", [P, ALL_TILES, P])
        undo = sb("undo", [P, ALL_TILES * P])
        xq_b = sb("xq_b", [P, TOK_TILES, DIM], BF16)
        xqT = sb("xqT", [P, DK, SEQ], BF16)
        h_pad = sb("h_pad", [P, RING, SEQ + 2])
        conv = sb("conv", [P, RING, SEQ])
        act_h = sb("act_h", [P, HID_TILES, SEQ])
        top = sb("top", [P, SEQ])
        tok2 = sb("tok2", [P, 4, TOK_TILES])
        spread2 = sb("spread2", [P, TOK_TILES, P])
        scaled = sb("scaled", [P, 2, SEQ])
        hq = sb("hq", [P, HID_TILES, SEQ], BF16)

        names = ("w_in taps_in ones_ready pads_zero w_summed w_total tern_ready w_turned wT_ready taps_turned taps_ready "
                 "stats_ready std_ready spread_ready undo_turned undo_ready xq_ready xq_turned xqT_ready h_mm h_ready centre "
                 "conv_done silu top_done top_turned spread2_ready up_turned hq_ready y_mm y_added dve_own pool_own identb_ready").split()
        S = {n: sem(n) for n in names}

        with nc.Block() as block:
            @block.sync
            def _(sp):
                sp.dma_start(w_raw[:, 0, :].rearrange("p (f d) -> p f d", d=DIM), A["L1_ffn_w1"].rearrange("(f p) d -> p f d", p=P)).then_inc(S["w_in"], 16)
                sp.dma_start(w_raw[:, 1, :].rearrange("p (o h) -> p o h", h=HID), A["L1_ffn_w2"].rearrange("(o p) h -> p o h", p=P)).then_inc(S["w_in"], 16)
                sp.dma_start(tap_raw[:, :], A["L1_ffn_conv_w"].rearrange("(f p) a j -> f (p a j)", p=P)).then_inc(S["taps_in"], 16)
                sp.dma_start(tap_rows[:, 3, :], A["L1_ffn_conv_b"].rearrange("(f p) -> f p", p=P)).then_inc(S["taps_in"], 16)

            @block.gpsimd
            def _(pool):
                pool.memset(ones[:, :], 1.0).then_inc(S["ones_ready"], 1)
                pool.memset(h_pad[:, :, :], 0.0).then_inc(S["pads_zero"], 1)

            @block.tensor
            def _(pe):
                pe.wait_ge(S["taps_in"], 32)
                pe.wait_ge(S["taps_turned"], 1)
                for j in range(4):
                    mm = pe.transpose(wide_ps[0][:, j * HID_TILES:(j + 1) * HID_TILES], tap_rows[:, j, :], ident[0:HID_TILES, 0:HID_TILES])
                mm.then_inc(S["taps_turned"], 1)
                pe.wait_ge(S["ones_ready"], 1)
                pe.wait_ge(S["w_summed"], 1)
                pe.matmul(wide_ps[1][:, 0:2], ones[:, :], w_sum[:, :], start=True, stop=True).then_inc(S["w_total"], 1)
                pe.wait_ge(S["spread_ready"], 1)
                for b in range(BATCH):
                    for q in range(TOK_TILES):
                        mm = pe.transpose(wide_ps[2 + b][:, q * P:(q + 1) * P], spread[:, b * TOK_TILES + q, :], ident[:, :])
                    mm.then_inc(S["undo_turned"], 1)
                pe.wait_ge(S["tern_ready"], 1)
                for k in range(DK):
                    for f in range(HID_TILES):
                        mm = pe.transpose(bf_ps[k][:, f * P:(f + 1) * P], w_tern[:, 0, f * DIM + k * P:f * DIM + (k + 1) * P], ident_b[:, :])
                mm.then_inc(S["w_turned"], 1)
                pe.wait_ge(S["tern_ready"], 2)
                pe.wait_ge(S["wT_ready"], 1)
                for o in range(DK):
                    for f in range(HID_TILES):
                        mm = pe.transpose(bf_ps[o][:, f * P:(f + 1) * P], w_tern[:, 1, o * HID + f * P:o * HID + (f + 1) * P], ident_b[:, :])
                mm.then_inc(S["w_turned"], 1)
                pe.wait_ge(S["wT_ready"], 2)
                pe.wait_ge(S["undo_ready"], 1)
                with pe.Fori(0, BATCH) as b:
                    pe.wait_ge(S["xq_ready"], b + 1)
                    for k in range(DK):
                        for q in range(TOK_TILES):
                            mm = pe.transpose(bf_ps[0][:, (k * TOK_TILES + q) * P:(k * TOK_TILES + q + 1) * P], xq_b[:, q, k * P:(k + 1) * P], ident_b[:, :])
                    mm.then_inc(S["xq_turned"], 1)
                    pe.wait_ge(S["xqT_ready"], b + 1)
                    for f in range(HID_TILES):
                        if f < 2:
                            pe.wait_ge(S["h_ready"], b * HID_TILES)
                        else:
                            pe.wait_ge(S["h_ready"], b * HID_TILES + f - 1)
                        for k in range(DK):
                            mm = pe.matmul(wide_ps[f % 2][:, :], w1T[:, k, f * P:(f + 1) * P], xqT[:, k, :], start=k == 0, stop=k == DK - 1)
                        mm.then_inc(S["h_mm"], 1)
                    pe.wait_ge(S["top_done"], b + 1)
                    for q in range(TOK_TILES):
                        mm = pe.transpose(wide_ps[2][:, q * P:(q + 1) * P], top[:, q * P:(q + 1) * P], ident[:, :])
                    mm.then_inc(S["top_turned"], 1)
                    pe.wait_ge(S["spread2_ready"], b + 1)
                    for q in range(TOK_TILES):
                        mm = pe.transpose(wide_ps[3][:, q * P:(q + 1) * P], spread2[:, q, :], ident[:, :])
                    mm.then_inc(S["up_turned"], 1)
                    pe.wait_ge(S["hq_ready"], (b + 1) * HID_TILES)
                    for q in range(TOK_TILES):
                        for f in range(HID_TILES):
                            mm = pe.matmul(wide_ps[4 + q // 2][:, (q % 2) * DIM:(q % 2 + 1) * DIM], hq[:, f, q * P:(q + 1) * P], w2T[:, f, :],
                                           start=f == 0, stop=f == HID_TILES - 1)
                        if q % 2:
                            mm.then_inc(S["y_mm"], 1)

            @block.scalar
            def _(act):
                act.wait_ge(S["stats_ready"], 1)
                act.activation(rstd[:, 0, :], moments[:, :, 1], ACT.Sqrt, bias=T["eps"][:, :]).then_inc(S["std_ready"], 1)
                for b in range(BATCH):
                    act.wait_ge(S["undo_turned"], b + 1)
                    s = act.copy(undo[:, b * SEQ:(b + 1) * SEQ], wide_ps[2 + b][:, :])
                s.then_inc(S["undo_ready"], 1)
                act.wait_ge(S["w_turned"], 1)
                for k in range(DK):
                    s = act.copy(w1T[:, k, :], bf_ps[k][:, :])
                s.then_inc(S["wT_ready"], 1)
                act.wait_ge(S["w_turned"], 2)
                for o in range(DK):
                    s = act.copy(w2T[:, :, o * P:(o + 1) * P], bf_ps[o][:, :].rearrange("p (f n) -> p f n", n=P))
                s.then_inc(S["wT_ready"], 1)
                act.wait_ge(S["taps_ready"], 1)
                with act.Fori(0, BATCH) as b:
                    act.wait_ge(S["xq_turned"], b + 1)
                    act.copy(xqT[:, :, :].rearrange("p k n -> p (k n)"), bf_ps[0][:, :]).then_inc(S["xqT_ready"], 1)
                    for f in range(HID_TILES + 2):
                        if f < HID_TILES:
                            act.wait_ge(S["h_ready"], b * HID_TILES + f + 1)
                            if f >= RING:
                                act.wait_ge(S["silu"], b * HID_TILES + f - RING + 1)
                            act.activation(conv[:, f % RING, :], h_pad[:, f % RING, 1:SEQ + 1], ACT.Identity, scale=taps[:, 1, f:f + 1],
                                           bias=taps[:, 3, f:f + 1]).then_inc(S["centre"], 1)
                        if f >= 2:
                            act.wait_ge(S["conv_done"], b * HID_TILES + f - 1)
                            act.activation(act_h[:, f - 2, :], conv[:, (f - 2) % RING, :], ACT.Silu).then_inc(S["silu"], 1)

            @block.vector
            def _(dve):
                own = Steps(dve, S["dve_own"])

                def do(instruction):
                    own.done(instruction)
                    own.wait()

                dve.tensor_copy(ident_b[:, :], ident[:, :]).then_inc(S["identb_ready"], 1)
                dve.wait_ge(S["taps_in"], 32)
                for j in range(3):
                    s = dve.tensor_copy(tap_rows[:, j, :], tap_raw[:, :].rearrange("f (p j) -> f j p", j=3)[:, j, :])
                s.then_inc(S["taps_turned"], 1)
                dve.wait_ge(S["w_in"], 32)
                for i in range(2):
                    s = dve.tensor_reduce(w_sum[:, i:i + 1], w_raw[:, i, :], AX.X, ALU.add, apply_absolute_value=True)
                s.then_inc(S["w_summed"], 1)
                s = layernorm_all(dve, own, S["stats_ready"], S["std_ready"], 1, x_res, stats, moments, rstd, z)
                do(s)
                do(dve.tensor_reduce(tok[:, 0, :], z[:, :, :], AX.X, ALU.max, apply_absolute_value=True))
                do(dve.tensor_scalar(tok[:, 0, :], tok[:, 0, :], 1e-5, None, ALU.max))
                dve.tensor_scalar(tok[:, 3, :], tok[:, 0, :], 1.0 / QMAX, None, ALU.mult)
                do(dve.reciprocal(tok[:, 1, :], tok[:, 0, :]))
                do(dve.tensor_scalar(tok[:, 2, :], tok[:, 1, :], QMAX, None, ALU.mult))
                dve.wait_ge(S["ones_ready"], 1)
                dve.tensor_tensor(spread[:, :, :], ones[:, :].rearrange("p (a n) -> p a n", a=1).broadcast_to([P, ALL_TILES, P]),
                                  tok[:, 3, :].rearrange("p (t a) -> p t a", a=1).broadcast_to([P, ALL_TILES, P]), ALU.mult).then_inc(S["spread_ready"], 1)
                for t in range(ALL_TILES):
                    s = dve.tensor_scalar(z[:, t, :], z[:, t, :], tok[:, 2, t:t + 1], ROUND, ALU.mult, ALU.add)
                dve.wait_ge(S["w_total"], 1)
                do(dve.tensor_scalar(w_inv[:, :], wide_ps[1][:, 0:2], 1.0 / (HID * DIM), 1e-5, ALU.mult, ALU.max))
                do(dve.reciprocal(w_scale[:, :], w_inv[:, :]))
                for i in range(2):
                    do(dve.tensor_scalar(w_raw[:, i, :], w_raw[:, i, :], w_scale[:, i:i + 1], ROUND, ALU.mult, ALU.add))
                    do(dve.tensor_scalar(w_raw[:, i, :], w_raw[:, i, :], ROUND + 1.0, ROUND - 1.0, ALU.min, ALU.max))
                    dve.tensor_scalar(w_tern[:, i, :], w_raw[:, i, :], ROUND, None, ALU.subtract).then_inc(S["tern_ready"], 1)
                dve.wait_ge(S["taps_turned"], 2)
                do(dve.tensor_scalar(taps[:, 0:3, :].rearrange("p j f -> p (j f)"), wide_ps[0][:, 0:3 * HID_TILES], w_inv[:, 0:1], None, ALU.mult))
                dve.tensor_copy(taps[:, 3, :], wide_ps[0][:, 3 * HID_TILES:4 * HID_TILES]).then_inc(S["taps_ready"], 1)
                dve.wait_ge(S["taps_ready"], 1)
                dve.wait_ge(S["pads_zero"], 1)
                dve.wait_ge(S["undo_ready"], 1)
                with dve.Fori(0, BATCH) as b:
                    own.loop(b, DVE_D)
                    zv = z[:, :, :].rearrange("p (b q) d -> p b (q d)", b=BATCH)
                    dve.tensor_scalar(xq_b[:, :, :].rearrange("p q d -> p (q d)"), flat(zv[:, bass.ds(b, 1), :]), ROUND, None, ALU.subtract).then_inc(S["xq_ready"], 1)

                    for f in range(HID_TILES + 1):
                        if f < HID_TILES:
                            dve.wait_ge(S["h_mm"], b * HID_TILES + f + 1)
                            if f >= RING:
                                dve.wait_ge(S["conv_done"], b * HID_TILES + f - RING + 1)
                            dve.tensor_tensor(h_pad[:, f % RING, 1:SEQ + 1], wide_ps[f % 2][:, :], undo[:, bass.ds(b * SEQ, SEQ)], ALU.mult).then_inc(S["h_ready"], 1)
                        if 1 <= f <= HID_TILES:
                            g = f - 1
                            c = conv[:, g % RING, :]
                            dve.wait_ge(S["centre"], b * HID_TILES + g + 1)
                            own.done(dve.scalar_tensor_tensor(out=c, in0=h_pad[:, g % RING, 0:SEQ], scalar=taps[:, 0, g:g + 1], in1=c, op0=ALU.mult, op1=ALU.add))
                            own.wait()
                            dve.scalar_tensor_tensor(out=c, in0=h_pad[:, g % RING, 2:SEQ + 2], scalar=taps[:, 2, g:g + 1], in1=c,
                                                     op0=ALU.mult, op1=ALU.add).then_inc(S["conv_done"], 1)
                    dve.wait_ge(S["silu"], (b + 1) * HID_TILES)
                    dve.tensor_reduce(top[:, :], act_h[:, :, :].rearrange("p f n -> p n f"), AX.X, ALU.max, apply_absolute_value=True).then_inc(S["top_done"], 1)
                    dve.wait_ge(S["top_turned"], b + 1)
                    do(dve.tensor_reduce(tok2[:, 0, :], wide_ps[2][:, :].rearrange("p (q n) -> p q n", n=P), AX.X, ALU.max))
                    do(dve.tensor_scalar(tok2[:, 0, :], tok2[:, 0, :], 1e-5, None, ALU.max))
                    do(dve.tensor_scalar(tok2[:, 3, :], tok2[:, 0, :], w_inv[:, 1:2], 1.0 / QMAX, ALU.mult, ALU.mult))
                    do(dve.reciprocal(tok2[:, 1, :], tok2[:, 0, :]))
                    do(dve.tensor_scalar(tok2[:, 2, :], tok2[:, 1, :], QMAX, None, ALU.mult))
                    dve.tensor_tensor(spread2[:, :, :], ones[:, :].rearrange("p (a n) -> p a n", a=1).broadcast_to([P, TOK_TILES, P]),
                                      tok2[:, 2, :].rearrange("p (t a) -> p t a", a=1).broadcast_to([P, TOK_TILES, P]), ALU.mult).then_inc(S["spread2_ready"], 1)
                    dve.wait_ge(S["up_turned"], b + 1)
                    for f in range(HID_TILES):
                        if f >= 2:
                            dve.wait_ge(S["hq_ready"], b * HID_TILES + f - 1)
                        else:
                            dve.wait_ge(S["hq_ready"], b * HID_TILES)
                        do(dve.tensor_tensor(scaled[:, f % 2, :], wide_ps[3][:, :], act_h[:, f, :], ALU.mult))
                        dve.tensor_scalar(hq[:, f, :], scaled[:, f % 2, :], ROUND, ROUND, ALU.add, ALU.subtract).then_inc(S["hq_ready"], 1)
                    xv = x_res[:, :, :].rearrange("p (b q) d -> p b (q d)", b=BATCH)
                    for q in range(TOK_TILES):
                        dve.wait_ge(S["y_mm"], 2 * b + q // 2 + 1)
                        xq = flat(xv[:, bass.ds(b, 1), q * DIM:(q + 1) * DIM])
                        dve.scalar_tensor_tensor(out=xq, in0=wide_ps[4 + q // 2][:, (q % 2) * DIM:(q % 2 + 1) * DIM], scalar=tok2[:, 3, q:q + 1], in1=xq,
                                                 op0=ALU.mult, op1=ALU.add).then_inc(S["y_added"], 1)
                    dve.wait_ge(S["y_added"], (b + 1) * TOK_TILES)
                    own.end_loop(BATCH)


DVE_D = HID_TILES + 5 + HID_TILES


def program(nc, A, out):
    with ExitStack() as ctx:
        T = {}
        T["x_res"] = ctx.enter_context(nc.sbuf_tensor("x_res", [P, ALL_TILES, DIM], F32))
        T["ident"] = ctx.enter_context(nc.sbuf_tensor("ident", [P, P], F32))
        T["eps"] = ctx.enter_context(nc.sbuf_tensor("eps", [P, 1], F32))
        T["ident_ready"] = ctx.enter_context(nc.semaphore("ident_ready"))
        T["stored"] = ctx.enter_context(nc.semaphore("stored"))
        T["ident_count"] = 2
        with nc.Block() as block:
            @block.gpsimd
            def _(pool):
                pool.memset(T["ident"][:, :], 0.0).then_inc(T["ident_ready"], 1)
                pool.memset(T["eps"][:, :], EPS)
                pool.wait_ge(T["ident_ready"], 1)
                pool.affine_select(out=T["ident"][:, :], in_=T["ident"][:, :], compare_op=ALU.not_equal, fill=1.0, base=0,
                                   pattern=[[-1, P]], channel_multiplier=1).then_inc(T["ident_ready"], 1)
        diff_attention(nc, ctx, T, A)
        experts(nc, ctx, T, A)
        cross_attention(nc, ctx, T, A)
        ternary_ffn(nc, ctx, T, A)
        with nc.Block() as block:
            @block.sync
            def _(sp):
                sp.dma_start(out.rearrange("b (q p) d -> p (b q) d", p=P), T["x_res"][:, :, :]).then_inc(T["stored"], 16)
                sp.wait_ge(T["stored"], 16)


_OUT = (BATCH, SEQ, DIM)


def kernel(**inputs):
    import concourse.bacc as bacc
    from concourse.bass_utils import run_bass_kernel_spmd

    nc = bacc.Bacc("TRN2", target_bir_lowering=False, num_devices=1)
    arrays, args = {}, {}
    for name, value in inputs.items():
        a = np.ascontiguousarray(value)
        arrays[f"in_{name}_dram"] = a
        args[name] = nc.dram_tensor(f"in_{name}_dram", a.shape, mybir.dt.from_np(a.dtype), kind="ExternalInput").ap()
    out = nc.dram_tensor("out_0_dram", _OUT, F32, kind="ExternalOutput").ap()
    program(nc, args, out)
    r = run_bass_kernel_spmd(nc, [arrays], core_ids=[0])
    return r.results[0]["out_0_dram"]
```

```python
from contextlib import ExitStack

import numpy as np

import concourse.bass as bass
from concourse import mybir

F32 = mybir.dt.float32
BF16 = mybir.dt.bfloat16
I32 = mybir.dt.int32
ALU = mybir.AluOpType
ACT = mybir.ActivationFunctionType
AX = mybir.AxisListType

P = 128
BATCH, SEQ, DIM = 4, 512, 256
TOK_TILES = SEQ // P
ALL_TILES = BATCH * TOK_TILES
DK = DIM // P
EPS = 1e-5

DH = 16
HEADS = 16
MAPS = 2
FEATS = HEADS * MAPS * DH
FEAT_TILES = FEATS // P
MAPS_PER_TILE = P // DH
LAMBDA_INIT = 0.8


class Steps:

    def __init__(self, eng, sem):
        self.eng, self.sem, self.base, self.n = eng, sem, 0, 0
        self.turn = self.per_turn = None

    def loop(self, turn, per_turn, start=0):
        self.base, self.n, self.turn, self.per_turn = self.base + self.n - start * per_turn, 0, turn, per_turn
        self.start = start

    def end_loop(self, turns):
        assert self.n == self.per_turn, f"{self.sem} counts {self.n} per turn, not {self.per_turn}"
        self.base, self.n, self.turn = self.base + (self.start + turns) * self.per_turn, 0, None

    def done(self, instruction):
        instruction.then_inc(self.sem, 1)
        self.n += 1
        return self.n

    def wait(self, n=None):
        n = self.n if n is None else n
        at = self.base + n
        self.eng.wait_ge(self.sem, at if self.turn is None else self.turn * self.per_turn + at)


def flat(ap):
    return ap.rearrange("p a n -> p (a n)")


def diff_attention(nc, ctx_outer, T, A):
    with ExitStack() as ctx:
        def sb(name, shape, dt=F32):
            return ctx.enter_context(nc.sbuf_tensor("a_" + name, shape, dt))

        def sem(name):
            return ctx_outer.enter_context(nc.semaphore("a_" + name))

        psum = [ctx.enter_context(nc.psum_tensor(f"a_bank{i}", [P, 512], F32)) for i in range(8)]
        score_ps, turn_ps, value_ps, job_ps = psum[0:4], psum[4:6], psum[6], psum[7]
        x_res, ident = T["x_res"], T["ident"]
        HALF = TOK_TILES // 2
        SCALE = 1.0 / float(np.sqrt(DH))
        PARTS = 3

        wq = sb("wq", [P, DK, FEATS])
        wk = sb("wk", [P, DK, FEATS])
        wv = sb("wv", [P, DK, DIM])
        wo = sb("wo", [P, DK, DIM])
        xnT = sb("xnT", [P, DK, SEQ])
        ctxT = sb("ctxT", [P, DK, SEQ])
        part = sb("part", [P, 2, PARTS, SEQ], BF16)
        rest = sb("rest", [P, SEQ])
        q_packed = sb("q_packed", [6 * DH, HEADS * MAPS, SEQ], BF16)
        k_packed = sb("k_packed", [6 * DH, HEADS * MAPS, SEQ], BF16)
        mask = sb("mask", [P, 2, TOK_TILES, SEQ])
        prob = sb("prob", [P, 2, TOK_TILES, MAPS, SEQ])
        attn = sb("attn", [P, 2, TOK_TILES, SEQ])
        attnT = sb("attnT", [P, TOK_TILES + 2, SEQ])
        value_part = sb("value_part", [P, SEQ])
        v = sb("v", [P, TOK_TILES, DIM + DH])
        o_heads = sb("o_heads", [P, HEADS, TOK_TILES, DH])
        o_norm = sb("o_norm", [P, TOK_TILES, HEADS, DH])
        xn_b = o_norm[:, :, :, :].rearrange("p q h d -> p q (h d)")
        oT = sb("oT", [P, DK, SEQ])
        ctx_b = oT[:, :, :].rearrange("p k n -> p (k n)").rearrange("p (q d) -> p q d", d=DIM)
        neg_max = sb("neg_max", [P, 2, TOK_TILES, MAPS])
        row_sum = sb("row_sum", [P, 2, MAPS, TOK_TILES])
        row_inv = sb("row_inv", [P, HEADS, MAPS, TOK_TILES])
        coef = sb("coef", [P, 2, TOK_TILES])
        o_sum = sb("o_sum", [P, TOK_TILES, DH])
        small = sb("small", [P, 3, HEADS * TOK_TILES])
        norm_now = sb("norm_now", [P, 3 * TOK_TILES])
        stats = sb("stats", [P, ALL_TILES, 6])
        moments = sb("moments", [P, ALL_TILES, 2])
        rstd = sb("rstd", [P, 2, ALL_TILES])
        lam_in = attnT[:, 0:TOK_TILES, 0:HEADS * DH]
        neg_lam = sb("neg_lam", [P, HEADS])
        rms_col = sb("rms_col", [P, 2])
        q_parts_d = nc.dram_tensor("a_q_parts", (BATCH, PARTS, FEATS, SEQ), BF16, kind="Internal").ap()
        k_parts_d = nc.dram_tensor("a_k_parts", (BATCH, PARTS, FEATS, SEQ), BF16, kind="Internal").ap()

        names = ("x_in w_in lam_loaded rms_loaded dve_setup act_setup zero_ready ctx_in mask_in0 mask_in1 "
                 "xn_ready in_turned in_copied qk_mm part1 part2 part3 parts_written0 parts_written1 v_mm v_copied "
                 "scores masked exp combined combined_pool coef_ready rest_ready pool_own turned attnT_ready values value_copied out_turned gathered "
                 "ms_ready rms_ready on_ready on_turned oT_ready wo_mm x_added dve_own").split()
        S = {n: sem(n) for n in names}
        pack_in = [sem(f"pack_in{f}") for f in range(FEAT_TILES)]

        UNITS = HEADS * TOK_TILES
        COEF, COMBINE, TURN, COPY, VALUES, COPY_VALUES, TURN_OUT, GATHER = 5, 6, 11, 11, 16, 16, 18, 18
        OUT_SQUARES, OUT_ROOT, OUT_NORM, NEXT_XN = 14, 15, 16, 28
        PLAN = [(2, "qk", 6), (5, "qk", 7), (12, "v", 0), (14, "v", 1), (21, "turn_o", 0), (24, "turn_o", 1), (27, "out", 0), (30, "out", 1),
                (33, "in", 0), (36, "in", 1), (39, "in", 2), (42, "in", 3), (45, "qk", 0), (48, "qk", 1), (51, "qk", 2), (54, "qk", 3),
                (57, "qk", 4), (60, "qk", 5)]
        COPY_JOB, SPLIT_JOB, THIRD_JOB, WRITE_JOB, TAIL = 0, 1, 2, 3, 32

        def batch_of(kind, i):
            if kind in ("turn_o", "out"):
                return -1
            return 1 if kind == "in" or (kind == "qk" and i < 6) else 0

        def released(kind, i, c):
            return {"qk": (S["rest_ready"], c * 8 + i + 1), "v": (S["v_copied"], c * 2 + i + 1), "turn_o": (S["oT_ready"], c * 2 + i + 1),
                    "out": (S["x_added"], c * 2 + i + 1), "in": (S["in_copied"], c * 4 + i + 1)}[kind]

        def in_plan(kind, i, first, last):
            c = batch_of(kind, i)
            return not (first and c < 0) and not (last and c > 0)

        def planned(u, first, last, delay=0):
            return [(k, i) for at, k, i in PLAN if at + delay == u and in_plan(k, i, first, last)]

        START = [("in", i) for i in range(4)] + [("qk", i) for i in range(6)]

        def head(u):
            return (u // TOK_TILES) % HEADS

        def stage(u, lag, first, tail):
            w = u - lag
            if (first and w < 0) or (tail and w >= UNITS):
                return None
            return head(w), w % TOK_TILES, w

        def over_batches(eng, body):
            for u in range(UNITS):
                body(0, u, True, False, False)
            with eng.Fori(1, BATCH - 1) as b:
                for u in range(UNITS):
                    body(b, u, False, False, False)
            for u in range(UNITS):
                body(BATCH - 1, u, False, True, False)
            for u in range(UNITS, UNITS + TAIL):
                body(BATCH - 1, u, False, True, True)

        scratch = sb("scratch", [P, COPY_VALUES])

        def place(h, k):
            return k + TOK_TILES if k < 2 and h % 2 else k

        def one(b):
            return bass.ds(b, 1)

        with nc.Block() as block:
            @block.sync
            def _(sp):
                def load_ctx(c):
                    sp.dma_start(ctx_b, A["ctx_1024"][one(c)].rearrange("a (q p) d -> p (a q) d", p=P)).then_inc(S["ctx_in"], 16)

                def load_mask(c, h):
                    sp.dma_start(mask[:, h % 2, :, :], A["mask_Bx16xSxS2_ff0"][one(c), h].rearrange("a (q p) n -> p (a q) n", p=P)
                                 ).then_inc(S[f"mask_in{h % 2}"], 16)

                def write_parts(c, i):
                    sp.wait_ge(S["part3"], c * 8 + i + 1)
                    dst = (k_parts_d if i % 2 else q_parts_d)[one(c), :, (i // 2) * P:(i // 2 + 1) * P, :]
                    sp.dma_start(dst.rearrange("a j p n -> p (a j) n"), part[:, i % 2, :, :]).then_inc(S[f"parts_written{i % 2}"], 16)

                def read_packed(c, f):
                    sp.wait_ge(S["parts_written0"], (c * 4 + f + 1) * 16)
                    sp.wait_ge(S["parts_written1"], (c * 4 + f + 1) * 16)
                    row = 0
                    maps = slice(f * MAPS_PER_TILE, (f + 1) * MAPS_PER_TILE)
                    for j in range(PARTS):
                        for r in range(PARTS - j):
                            rows = slice(row, row + DH)
                            for dst, src, n in ((q_packed, q_parts_d, r), (k_packed, k_parts_d, j)):
                                sp.dma_start(dst[rows, maps, :], src[one(c), n, f * P:(f + 1) * P, :].rearrange("a (s d) n -> d (a s) n", d=DH)
                                             ).then_inc(pack_in[f], 16)
                            row += DH

                sp.dma_start(x_res[:, :, :], A["x"].rearrange("b (q p) d -> p (b q) d", p=P)).then_inc(S["x_in"], 16)
                load_ctx(0)
                for w, name in ((wq, "W_q"), (wk, "W_k"), (wv, "W_v"), (wo, "W_o")):
                    sp.dma_start(w[:, :, :], A["L0_xattn_" + name].rearrange("(k p) n -> p k n", p=P)).then_inc(S["w_in"], 16)
                load_mask(0, 0)
                load_mask(0, 1)
                for f in range(3):
                    write_parts(0, 2 * f)
                    write_parts(0, 2 * f + 1)
                    read_packed(0, f)

                def body(b, u, first, last, tail):
                    if tail:
                        return
                    if u % TOK_TILES == TOK_TILES - 1:
                        h = u // TOK_TILES + 2
                        if not (last and h >= HEADS):
                            sp.wait_ge(S["masked"], (b * UNITS + u + 1) * MAPS)
                            load_mask(b + h // HEADS, h % HEADS)
                    if u == NEXT_XN - 1 and not last:
                        if not first:
                            sp.wait_ge(S["wo_mm"], b * 2)
                        load_ctx(b + 1)
                    for kind, i in planned(u, first, last, WRITE_JOB):
                        if kind == "qk":
                            c = b + batch_of(kind, i)
                            write_parts(c, i)
                            if i % 2:
                                read_packed(c, i // 2)

                over_batches(sp, body)

            @block.gpsimd
            def _(pool):
                pool.memset(v[:, :, DIM:], 0.0).then_inc(S["zero_ready"], 1)
                for i, n in enumerate(("q1", "k1", "q2", "k2")):
                    pool.dma_start(lam_in[:, i, :], A["L0_xattn_lambda_" + n].rearrange("h d -> (h d)").rearrange("(a n) -> a n", a=1)
                                   .broadcast_to([P, HEADS * DH])).then_inc(S["lam_loaded"], 16)
                for g in range(P // DH):
                    pool.dma_start(rms_col[g * DH:(g + 1) * DH, 0:1], A["L0_xattn_rms_scale"].rearrange("(d a) -> d a", a=1)).then_inc(S["rms_loaded"], 16)

                def third_part(c, i):
                    pool.wait_ge(S["part2"], c * 8 + i + 1)
                    pool.tensor_tensor(part[:, i % 2, 2, :], rest[:, :], part[:, i % 2, 1, :], ALU.subtract).then_inc(S["part3"], 1)

                for kind, i in START:
                    if kind == "qk":
                        third_part(0, i)

                def combine(b, h, w):
                    pool.wait_ge(S["coef_ready"], b * HEADS + w // TOK_TILES + 1)
                    if not (isinstance(b, int) and b == 0 and w < 2 * TOK_TILES):
                        pool.wait_ge(S["turned"], b * UNITS + w - TOK_TILES)
                    for q in range(HALF, TOK_TILES):
                        pool.tensor_tensor(prob[:, h % 2, q, 1, :], prob[:, h % 2, q, 1, :],
                                           coef[:, h % 2, q:q + 1].broadcast_to([P, SEQ]), ALU.mult).then_inc(S["pool_own"], 1)
                    for q in range(HALF, TOK_TILES):
                        pool.wait_ge(S["pool_own"], (b * HEADS + w // TOK_TILES) * HALF + q - HALF + 1)
                        pool.tensor_tensor(attn[:, h % 2, q, :], prob[:, h % 2, q, 1, :], prob[:, h % 2, q, 0, :], ALU.add).then_inc(S["combined_pool"], 1)

                def body(b, u, first, last, tail):
                    if (s := stage(u, COEF, first, tail)) and s[1] == 0:
                        combine(b, s[0], s[2])
                    for kind, i in [] if tail else planned(u, first, last, THIRD_JOB):
                        if kind == "qk":
                            third_part(b + batch_of(kind, i), i)

                over_batches(pool, body)

            @block.tensor
            def _(pe):
                def product(kind, i, c):
                    if kind == "in":
                        src, k = (ctx_b, i - 2) if i >= 2 else (xn_b, i)
                        if i == 0:
                            pe.wait_ge(S["xn_ready"], c + 1)
                        if i == 2:
                            pe.wait_ge(S["ctx_in"], (c + 1) * 16)
                        for q in range(TOK_TILES):
                            mm = pe.transpose(job_ps[:, q * P:(q + 1) * P], src[:, q, k * P:(k + 1) * P], ident[:, :])
                        mm.then_inc(S["in_turned"], 1)
                    elif kind == "qk":
                        w, src, f = (wk, ctxT, i // 2) if i % 2 else (wq, xnT, i // 2)
                        for k in range(DK):
                            mm = pe.matmul(job_ps[:, :], w[:, k, f * P:(f + 1) * P], src[:, k, :], start=k == 0, stop=k == DK - 1)
                        mm.then_inc(S["qk_mm"], 1)
                    elif kind == "v":
                        for t in range(2):
                            for k in range(DK):
                                mm = pe.matmul(job_ps[:, t * DIM:(t + 1) * DIM], ctxT[:, k, (2 * i + t) * P:(2 * i + t + 1) * P],
                                               wv[:, k, :], start=k == 0, stop=k == DK - 1)
                        mm.then_inc(S["v_mm"], 1)
                    elif kind == "turn_o":
                        pe.wait_ge(S["on_ready"], c + 1)
                        for q in range(TOK_TILES):
                            mm = pe.transpose(job_ps[:, q * P:(q + 1) * P], o_norm[:, q, 8 * i:8 * (i + 1), :].rearrange("p h d -> p (h d)"), ident[:, :])
                        mm.then_inc(S["on_turned"], 1)
                    else:
                        for t in range(2):
                            q = 2 * i + t
                            for k in range(DK):
                                mm = pe.matmul(job_ps[:, t * DIM:(t + 1) * DIM], oT[:, k, q * P:(q + 1) * P], wo[:, k, :], start=k == 0, stop=k == DK - 1)
                        mm.then_inc(S["wo_mm"], 1)

                pe.wait_ge(S["w_in"], 64)
                pe.wait_ge(T["ident_ready"], T["ident_count"])
                for n, (kind, i) in enumerate(START):
                    if n:
                        pe.wait_ge(*released(*START[n - 1], 0))
                    product(kind, i, 0)

                def scores(b, u):
                    h, q = head(u), u % TOK_TILES
                    if h % 4 == 0 and q == 0:
                        pe.wait_ge(pack_in[h // 4], (b + 1) * 192)
                    for m in range(MAPS):
                        n = u * MAPS + m
                        if not (isinstance(b, int) and b == 0 and n < 4):
                            pe.wait_ge(S["masked"], b * UNITS * MAPS + n - 3)
                        hm = h * MAPS + m
                        pe.matmul(score_ps[n % 4][:, :], q_packed[:, hm, q * P:(q + 1) * P], k_packed[:, hm, :], start=True, stop=True).then_inc(S["scores"], 1)

                def turn(b, h, k, w):
                    if k == 0:
                        pe.wait_ge(S["combined"], (b * HEADS + w // TOK_TILES + 1) * HALF)
                        pe.wait_ge(S["combined_pool"], (b * HEADS + w // TOK_TILES + 1) * HALF)
                    if not (isinstance(b, int) and b == 0 and w < 2):
                        pe.wait_ge(S["attnT_ready"], b * UNITS + w - 1)
                    for q in range(TOK_TILES):
                        mm = pe.transpose(turn_ps[w % 2][:, q * P:(q + 1) * P], attn[:, h % 2, q, k * P:(k + 1) * P], ident[:, :])
                    mm.then_inc(S["turned"], 1)

                def values(b, h, w):
                    pe.wait_ge(S["attnT_ready"], b * UNITS + w + TOK_TILES)
                    if h == 0:
                        pe.wait_ge(S["v_copied"], b * 2 + w // UNITS * 2 + 2)
                    if not (isinstance(b, int) and b == 0 and w == 0):
                        pe.wait_ge(S["gathered"], b * HEADS + w // TOK_TILES)
                    for k in range(TOK_TILES):
                        mm = pe.matmul(value_ps[32 * k:32 * (k + 1), :], v[:, k, h * DH:h * DH + 32], attnT[:, place(h, k), :], start=True, stop=True)
                    mm.then_inc(S["values"], 1)

                def turn_out(b, w):
                    pe.wait_ge(S["value_copied"], b * HEADS + w // TOK_TILES + 1)
                    for q in range(TOK_TILES):
                        mm = pe.transpose(value_ps[:, q * P:(q + 1) * P], value_part[:, q * P:(q + 1) * P], ident[:, :])
                    mm.then_inc(S["out_turned"], 1)

                pe.wait_ge(S["zero_ready"], 1)

                def body(b, u, first, last, tail):
                    if not tail:
                        scores(b, u)
                    if (s := stage(u, VALUES, first, tail)) and s[1] == 0:
                        values(b, s[0], s[2])
                    if (s := stage(u, TURN, first, tail)):
                        turn(b, *s)
                    if (s := stage(u, TURN_OUT, first, tail)) and s[1] == 0:
                        turn_out(b, s[2])
                    due = [(k, i) for at, k, i in PLAN if in_plan(k, i, first, last)] if not tail else []
                    for kind, i in planned(u, first, last) if not tail else []:
                        n = due.index((kind, i))
                        if n:
                            before, c = due[n - 1], batch_of(*due[n - 1])
                        else:
                            before, c = ("qk", 5), 0
                        pe.wait_ge(*released(*before, b + c))
                        product(kind, i, b + batch_of(kind, i))
                    if tail:
                        for at, kind, i in PLAN:
                            if kind in ("turn_o", "out") and at + UNITS == u:
                                if (kind, i) == ("turn_o", 0):
                                    pe.wait_ge(*released("v", 1, b))
                                else:
                                    pe.wait_ge(*released(*{("turn_o", 1): ("turn_o", 0), ("out", 0): ("turn_o", 1), ("out", 1): ("out", 0)}[kind, i], b))
                                if (kind, i) == ("out", 0):
                                    pe.wait_ge(S["oT_ready"], b * 2 + 2)
                                product(kind, i, b)

                over_batches(pe, body)

            @block.scalar
            def _(act):
                act.wait_ge(S["dve_setup"], 1)
                act.activation(rstd[:, 0, :], moments[:, :, 1], ACT.Sqrt, bias=T["eps"][:, :]).then_inc(S["act_setup"], 1)
                act.wait_ge(S["dve_setup"], 2)
                act.activation(small[:, 1, 0:2 * HEADS], small[:, 0, 0:2 * HEADS], ACT.Exp).then_inc(S["act_setup"], 1)
                act.wait_ge(S["dve_setup"], 3)

                def copy_product(kind, i, c):
                    if kind == "in":
                        act.wait_ge(S["in_turned"], c * 4 + i + 1)
                        act.copy((ctxT if i >= 2 else xnT)[:, i % 2, :], job_ps[:, :]).then_inc(S["in_copied"], 1)
                    elif kind == "qk":
                        act.wait_ge(S["qk_mm"], c * 8 + i + 1)
                        if not (isinstance(c, int) and c == 0 and i < 2):
                            act.wait_ge(S[f"parts_written{i % 2}"], (c * 4 + i // 2) * 16)
                        act.activation(part[:, i % 2, 0, :], job_ps[:, :], ACT.Copy, scale=1.0 if i % 2 else SCALE).then_inc(S["part1"], 1)
                    elif kind == "v":
                        act.wait_ge(S["v_mm"], c * 2 + i + 1)
                        act.copy(v[:, 2 * i:2 * i + 2, 0:DIM], job_ps[:, :].rearrange("p (t n) -> p t n", n=DIM)).then_inc(S["v_copied"], 1)
                    elif kind == "turn_o":
                        act.wait_ge(S["on_turned"], c * 2 + i + 1)
                        act.activation(oT[:, i, :], job_ps[:, :], ACT.Copy, scale=rms_col[:, 1:2]).then_inc(S["oT_ready"], 1)

                for kind, i in START:
                    copy_product(kind, i, 0)

                def exps(b, u):
                    h, q = head(u), u % TOK_TILES
                    for m in range(MAPS):
                        act.wait_ge(S["masked"], (b * UNITS + u) * MAPS + m + 1)
                        tile = prob[:, h % 2, q, m, :]
                        act.activation(tile, tile, ACT.Exp, bias=neg_max[:, h % 2, q, m:m + 1], scale=-1.0,
                                       accum_out=row_sum[:, h % 2, m, q:q + 1]).then_inc(S["exp"], 1)

                def copy_turned(b, h, k, w):
                    if k == 2 and not (isinstance(b, int) and b == 0 and w < TOK_TILES):
                        act.wait_ge(S["values"], b * HEADS + w // TOK_TILES)
                    act.wait_ge(S["turned"], b * UNITS + w + 1)
                    act.copy(attnT[:, place(h, k), :], turn_ps[w % 2][:, :]).then_inc(S["attnT_ready"], 1)

                def body(b, u, first, last, tail):
                    if (s := stage(u, COPY, first, tail)):
                        copy_turned(b, *s)
                    for kind, i in [] if tail else planned(u, first, last, COPY_JOB):
                        copy_product(kind, i, b + batch_of(kind, i))
                    if not tail:
                        exps(b, u)
                    if u % UNITS == OUT_ROOT and not first and (tail or not u >= UNITS):
                        c = b if tail else b - 1
                        act.wait_ge(S["ms_ready"], c + 1)
                        act.activation(small[:, 2, :], small[:, 1, :], ACT.Sqrt, bias=T["eps"][:, :], scale=1.0 / DH).then_inc(S["rms_ready"], 1)
                    if tail:
                        for at, kind, i in PLAN:
                            if kind == "turn_o" and at + COPY_JOB + UNITS == u:
                                copy_product(kind, i, b)

                over_batches(act, body)

            @block.vector
            def _(dve):
                own = Steps(dve, S["dve_own"])
                dve.wait_ge(S["x_in"], 16)
                for t in range(ALL_TILES):
                    s = dve.bn_stats(stats[:, t, :], x_res[:, t, :])
                own.done(s)
                own.wait()
                for t in range(ALL_TILES):
                    s = dve.bn_aggr(moments[:, t, :], stats[:, t, :])
                s.then_inc(S["dve_setup"], 1)
                dve.wait_ge(S["lam_loaded"], 64)
                for i in range(2):
                    own.done(dve.tensor_tensor(lam_in[:, 2 * i, :], lam_in[:, 2 * i, :], lam_in[:, 2 * i + 1, :], ALU.mult))
                own.wait()
                for i in range(2):
                    s = dve.tensor_reduce(small[:, 0, i * HEADS:(i + 1) * HEADS], lam_in[:, 2 * i, :].rearrange("p (h d) -> p h d", d=DH), AX.X, ALU.add)
                s.then_inc(S["dve_setup"], 1)
                dve.wait_ge(S["act_setup"], 1)
                own.done(dve.reciprocal(rstd[:, 1, :], rstd[:, 0, :]))
                own.wait()

                xv = x_res[:, :, :].rearrange("p (b q) d -> p b (q d)", b=BATCH)

                def normalise_x(c):
                    mom = moments[:, :, :].rearrange("p (b q) c -> p b (q c)", b=BATCH)
                    rs = rstd[:, 1, :].rearrange("p (b q) -> p b q", b=BATCH)
                    own.done(dve.tensor_copy(norm_now[:, 0:8], flat(mom[:, one(c), :])))
                    own.done(dve.tensor_copy(norm_now[:, 8:12], flat(rs[:, one(c), :])))
                    own.wait()
                    for q in range(TOK_TILES):
                        s = dve.tensor_scalar(xn_b[:, q, :], flat(xv[:, one(c), q * DIM:(q + 1) * DIM]),
                                              norm_now[:, 2 * q:2 * q + 1], norm_now[:, 8 + q:9 + q], ALU.subtract, ALU.mult)
                    s.then_inc(S["xn_ready"], 1)

                def split(i, c):
                    dve.wait_ge(S["part1"], c * 8 + i + 1)
                    if not (isinstance(c, int) and c == 0 and i < 1):
                        dve.wait_ge(S["part3"], c * 8 + i)
                    dve.scalar_tensor_tensor(out=rest[:, :], in0=job_ps[:, :], scalar=1.0 if i % 2 else SCALE,
                                             in1=part[:, i % 2, 0, :], op0=ALU.mult, op1=ALU.subtract).then_inc(S["rest_ready"], 1)
                    dve.wait_ge(S["rest_ready"], c * 8 + i + 1)
                    dve.tensor_copy(part[:, i % 2, 1, :], rest[:, :]).then_inc(S["part2"], 1)

                normalise_x(0)
                dve.wait_ge(S["act_setup"], 2)
                dve.scalar_tensor_tensor(out=neg_lam[:, :], in0=small[:, 1, HEADS:2 * HEADS], scalar=-LAMBDA_INIT, in1=small[:, 1, 0:HEADS],
                                         op0=ALU.add, op1=ALU.subtract)
                dve.wait_ge(S["rms_loaded"], 128)
                dve.tensor_scalar(rms_col[:, 1:2], rms_col[:, 0:1], 1.0 - LAMBDA_INIT, None, ALU.mult).then_inc(S["dve_setup"], 1)
                for kind, i in START:
                    if kind == "qk":
                        split(i, 0)

                def ready(b, u):
                    h = head(u)
                    if u % TOK_TILES == 0:
                        dve.wait_ge(S[f"mask_in{h % 2}"], (b * (HEADS // 2) + h // 2 + 1) * 16)
                    if not (isinstance(b, int) and b == 0 and u < 2 * TOK_TILES):
                        done = S["combined_pool" if u % TOK_TILES >= HALF else "combined"]
                        dve.wait_ge(done, (b * HEADS + u // TOK_TILES - 2) * HALF + u % HALF + 1)
                    dve.wait_ge(S["scores"], (b * UNITS + u + 1) * MAPS)

                def add_mask(u, m):
                    h, q = head(u), u % TOK_TILES
                    dve.tensor_tensor_reduce(prob[:, h % 2, q, m, :], score_ps[(u * MAPS + m) % 4][:, :], mask[:, h % 2, q, :], -1.0, 3.0e38,
                                             ALU.add, ALU.min, neg_max[:, h % 2, q, m:m + 1]).then_inc(S["masked"], 1)

                def invert_sums(h):
                    own.done(dve.reciprocal(row_inv[:, h, :, :], row_sum[:, h % 2, :, :]))

                def coefficients(h):
                    own.wait()
                    dve.scalar_tensor_tensor(out=coef[:, h % 2, :], in0=row_sum[:, h % 2, 0, :], scalar=neg_lam[:, h:h + 1],
                                             in1=row_inv[:, h, 1, :], op0=ALU.mult, op1=ALU.mult).then_inc(S["coef_ready"], 1)

                def combine(b, h, q, w):
                    if q == 0:
                        dve.wait_ge(S["coef_ready"], b * HEADS + w // TOK_TILES + 1)
                    if q == 0 and not (isinstance(b, int) and b == 0 and w < 2 * TOK_TILES):
                        dve.wait_ge(S["turned"], b * UNITS + w - TOK_TILES)
                    dve.scalar_tensor_tensor(out=attn[:, h % 2, q, :], in0=prob[:, h % 2, q, 1, :], scalar=coef[:, h % 2, q:q + 1],
                                             in1=prob[:, h % 2, q, 0, :], op0=ALU.mult, op1=ALU.add).then_inc(S["combined"], 1)

                def copy_values(b, w):
                    dve.wait_ge(S["values"], b * HEADS + w // TOK_TILES + 1)
                    dve.tensor_copy(value_part[:, :], value_ps[:, :]).then_inc(S["value_copied"], 1)

                def gather(b, w):
                    own.wait()
                    dve.wait_ge(S["out_turned"], b * HEADS + w // TOK_TILES + 1)
                    dve.tensor_reduce(o_sum[:, :, :], value_ps[:, :].rearrange("p (q g d) -> p q d g", q=TOK_TILES, g=4)[:, :, 0:DH, :],
                                      AX.X, ALU.add).then_inc(S["gathered"], 1)

                def scale_gathered(b, h, w):
                    dve.wait_ge(S["gathered"], b * HEADS + w // TOK_TILES + 1)
                    own.done(dve.tensor_tensor(o_heads[:, h, :, :], o_sum[:, :, :],
                                               row_inv[:, h, 0, :].rearrange("p (q a) -> p q a", a=1).broadcast_to([P, TOK_TILES, DH]), ALU.mult))

                oh = o_heads[:, :, :, :].rearrange("p h q d -> p (h q) d")

                def squares():
                    own.wait()
                    own.done(dve.tensor_tensor(o_norm[:, :, :, :].rearrange("p q h d -> p (q h) d"), oh, oh, ALU.mult))
                    own.wait()
                    dve.tensor_reduce(small[:, 1, :], o_norm[:, :, :, :].rearrange("p q h d -> p (q h) d"), AX.X, ALU.add).then_inc(S["ms_ready"], 1)

                def rms_norm(c):
                    dve.wait_ge(S["rms_ready"], c + 1)
                    own.done(dve.reciprocal(small[:, 0, :], small[:, 2, :]))
                    own.wait()
                    dve.tensor_tensor(o_norm[:, :, :, :].rearrange("p q h d -> p h q d"), o_heads[:, :, :, :],
                                      small[:, 0, :].rearrange("p (h q a) -> p h q a", q=TOK_TILES, a=1).broadcast_to([P, HEADS, TOK_TILES, DH]),
                                      ALU.mult).then_inc(S["on_ready"], 1)

                def add_out(i, c):
                    dve.wait_ge(S["wo_mm"], c * 2 + i + 1)
                    xq = flat(xv[:, one(c), i * 2 * DIM:(i + 1) * 2 * DIM])
                    dve.tensor_tensor(xq, job_ps[:, :], xq, ALU.add).then_inc(S["x_added"], 1)

                per_turn = None

                def body(b, u, first, last, tail):
                    mixed, sums, copied, out = (stage(u, lag, first, tail) for lag in (COMBINE, COEF, COPY_VALUES, GATHER))
                    mixed = mixed if mixed and mixed[1] < HALF else None
                    copied = copied if copied and copied[1] == 0 else None
                    sums = sums if sums and sums[1] == 0 else None
                    out = out if out and out[1] == 0 else None
                    if sums:
                        dve.wait_ge(S["exp"], (b * UNITS + sums[2] + TOK_TILES) * MAPS)
                    if not tail:
                        ready(b, u)
                    if mixed:
                        combine(b, *mixed)
                    elif copied:
                        copy_values(b, copied[2])
                    elif sums:
                        invert_sums(sums[0])
                    elif not tail:
                        dve.memset(scratch[:, u:u + 1], 0.0)
                    if not tail:
                        add_mask(u, 0)
                    if sums:
                        coefficients(sums[0])
                    if out:
                        gather(b, out[2])
                    if not tail:
                        add_mask(u, 1)
                    if out:
                        scale_gathered(b, out[0], out[2])
                    if not first and (tail or u < UNITS):
                        c = b if tail else b - 1
                        at = u - UNITS if tail else u
                        if at == OUT_SQUARES:
                            squares()
                        if at == OUT_NORM:
                            rms_norm(c)
                        for when, kind, i in PLAN:
                            if kind == "out" and at == when + 1:
                                add_out(i, c)
                    if not tail:
                        if u == NEXT_XN and not last:
                            if not first:
                                dve.wait_ge(S["on_turned"], b * 2)
                            normalise_x(b + 1)
                        for kind, i in planned(u, first, last, SPLIT_JOB):
                            if kind == "qk":
                                split(i, b + batch_of(kind, i))

                for u in range(UNITS):
                    body(0, u, True, False, False)
                with dve.Fori(1, BATCH - 1) as b:
                    own.loop(b, DVE_A, 1)
                    for u in range(UNITS):
                        body(b, u, False, False, False)
                own.end_loop(BATCH - 2)
                for u in range(UNITS):
                    body(BATCH - 1, u, False, True, False)
                for u in range(UNITS, UNITS + TAIL):
                    body(BATCH - 1, u, False, True, True)
                dve.wait_ge(S["x_added"], BATCH * 2)


DVE_A = HEADS + HEADS + 1 + 1 + 2



EXPERTS = 8
FF = 1024
FF_TILES = FF // P
SLOT_TILES = 24
FETCHED_TILES = SLOT_TILES + 2


def layernorm_all(dve, own, sem_stats, sem_std, std_at, x_res, stats, moments, rstd, out):
    for t in range(ALL_TILES):
        s = dve.bn_stats(stats[:, t, :], x_res[:, t, :])
    own.done(s)
    own.wait()
    for t in range(ALL_TILES):
        s = dve.bn_aggr(moments[:, t, :], stats[:, t, :])
    s.then_inc(sem_stats, 1)
    dve.wait_ge(sem_std, std_at)
    own.done(dve.reciprocal(rstd[:, 1, :], rstd[:, 0, :]))
    own.wait()
    for t in range(ALL_TILES):
        s = dve.tensor_scalar(out[:, t, :], x_res[:, t, :], moments[:, t, 0:1], rstd[:, 1, t:t + 1], ALU.subtract, ALU.mult)
    return s


def experts(nc, ctx_outer, T, A):
    with ExitStack() as ctx:
        def sb(name, shape, dt=F32):
            return ctx.enter_context(nc.sbuf_tensor("b_" + name, shape, dt))

        def sem(name):
            return ctx_outer.enter_context(nc.semaphore("b_" + name))

        psum = [ctx.enter_context(nc.psum_tensor(f"b_bank{i}", [P, 512], F32)) for i in range(8)]
        x_res, ident = T["x_res"], T["ident"]
        stats = sb("stats", [P, ALL_TILES, 6])
        moments = sb("moments", [P, ALL_TILES, 2])
        rstd = sb("rstd", [P, 2, ALL_TILES])
        xn = sb("xn", [P, ALL_TILES, DIM])
        router = sb("router", [P, DK, EXPERTS])
        router_b = sb("router_b", [P, EXPERTS])
        logits = sb("logits", [P, ALL_TILES, EXPERTS])
        expd = sb("expd", [P, ALL_TILES, EXPERTS])
        pick = sb("pick", [P, ALL_TILES, EXPERTS])
        onehot = sb("onehot", [P, ALL_TILES, EXPERTS])
        onehot_b = sb("onehot_b", [P, ALL_TILES, EXPERTS], BF16)
        col = sb("col", [P, 6, ALL_TILES])
        gate = sb("gate", [P, ALL_TILES])
        first_w = sb("first_w", [P, EXPERTS])
        before = sb("before", [P, P], BF16)
        ones_b = sb("ones_b", [P, P], BF16)
        totals = sb("totals", [P, ALL_TILES, EXPERTS])
        cum = sb("cum", [P, 2, ALL_TILES, EXPERTS])
        where = sb("where", [P, ALL_TILES, EXPERTS])
        count_i = sb("count_i", [P, 2, EXPERTS], I32)
        need = sb("need", [P, 4, EXPERTS])
        slot_f = sb("slot_f", [P, ALL_TILES])
        slot = sb("slot", [P, ALL_TILES], I32)
        tile_no = sb("tile_no", [P, FETCHED_TILES])
        past = sb("past", [P, FETCHED_TILES, EXPERTS])
        owner_f = sb("owner_f", [P, FETCHED_TILES])
        owner = sb("owner", [P, FETCHED_TILES], I32)
        b1_rows = sb("b1_rows", [EXPERTS * FF_TILES, P])
        b1T = sb("b1T", [P, EXPERTS * FF_TILES])
        b2_all = sb("b2_all", [P, EXPERTS, DIM])
        w1_all = sb("w1_all", [P, EXPERTS * DK, FF])
        w2_all = sb("w2_all", [P, EXPERTS * FF_TILES, DIM])
        w1 = sb("w1", [P, 2, DK * FF])
        xnT = w1[:, :, :].rearrange("p r n -> p (r n)").rearrange("p (b k n) -> p b k n", b=BATCH, k=DK)
        x_slots = sb("x_slots", [P, 2, DIM])
        x_slotsT = sb("x_slotsT", [P, 2, DK, P])
        hiddenT = sb("hiddenT", [P, 2, FF_TILES, P])
        b1_t = sb("b1_t", [P, 2, FF_TILES])
        y_slots = sb("y_slots", [P, 2, DIM])
        y_tok = hiddenT[:, 0, :, :].rearrange("p (t a) n -> p t (a n)", t=4)
        x_slots_d = nc.dram_tensor("b_x_sorted", (FETCHED_TILES * P, DIM), F32, kind="Internal").ap()
        y_slots_d = nc.dram_tensor("b_y_sorted", (SLOT_TILES * P, DIM), F32, kind="Internal").ap()

        names = ("w_in b1_in b1_turned b1_ready zeroed experts_in stats_ready std_ready xn_ready turned turn_act turn_dve "
                 "logit_mm shifted exp_done onehot_ready masks_ready ranks totals_mm slot_ready owner_ready scattered "
                 "w1_ready0 w1_ready1 xs_in0 xs_in1 xs_turned xsT_ready b1_picked h_mm0 h_mm1 "
                 "relu_act relu_dve y_mm y_ready y_out0 y_out1 combined dve_own pool_own iota_done").split()
        S = {n: sem(n) for n in names}
        gathered = [sem(f"gathered{i}") for i in range(4)]
        EB, NTILE = EXPERTS, ALL_TILES

        with nc.Block() as block:
            @block.sync
            def _(sp):
                sp.dma_start(router[:, :, :], A["L0_ffn_router_W"].rearrange("(k p) e -> p k e", p=P)).then_inc(S["w_in"], 16)
                sp.dma_start(router_b[:, :], A["L0_ffn_router_b"].rearrange("(a e) -> a e", a=1).broadcast_to([P, EXPERTS])).then_inc(S["w_in"], 16)
                sp.dma_start(b1_rows[:, :], A["L0_ffn_b1"].rearrange("e (f p) -> (e f) p", p=P)).then_inc(S["b1_in"], 16)
                sp.dma_start(b2_all[:, :, :], A["L0_ffn_b2"].rearrange("(a e) d -> a e d", a=1).broadcast_to([P, EXPERTS, DIM])).then_inc(S["b1_in"], 16)
                sp.wait_ge(S["zeroed"], 1)
                half = FETCHED_TILES // 2
                for r in range(2):
                    sp.dma_start(x_slots_d.rearrange("(i t p) d -> i p t d", i=2, p=P)[r],
                                 y_slots[:, r, :].rearrange("p (a d) -> p a d", a=1).broadcast_to([P, half, DIM])).then_inc(S[f"y_out{r}"], 16)
                for e in range(EXPERTS):
                    sp.dma_start(w1_all[:, e * DK:(e + 1) * DK, :], A["L0_ffn_W1"][e].rearrange("(k p) f -> p k f", p=P)).then_inc(S["experts_in"], 16)
                    sp.dma_start(w2_all[:, e * FF_TILES:(e + 1) * FF_TILES, :], A["L0_ffn_W2"][e].rearrange("(k p) d -> p k d", p=P)).then_inc(S["experts_in"], 16)
                sorted_x = x_slots_d.rearrange("(i r p) d -> i r p d", r=2, p=P)
                sp.wait_ge(S["scattered"], 16 * ALL_TILES)
                for r in range(2):
                    sp.dma_start(x_slots[:, r, :], sorted_x[0, r]).then_inc(S[f"xs_in{r}"], 16)
                with sp.Fori(0, SLOT_TILES // 2) as i:
                    for r in range(2):
                        sp.wait_ge(S["xs_turned"], 2 * i + r + 1)
                        sp.dma_start(x_slots[:, r, :], sorted_x[bass.ds(i + 1, 1), r].rearrange("a p d -> p (a d)")).then_inc(S[f"xs_in{r}"], 16)

            @block.gpsimd
            def _(pool):
                own = Steps(pool, S["pool_own"])
                pool.memset(y_slots[:, :, :], 0.0).then_inc(S["zeroed"], 1)
                pool.memset(ones_b[:, :], 1.0)
                own.done(pool.memset(before[:, :], 1.0))
                own.wait()
                pool.affine_select(out=before[:, :], in_=before[:, :], compare_op=ALU.is_gt, fill=0.0, base=0,
                                   pattern=[[1, P]], channel_multiplier=-1).then_inc(S["masks_ready"], 1)
                pool.iota(first_w[:, :], pattern=[[-1, EXPERTS]], base=EXPERTS, channel_multiplier=0,
                          allow_small_or_imprecise_dtypes=True).then_inc(S["iota_done"], 1)
                pool.iota(tile_no[:, :], pattern=[[1, FETCHED_TILES]], base=0, channel_multiplier=0,
                          allow_small_or_imprecise_dtypes=True).then_inc(S["iota_done"], 1)
                pool.wait_ge(S["slot_ready"], 1)
                pool.wait_ge(S["xn_ready"], 1)
                pool.wait_ge(S["y_out0"], 16)
                pool.wait_ge(S["y_out1"], 16)
                for t in range(ALL_TILES):
                    pool.indirect_dma_start(x_slots_d, bass.IndirectOffsetOnAxis(slot[:, t:t + 1], 0), xn[:, t, :], None).then_inc(S["scattered"], 16)
                pool.wait_ge(S["y_out0"], 16 * (SLOT_TILES // 2 + 1))
                pool.wait_ge(S["y_out1"], 16 * (SLOT_TILES // 2 + 1))
                for t in range(ALL_TILES):
                    if t >= 4:
                        pool.wait_ge(S["combined"], t - 3)
                    pool.indirect_dma_start(y_tok[:, t % 4, :], None, y_slots_d, bass.IndirectOffsetOnAxis(slot[:, t:t + 1], 0)).then_inc(gathered[t % 4], 16)

            @block.tensor
            def _(pe):
                pe.wait_ge(S["b1_in"], 32)
                pe.transpose(psum[7][:, 0:EXPERTS * FF_TILES], b1_rows[:, :], ident[0:EXPERTS * FF_TILES, 0:EXPERTS * FF_TILES]).then_inc(S["b1_turned"], 1)
                pe.wait_ge(S["w_in"], 32)
                pe.wait_ge(S["xn_ready"], 1)
                for b in range(BATCH):
                    for k in range(DK):
                        n = b * DK + k
                        if n >= 4:
                            pe.wait_ge((S["turn_dve"] if k else S["turn_act"]), b - 1)
                        for q in range(TOK_TILES):
                            mm = pe.transpose(psum[n % 4][:, q * P:(q + 1) * P], xn[:, b * TOK_TILES + q, k * P:(k + 1) * P], ident[:, :])
                        mm.then_inc(S["turned"], 1)
                for b in range(BATCH):
                    pe.wait_ge(S["turn_act"], b + 1)
                    pe.wait_ge(S["turn_dve"], b + 1)
                    for q in range(TOK_TILES):
                        for k in range(DK):
                            t = b * TOK_TILES + q
                            mm = pe.matmul(psum[4][:, t * EB:(t + 1) * EB], xnT[:, b, k, q * P:(q + 1) * P], router[:, k, :], start=k == 0, stop=k == DK - 1)
                mm.then_inc(S["logit_mm"], 1)
                pe.wait_ge(S["masks_ready"], 1)
                pe.wait_ge(S["onehot_ready"], 1)
                pe.matmul(psum[5][:, 0:NTILE * EB], ones_b[:, :], onehot_b[:, :, :].rearrange("p t e -> p (t e)"), start=True, stop=True).then_inc(S["totals_mm"], 1)
                pe.matmul(psum[6][:, 0:NTILE * EB], before[:, :], onehot_b[:, :, :].rearrange("p t e -> p (t e)"), start=True, stop=True).then_inc(S["ranks"], 1)

                def turn(r, at):
                    pe.wait_ge(S[f"xs_in{r}"], at)
                    for k in range(DK):
                        mm = pe.transpose(psum[r][:, k * P:(k + 1) * P], x_slots[:, r, k * P:(k + 1) * P], ident[:, :])
                    mm.then_inc(S["xs_turned"], 1)

                turn(0, 16)
                turn(1, 16)
                with pe.Fori(0, SLOT_TILES // 2) as i:
                    def hidden(r):
                        pe.wait_ge(S["xsT_ready"], 2 * i + r + 1)
                        pe.wait_ge(S[f"w1_ready{r}"], i + 1)
                        for f in range(FF_TILES):
                            for k in range(DK):
                                mm = pe.matmul(psum[2 + 2 * r + f // 4][:, (f % 4) * P:(f % 4 + 1) * P], w1[:, r, k * FF + f * P:k * FF + (f + 1) * P],
                                               x_slotsT[:, r, k, :], start=k == 0, stop=k == DK - 1)
                        mm.then_inc(S[f"h_mm{r}"], 1)

                    def down(r):
                        pe.wait_ge(S["relu_act"], 2 * i + r + 1)
                        pe.wait_ge(S["relu_dve"], 2 * i + r + 1)
                        for f in range(FF_TILES):
                            mm = pe.matmul(psum[6 + r][:, 0:DIM], hiddenT[:, r, f, :], flat(w2_all[:, bass.ds(experts_now[r] * FF_TILES + f, 1), :]),
                                           start=f == 0, stop=f == FF_TILES - 1)
                        mm.then_inc(S["y_mm"], 1)

                    experts_now = [pe.value_load(owner[0:1, bass.ds(2 * i + r, 1)], min_val=0, max_val=EXPERTS - 1) for r in range(2)]
                    hidden(0)
                    hidden(1)
                    turn(0, (i + 2) * 16)
                    turn(1, (i + 2) * 16)
                    down(0)
                    down(1)

            @block.scalar
            def _(act):
                act.wait_ge(S["b1_turned"], 1)
                act.copy(b1T[:, :], psum[7][:, 0:EXPERTS * FF_TILES]).then_inc(S["b1_ready"], 1)
                act.wait_ge(S["stats_ready"], 1)
                act.activation(rstd[:, 0, :], moments[:, :, 1], ACT.Sqrt, bias=T["eps"][:, :]).then_inc(S["std_ready"], 1)
                for b in range(BATCH):
                    act.wait_ge(S["turned"], b * DK + 1)
                    act.copy(xnT[:, b, 0, :], psum[(b * DK) % 4][:, :]).then_inc(S["turn_act"], 1)
                act.wait_ge(S["shifted"], 1)
                act.activation(expd[:, :, :], logits[:, :, :], ACT.Exp).then_inc(S["exp_done"], 1)

                def turned(r, at):
                    act.wait_ge(S["xs_turned"], at)
                    act.copy(x_slotsT[:, r, :, :].rearrange("p k n -> p (k n)"), psum[r][:, 0:2 * P]).then_inc(S["xsT_ready"], 1)

                turned(0, 1)
                turned(1, 2)
                with act.Fori(0, SLOT_TILES // 2) as i:
                    def relu(r):
                        act.wait_ge(S["b1_picked"], 2 * i + r + 1)
                        act.wait_ge(S[f"h_mm{r}"], i + 1)
                        for f in range(4):
                            s = act.activation(hiddenT[:, r, f, :], psum[2 + 2 * r][:, f * P:(f + 1) * P], ACT.Relu, bias=b1_t[:, r, f:f + 1])
                        s.then_inc(S["relu_act"], 1)

                    relu(0)
                    relu(1)
                    turned(0, 2 * i + 3)
                    turned(1, 2 * i + 4)
                    for r in range(2):
                        act.wait_ge(S["y_ready"], 2 * i + r + 1)
                        act.dma_start(y_slots_d.rearrange("(i r p) d -> i r p d", r=2, p=P)[bass.ds(i, 1), r].rearrange("a p d -> p (a d)"),
                                      y_slots[:, r, :]).then_inc(S[f"y_out{r}"], 16)

            @block.vector
            def _(dve):
                own = Steps(dve, S["dve_own"])

                def do(instruction):
                    own.done(instruction)
                    own.wait()

                s = layernorm_all(dve, own, S["stats_ready"], S["std_ready"], 1, x_res, stats, moments, rstd, xn)
                s.then_inc(S["xn_ready"], 1)
                for b in range(BATCH):
                    dve.wait_ge(S["turned"], b * DK + 2)
                    dve.tensor_copy(xnT[:, b, 1, :], psum[(b * DK + 1) % 4][:, :]).then_inc(S["turn_dve"], 1)
                wide = lambda ap: ap.rearrange("p (t a) -> p t a", a=1).broadcast_to([P, NTILE, EB])
                every = lambda ap: ap.rearrange("p (a e) -> p a e", a=1).broadcast_to([P, NTILE, EB])
                dve.wait_ge(S["logit_mm"], 1)
                do(dve.tensor_tensor(logits[:, :, :], psum[4][:, 0:NTILE * EB].rearrange("p (t e) -> p t e", e=EB), every(router_b[:, :]), ALU.add))
                do(dve.tensor_reduce(col[:, 0, :], logits[:, :, :], AX.X, ALU.max))
                dve.tensor_tensor(logits[:, :, :], logits[:, :, :], wide(col[:, 0, :]), ALU.subtract).then_inc(S["shifted"], 1)
                dve.wait_ge(S["exp_done"], 1)
                dve.wait_ge(S["iota_done"], 2)
                dve.tensor_reduce(col[:, 1, :], expd[:, :, :], AX.X, ALU.add)
                do(dve.tensor_reduce(col[:, 2, :], expd[:, :, :], AX.X, ALU.max))
                dve.reciprocal(col[:, 3, :], col[:, 1, :])
                do(dve.tensor_tensor(pick[:, :, :], expd[:, :, :], wide(col[:, 2, :]), ALU.is_ge))
                dve.tensor_tensor(gate[:, :], col[:, 2, :], col[:, 3, :], ALU.mult)
                do(dve.tensor_tensor(pick[:, :, :], pick[:, :, :], every(first_w[:, :]), ALU.mult))
                do(dve.tensor_reduce(col[:, 4, :], pick[:, :, :], AX.X, ALU.max))
                do(dve.tensor_tensor(onehot[:, :, :], pick[:, :, :], wide(col[:, 4, :]), ALU.is_equal))
                dve.tensor_copy(onehot_b[:, :, :], onehot[:, :, :]).then_inc(S["onehot_ready"], 1)
                dve.wait_ge(S["totals_mm"], 1)
                flat_ps = psum[5][:, 0:NTILE * EB].rearrange("p (t e) -> p t e", e=EB)
                dve.tensor_copy(totals[:, :, :], flat_ps)
                do(dve.tensor_copy(cum[:, 0, :, :], flat_ps))
                at, step = 0, 1
                while step < NTILE:
                    dve.tensor_copy(cum[:, 1 - at, 0:step, :], cum[:, at, 0:step, :])
                    do(dve.tensor_tensor(cum[:, 1 - at, step:, :], cum[:, at, step:, :], cum[:, at, 0:NTILE - step, :], ALU.add))
                    at, step = 1 - at, 2 * step
                do(dve.tensor_scalar(count_i[:, 0, :], cum[:, at, NTILE - 1, :], float(P - 1), None, ALU.add))
                do(dve.tensor_scalar(count_i[:, 1, :], count_i[:, 0, :], P.bit_length() - 1, None, ALU.arith_shift_right))
                dve.tensor_copy(need[:, 0, :], count_i[:, 1, :])
                do(dve.tensor_copy(need[:, 1, :], count_i[:, 1, :]))
                here, step = 1, 1
                while step < EB:
                    dve.tensor_copy(need[:, 3 - here, 0:step], need[:, here, 0:step])
                    do(dve.tensor_tensor(need[:, 3 - here, step:], need[:, here, step:], need[:, here, 0:EB - step], ALU.add))
                    here, step = 3 - here, 2 * step
                ends = need[:, here, :].rearrange("p (a e) -> p a e", a=1).broadcast_to([P, FETCHED_TILES, EB])
                do(dve.tensor_tensor(past[:, :, :], tile_no[:, :].rearrange("p (t a) -> p t a", a=1).broadcast_to([P, FETCHED_TILES, EB]), ends, ALU.is_ge))
                do(dve.tensor_reduce(owner_f[:, :], past[:, :, :], AX.X, ALU.add))
                dve.tensor_scalar(owner[:, :], owner_f[:, :], float(EB - 1), None, ALU.min).then_inc(S["owner_ready"], 1)
                do(dve.tensor_tensor(need[:, 3, :], need[:, here, :], need[:, 0, :], ALU.subtract))
                do(dve.tensor_scalar(need[:, 3, :], need[:, 3, :], float(P), None, ALU.mult))
                do(dve.tensor_tensor(where[:, :, :], cum[:, at, :, :], totals[:, :, :], ALU.subtract))
                dve.wait_ge(S["ranks"], 1)
                do(dve.tensor_tensor(where[:, :, :], where[:, :, :], psum[6][:, 0:NTILE * EB].rearrange("p (t e) -> p t e", e=EB), ALU.add))
                do(dve.tensor_tensor(where[:, :, :], where[:, :, :], every(need[:, 3, :]), ALU.add))
                do(dve.tensor_tensor(where[:, :, :], where[:, :, :], onehot[:, :, :], ALU.mult))
                do(dve.tensor_reduce(slot_f[:, :], where[:, :, :], AX.X, ALU.add))
                dve.tensor_copy(slot[:, :], slot_f[:, :]).then_inc(S["slot_ready"], 1)
                dve.wait_ge(S["b1_ready"], 1)
                dve.wait_ge(S["owner_ready"], 1)
                dve.wait_ge(S["experts_in"], 32 * EXPERTS)

                def load_owner(tile):
                    return dve.value_load(owner[0:1, tile], min_val=0, max_val=EXPERTS - 1)

                def place_w1(r, e):
                    dve.tensor_copy(w1[:, r, :], w1_all[:, bass.ds(e * DK, DK), :].rearrange("p k n -> p (k n)")).then_inc(S[f"w1_ready{r}"], 1)

                def pick_b1(r, e):
                    dve.tensor_copy(b1_t[:, r, :], b1T[:, bass.ds(e * FF_TILES, FF_TILES)]).then_inc(S["b1_picked"], 1)

                for r in range(2):
                    e = load_owner(slice(r, r + 1))
                    place_w1(r, e)
                    pick_b1(r, e)
                with dve.Fori(0, SLOT_TILES // 2) as i:
                    now = [load_owner(bass.ds(2 * i + r, 1)) for r in range(2)]
                    for r in range(2):
                        dve.wait_ge(S["b1_picked"], 2 * i + r + 1)
                        dve.wait_ge(S[f"h_mm{r}"], i + 1)
                        for f in range(4, 8):
                            s = dve.tensor_scalar(hiddenT[:, r, f, :], psum[3 + 2 * r][:, (f - 4) * P:(f - 3) * P], b1_t[:, r, f:f + 1], 0.0, ALU.add, ALU.max)
                        s.then_inc(S["relu_dve"], 1)
                        following = load_owner(bass.ds(2 * i + 2 + r, 1))
                        place_w1(r, following)
                        dve.wait_ge(S["relu_act"], 2 * i + r + 1)
                        dve.wait_ge(S["relu_dve"], 2 * i + r + 1)
                        pick_b1(r, following)
                    for r in range(2):
                        dve.wait_ge(S[f"y_out{r}"], (i + 1) * 16)
                        dve.wait_ge(S["y_mm"], 2 * i + r + 1)
                        dve.tensor_tensor(y_slots[:, r, :], psum[6 + r][:, 0:DIM], flat(b2_all[:, bass.ds(now[r], 1), :]), ALU.add).then_inc(S["y_ready"], 1)
                for t in range(ALL_TILES):
                    dve.wait_ge(gathered[t % 4], 16 * (t // 4 + 1))
                    dve.scalar_tensor_tensor(out=x_res[:, t, :], in0=y_tok[:, t % 4, :], scalar=gate[:, t:t + 1], in1=x_res[:, t, :],
                                             op0=ALU.mult, op1=ALU.add).then_inc(S["combined"], 1)


HD = 64
INNER = HEADS * HD
PAIRS = HEADS // 2
CLIP = 11.0


def cross_attention(nc, ctx_outer, T, A):
    with ExitStack() as ctx:
        def sb(name, shape, dt=F32):
            return ctx.enter_context(nc.sbuf_tensor("c_" + name, shape, dt))

        def sem(name):
            return ctx_outer.enter_context(nc.semaphore("c_" + name))

        score_ps = ctx.enter_context(nc.psum_tensor("c_scores", [P, 4, 512], F32))
        value_ps = ctx.enter_context(nc.psum_tensor("c_values", [P, 2, 512], F32))
        sum_ps = ctx.enter_context(nc.psum_tensor("c_sums", [P, 2, 512], F32))
        x_res, ident = T["x_res"], T["ident"]
        SCALE = HD ** -0.5
        LOW, HIGH = float(np.exp(-CLIP)), float(np.exp(CLIP))

        wq = sb("wq", [P, DK, INNER])
        wkv = sb("wkv", [P, DK, 2 * INNER])
        wo = sb("wo", [P, PAIRS, DIM])
        bo = sb("bo", [P, DIM])
        ln_col = sb("ln_col", [P, 4, DK])
        z1 = sb("z1", [P, ALL_TILES, DIM])
        stats = sb("stats", [P, ALL_TILES, 6])
        moments = sb("moments", [P, 3, ALL_TILES, 2])
        rstd = sb("rstd", [P, 3, 2, ALL_TILES])
        now = sb("now", [P, 2, 12])
        lat_b = sb("lat_b", [P, TOK_TILES, DIM])
        ctx_raw = sb("ctx_raw", [P, TOK_TILES, DIM])
        latT = sb("latT", [P, DK, SEQ])
        ctxT = sb("ctxT", [P, DK, SEQ])
        q_half = sb("q_half", [P, HEADS, SEQ])
        kT = sb("kT", [P, PAIRS, SEQ])
        v = sb("v", [P, TOK_TILES, INNER])
        ctx_all = v[:, :, :].rearrange("p t n -> p (t n)").rearrange("p (t d) -> p t d", d=DIM)
        prob = sb("prob", [P, 2, TOK_TILES, 2, SEQ])
        key_sum = sb("key_sum", [P, 2, 2, SEQ])
        rinv = key_sum
        oT = sb("oT", [P, PAIRS, SEQ])
        recip = sb("recip", [P, SEQ])
        ones = sb("ones", [P, HD])

        names = ("w_in ctx_all_in ln_in bo_in stats1 stats2 stats3 std1 std2 std3 half_zero ones_ready ctx_in lat_ready "
                 "pro_mm pro_act pro_dve scores exp clipped summed values sums normed wo_mm dve_own pool_own").split()
        S = {n: sem(n) for n in names}

        JOBS = [("lat", 0, "d"), ("lat", 1, "d"), ("ctx", 0, "a"), ("ctx", 1, "a")]
        JOBS += [("q", f, "ad") for f in range(PAIRS)] + [("k", f, "ad"[f % 2]) for f in range(PAIRS)]
        JOBS += [("v", f, "ad"[f % 2]) for f in range(8)]

        def copied(engine, upto):
            return sum(engine in e for _, _, e in JOBS[:upto])

        ACT_JOBS, DVE_JOBS, N_JOBS = copied("a", len(JOBS)), copied("d", len(JOBS)), len(JOBS)
        STEPS = PAIRS * TOK_TILES

        with nc.Block() as block:
            @block.sync
            def _(sp):
                sp.dma_start(ctx_all, A["ctx_1024"].rearrange("b (q p) d -> p (b q) d", p=P)).then_inc(S["ctx_all_in"], 16)
                sp.dma_start(wq[:, :, :], A["L1_xattn_Wq"].rearrange("(k p) n -> p k n", p=P)).then_inc(S["w_in"], 16)
                sp.dma_start(wkv[:, :, :], A["L1_xattn_Wkv"].rearrange("(k p) n -> p k n", p=P)).then_inc(S["w_in"], 16)
                sp.dma_start(wo[:, :, :], A["L1_xattn_Wo"].rearrange("(k p) n -> p k n", p=P)).then_inc(S["w_in"], 16)
                sp.dma_start(bo[:, :], A["L1_xattn_bo"].rearrange("(a n) -> a n", a=1).broadcast_to([P, DIM])).then_inc(S["bo_in"], 16)
                for i, n in enumerate(("ln_l_w", "ln_l_b", "ln_c_w", "ln_c_b")):
                    for k in range(DK):
                        sp.dma_start(ln_col[:, i, k:k + 1], A["L1_xattn_" + n][k * P:(k + 1) * P].rearrange("(p a) -> p a", a=1)).then_inc(S["ln_in"], 16)
                with sp.Fori(0, BATCH) as b:
                    sp.wait_ge(S["pro_mm"], b * N_JOBS)
                    sp.dma_start(ctx_raw[:, :, :], A["ctx_1024"][bass.ds(b, 1)].rearrange("a (q p) d -> p (a q) d", p=P)).then_inc(S["ctx_in"], 16)

            @block.gpsimd
            def _(pool):
                own = Steps(pool, S["pool_own"])
                pool.memset(ones[:, :], 1.0).then_inc(S["ones_ready"], 1)
                pool.memset(q_half[:, :, :], 0.0).then_inc(S["half_zero"], 1)
                with pool.Fori(0, BATCH) as b:
                    own.loop(b, PAIRS * 2)
                    for p in range(PAIRS):
                        acc = key_sum[:, p % 2, :, :]
                        for k in range(1, TOK_TILES):
                            if k > 1:
                                own.wait()
                            elif p >= 2:
                                pool.wait_ge(S["sums"], b * PAIRS + p - 1)
                            else:
                                pool.wait_ge(S["sums"], b * PAIRS)
                            pool.wait_ge(S["clipped"], b * STEPS + p * TOK_TILES + k + 1)
                            first = prob[:, p % 2, 0, :, :] if k == 1 else acc
                            s = pool.tensor_tensor(acc, first, prob[:, p % 2, k, :, :], ALU.add)
                            if k < TOK_TILES - 1:
                                own.done(s)
                        s.then_inc(S["summed"], 1)
                    own.end_loop(BATCH)

            @block.tensor
            def _(pe):
                pe.wait_ge(S["w_in"], 48)
                pe.wait_ge(S["ones_ready"], 1)
                with pe.Fori(0, BATCH) as b:
                    for j, (kind, f, _) in enumerate(JOBS):
                        bank = score_ps[:, j % 4, :]
                        if j >= 4:
                            upto = max(j - 3, 2 if kind == "q" else 4)
                            pe.wait_ge(S["pro_act"], b * ACT_JOBS + copied("a", upto))
                            pe.wait_ge(S["pro_dve"], b * DVE_JOBS + copied("d", upto))
                        else:
                            pe.wait_ge(S["exp"], b * STEPS)
                            pe.wait_ge(S["normed"], b * (PAIRS + 2))
                        if kind in ("lat", "ctx"):
                            if f == 0 and kind == "lat":
                                pe.wait_ge(S["lat_ready"], 2 * b + 1)
                            if f == 0 and kind == "ctx":
                                pe.wait_ge(S["lat_ready"], 2 * b + 2)
                            src = lat_b if kind == "lat" else ctx_raw
                            for q in range(TOK_TILES):
                                mm = pe.transpose(bank[:, q * P:(q + 1) * P], src[:, q, f * P:(f + 1) * P], ident[:, :])
                        elif kind == "q":
                            for k in range(DK):
                                mm = pe.matmul(bank, wq[:, k, f * P:(f + 1) * P], latT[:, k, :], start=k == 0, stop=k == DK - 1)
                        elif kind == "k":
                            for k in range(DK):
                                mm = pe.matmul(bank, wkv[:, k, f * P:(f + 1) * P], ctxT[:, k, :], start=k == 0, stop=k == DK - 1)
                        else:
                            t, half = f // 2, f % 2
                            for k in range(DK):
                                mm = pe.matmul(bank, ctxT[:, k, t * P:(t + 1) * P], wkv[:, k, INNER + half * 512:INNER + (half + 1) * 512],
                                               start=k == 0, stop=k == DK - 1)
                        mm.then_inc(S["pro_mm"], 1)
                    pe.wait_ge(S["pro_act"], (b + 1) * ACT_JOBS)
                    pe.wait_ge(S["pro_dve"], (b + 1) * DVE_JOBS)
                    for p in range(PAIRS + 1):
                        for k in range(TOK_TILES):
                            n = p * TOK_TILES + k
                            if p < PAIRS:
                                if n >= 2:
                                    pe.wait_ge(S["exp"], b * STEPS + n - 1)
                                for m in range(2):
                                    mm = pe.matmul(score_ps[:, 2 * (k % 2) + m, :], kT[:, p, k * P:(k + 1) * P], q_half[:, 2 * p + m, :], start=True, stop=True)
                                mm.then_inc(S["scores"], 1)
                            if p:
                                g = p - 1
                                pe.wait_ge(S["clipped"], b * STEPS + g * TOK_TILES + k + 1)
                                if k == 0 and g >= 2:
                                    pe.wait_ge(S["normed"], b * (PAIRS + 2) + g - 1)
                                for m in range(2):
                                    mm = pe.matmul(value_ps[m * HD:(m + 1) * HD, g % 2, :], v[:, k, (2 * g + m) * HD:(2 * g + m + 1) * HD],
                                                   prob[:, g % 2, k, m, :], start=k == 0, stop=k == TOK_TILES - 1)
                                mm.then_inc(S["values"], 1)
                        if p:
                            pe.wait_ge(S["summed"], b * PAIRS + p)
                            for m in range(2):
                                mm = pe.matmul(sum_ps[m * HD:(m + 1) * HD, (p - 1) % 2, :], ones[:, :], key_sum[:, (p - 1) % 2, m, :], start=True, stop=True)
                            mm.then_inc(S["sums"], 1)
                    pe.wait_ge(S["normed"], b * (PAIRS + 2) + PAIRS)
                    for q in range(TOK_TILES):
                        for k in range(PAIRS):
                            mm = pe.matmul(score_ps[:, q // 2, (q % 2) * DIM:(q % 2 + 1) * DIM], oT[:, k, q * P:(q + 1) * P], wo[:, k, :],
                                           start=k == 0, stop=k == PAIRS - 1)
                        if q % 2:
                            mm.then_inc(S["wo_mm"], 1)

            @block.scalar
            def _(act):
                for i in range(3):
                    act.wait_ge(S[f"stats{i + 1}"], 1)
                    act.activation(rstd[:, i, 0, :], moments[:, i, :, 1], ACT.Sqrt, bias=T["eps"][:, :]).then_inc(S[f"std{i + 1}"], 1)
                act.wait_ge(S["ln_in"], 64 * DK)
                act.wait_ge(S["half_zero"], 1)
                with act.Fori(0, BATCH) as b:
                    for j, (kind, f, engines) in enumerate(JOBS):
                        if "a" not in engines:
                            continue
                        bank = score_ps[:, j % 4, :]
                        act.wait_ge(S["pro_mm"], b * N_JOBS + j + 1)
                        if kind == "ctx":
                            s = act.activation(ctxT[:, f, :], bank, ACT.Identity, scale=ln_col[:, 2, f:f + 1], bias=ln_col[:, 3, f:f + 1])
                        elif kind == "q":
                            s = act.activation(q_half[0:HD, 2 * f, :], bank[0:HD, :], ACT.Copy, scale=SCALE)
                        elif kind == "k":
                            s = act.copy(kT[:, f, :], bank)
                        else:
                            s = act.copy(v[:, f // 2, (f % 2) * 512:(f % 2 + 1) * 512], bank)
                        s.then_inc(S["pro_act"], 1)
                    for p in range(PAIRS):
                        for k in range(TOK_TILES):
                            n = p * TOK_TILES + k
                            if p >= 2:
                                act.wait_ge(S["values"], b * STEPS + n - 2 * TOK_TILES + 1)
                                if k == 0:
                                    act.wait_ge(S["summed"], b * PAIRS + p - 1)
                            act.wait_ge(S["scores"], b * STEPS + n + 1)
                            act.activation(prob[:, p % 2, k, :, :], score_ps[:, 2 * (k % 2):2 * (k % 2) + 2, :], ACT.Exp).then_inc(S["exp"], 1)

            @block.vector
            def _(dve):
                own = Steps(dve, S["dve_own"])

                def stats_of(i, src):
                    for t in range(ALL_TILES):
                        s = dve.bn_stats(stats[:, t, :], src[:, t, :])
                    own.done(s)
                    own.wait()
                    for t in range(ALL_TILES):
                        s = dve.bn_aggr(moments[:, i, t, :], stats[:, t, :])
                    own.done(s)
                    own.wait()
                    dve.tensor_copy(now[:, 0, i:i + 1], moments[:, i, 0, 0:1]).then_inc(S[f"stats{i + 1}"], 1)

                def root_of(i):
                    dve.wait_ge(S[f"std{i + 1}"], 1)
                    own.done(dve.reciprocal(rstd[:, i, 1, :], rstd[:, i, 0, :]))
                    own.wait()

                stats_of(0, x_res)
                root_of(0)
                for t in range(ALL_TILES):
                    s = dve.tensor_scalar(z1[:, t, :], x_res[:, t, :], moments[:, 0, t, 0:1], rstd[:, 0, 1, t:t + 1], ALU.subtract, ALU.mult)
                own.done(s)
                own.wait()
                stats_of(1, z1)
                root_of(1)
                dve.wait_ge(S["ctx_all_in"], 16)
                stats_of(2, ctx_all)
                root_of(2)
                dve.wait_ge(S["bo_in"], 16)
                own.done(dve.tensor_tensor(x_res[:, :, :], x_res[:, :, :], bo[:, :].rearrange("p (a n) -> p a n", a=1).broadcast_to([P, ALL_TILES, DIM]), ALU.add))
                own.wait()
                dve.wait_ge(S["ln_in"], 64 * DK)
                dve.wait_ge(S["half_zero"], 1)
                with dve.Fori(0, BATCH) as b:
                    own.loop(b, 4 + PAIRS)
                    for i in range(2):
                        mom = moments[:, i + 1, :, :].rearrange("p (b q) c -> p b (q c)", b=BATCH)
                        rs = rstd[:, i + 1, 1, :].rearrange("p (b q) -> p b q", b=BATCH)
                        own.done(dve.tensor_copy(now[:, i, 0:8], mom[:, bass.ds(b, 1), :].rearrange("p a n -> p (a n)")))
                        own.done(dve.tensor_copy(now[:, i, 8:12], rs[:, bass.ds(b, 1), :].rearrange("p a n -> p (a n)")))
                    own.wait()
                    zv = z1[:, :, :].rearrange("p (b q) d -> p b (q d)", b=BATCH)
                    for q in range(TOK_TILES):
                        s = dve.tensor_scalar(lat_b[:, q, :], flat(zv[:, bass.ds(b, 1), q * DIM:(q + 1) * DIM]),
                                              now[:, 0, 2 * q:2 * q + 1], now[:, 0, 8 + q:9 + q], ALU.subtract, ALU.mult)
                    s.then_inc(S["lat_ready"], 1)
                    dve.wait_ge(S["ctx_in"], b * 16 + 16)
                    for q in range(TOK_TILES):
                        s = dve.tensor_scalar(ctx_raw[:, q, :], ctx_raw[:, q, :], now[:, 1, 2 * q:2 * q + 1], now[:, 1, 8 + q:9 + q],
                                              ALU.subtract, ALU.mult)
                    s.then_inc(S["lat_ready"], 1)
                    for j, (kind, f, engines) in enumerate(JOBS):
                        if "d" not in engines:
                            continue
                        bank = score_ps[:, j % 4, :]
                        dve.wait_ge(S["pro_mm"], b * N_JOBS + j + 1)
                        if kind == "lat":
                            s = dve.tensor_scalar(latT[:, f, :], bank, ln_col[:, 0, f:f + 1], ln_col[:, 1, f:f + 1], ALU.mult, ALU.add)
                        elif kind == "q":
                            s = dve.tensor_scalar(q_half[HD:P, 2 * f + 1, :], bank[HD:P, :], SCALE, None, ALU.mult)
                        elif kind == "k":
                            s = dve.tensor_copy(kT[:, f, :], bank)
                        else:
                            s = dve.tensor_copy(v[:, f // 2, (f % 2) * 512:(f % 2 + 1) * 512], bank)
                        s.then_inc(S["pro_dve"], 1)

                    def normalise(g):
                        dve.wait_ge(S["sums"], b * PAIRS + g + 1)
                        dve.wait_ge(S["normed"], b * (PAIRS + 2) + g)
                        own.done(dve.reciprocal(recip[:, :], sum_ps[:, g % 2, :]))
                        own.wait()
                        dve.tensor_tensor(oT[:, g, :], value_ps[:, g % 2, :], recip[:, :], ALU.mult).then_inc(S["normed"], 1)

                    for p in range(PAIRS + 2):
                        for k in range(TOK_TILES):
                            if p < PAIRS:
                                dve.wait_ge(S["exp"], b * STEPS + p * TOK_TILES + k + 1)
                                tile = prob[:, p % 2, k, :, :]
                                dve.tensor_scalar(tile, tile, LOW, HIGH, ALU.max, ALU.min).then_inc(S["clipped"], 1)
                            if k == 1 and p >= 2:
                                normalise(p - 2)
                    xv = x_res[:, :, :].rearrange("p (b q) d -> p b (q d)", b=BATCH)
                    for h in range(2):
                        dve.wait_ge(S["wo_mm"], 2 * b + h + 1)
                        xq = flat(xv[:, bass.ds(b, 1), h * 512:(h + 1) * 512])
                        dve.tensor_tensor(xq, score_ps[:, h, :], xq, ALU.add).then_inc(S["normed"], 1)
                    own.end_loop(BATCH)


HID = 1024
HID_TILES = HID // P
ROUND = 1.5 * 2.0 ** 23
QMAX = 127.0
RING = 4


def ternary_ffn(nc, ctx_outer, T, A):
    with ExitStack() as ctx:
        def sb(name, shape, dt=F32):
            return ctx.enter_context(nc.sbuf_tensor("d_" + name, shape, dt))

        def sem(name):
            return ctx_outer.enter_context(nc.semaphore("d_" + name))

        wide_ps = [ctx.enter_context(nc.psum_tensor(f"d_wide{i}", [P, 512], F32)) for i in range(6)]
        bf_ps = [ctx.enter_context(nc.psum_tensor(f"d_bf{i}", [P, 1024], BF16)) for i in range(2)]
        x_res, ident = T["x_res"], T["ident"]

        w_raw = sb("w_raw", [P, 2, 2048])
        w_tern = sb("w_tern", [P, 2, 2048], BF16)
        w1T = sb("w1T", [P, DK, HID], BF16)
        w2T = sb("w2T", [P, HID_TILES, DIM], BF16)
        ident_b = sb("ident_b", [P, P], BF16)
        ones = sb("ones", [P, P])
        tap_rows = sb("tap_rows", [HID_TILES, 4, P])
        tap_raw = sb("tap_raw", [HID_TILES, P * 3])
        taps = sb("taps", [P, 4, HID_TILES])
        w_sum = sb("w_sum", [P, 2])
        w_inv = sb("w_inv", [P, 2])
        w_scale = sb("w_scale", [P, 2])
        stats = sb("stats", [P, ALL_TILES, 6])
        moments = sb("moments", [P, ALL_TILES, 2])
        rstd = sb("rstd", [P, 2, ALL_TILES])
        z = sb("z", [P, ALL_TILES, DIM])
        tok = sb("tok", [P, 4, ALL_TILES])
        spread = sb("spread", [P, ALL_TILES, P])
        undo = sb("undo", [P, ALL_TILES * P])
        xq_b = sb("xq_b", [P, TOK_TILES, DIM], BF16)
        xqT = sb("xqT", [P, DK, SEQ], BF16)
        h_pad = sb("h_pad", [P, RING, SEQ + 2])
        conv = sb("conv", [P, RING, SEQ])
        act_h = sb("act_h", [P, HID_TILES, SEQ])
        top = sb("top", [P, SEQ])
        tok2 = sb("tok2", [P, 4, TOK_TILES])
        spread2 = sb("spread2", [P, TOK_TILES, P])
        scaled = sb("scaled", [P, 2, SEQ])
        hq = sb("hq", [P, HID_TILES, SEQ], BF16)

        names = ("w_in taps_in ones_ready pads_zero w_summed w_total tern_ready w_turned wT_ready taps_turned taps_ready "
                 "stats_ready std_ready spread_ready undo_turned undo_ready xq_ready xq_turned xqT_ready h_mm h_ready centre "
                 "conv_done silu top_done top_turned spread2_ready up_turned hq_ready y_mm y_added dve_own identb_ready").split()
        S = {n: sem(n) for n in names}

        with nc.Block() as block:
            @block.sync
            def _(sp):
                sp.dma_start(w_raw[:, 0, :].rearrange("p (f d) -> p f d", d=DIM), A["L1_ffn_w1"].rearrange("(f p) d -> p f d", p=P)).then_inc(S["w_in"], 16)
                sp.dma_start(w_raw[:, 1, :].rearrange("p (o h) -> p o h", h=HID), A["L1_ffn_w2"].rearrange("(o p) h -> p o h", p=P)).then_inc(S["w_in"], 16)
                sp.dma_start(tap_raw[:, :], A["L1_ffn_conv_w"].rearrange("(f p) a j -> f (p a j)", p=P)).then_inc(S["taps_in"], 16)
                sp.dma_start(tap_rows[:, 3, :], A["L1_ffn_conv_b"].rearrange("(f p) -> f p", p=P)).then_inc(S["taps_in"], 16)

            @block.gpsimd
            def _(pool):
                pool.memset(ones[:, :], 1.0).then_inc(S["ones_ready"], 1)
                pool.memset(h_pad[:, :, :], 0.0).then_inc(S["pads_zero"], 1)

            @block.tensor
            def _(pe):
                pe.wait_ge(S["taps_in"], 32)
                pe.wait_ge(S["taps_turned"], 1)
                for j in range(4):
                    mm = pe.transpose(wide_ps[0][:, j * HID_TILES:(j + 1) * HID_TILES], tap_rows[:, j, :], ident[0:HID_TILES, 0:HID_TILES])
                mm.then_inc(S["taps_turned"], 1)
                pe.wait_ge(S["ones_ready"], 1)
                pe.wait_ge(S["w_summed"], 1)
                pe.matmul(wide_ps[1][:, 0:2], ones[:, :], w_sum[:, :], start=True, stop=True).then_inc(S["w_total"], 1)
                pe.wait_ge(S["spread_ready"], 1)
                for b in range(BATCH):
                    for q in range(TOK_TILES):
                        mm = pe.transpose(wide_ps[2 + b][:, q * P:(q + 1) * P], spread[:, b * TOK_TILES + q, :], ident[:, :])
                    mm.then_inc(S["undo_turned"], 1)
                pe.wait_ge(S["tern_ready"], 1)
                for k in range(DK):
                    for f in range(HID_TILES):
                        mm = pe.transpose(bf_ps[k][:, f * P:(f + 1) * P], w_tern[:, 0, f * DIM + k * P:f * DIM + (k + 1) * P], ident_b[:, :])
                mm.then_inc(S["w_turned"], 1)
                pe.wait_ge(S["tern_ready"], 2)
                pe.wait_ge(S["wT_ready"], 1)
                for o in range(DK):
                    for f in range(HID_TILES):
                        mm = pe.transpose(bf_ps[o][:, f * P:(f + 1) * P], w_tern[:, 1, o * HID + f * P:o * HID + (f + 1) * P], ident_b[:, :])
                mm.then_inc(S["w_turned"], 1)
                pe.wait_ge(S["wT_ready"], 2)
                pe.wait_ge(S["undo_ready"], 1)
                with pe.Fori(0, BATCH) as b:
                    pe.wait_ge(S["xq_ready"], b + 1)
                    for k in range(DK):
                        for q in range(TOK_TILES):
                            mm = pe.transpose(bf_ps[0][:, (k * TOK_TILES + q) * P:(k * TOK_TILES + q + 1) * P], xq_b[:, q, k * P:(k + 1) * P], ident_b[:, :])
                    mm.then_inc(S["xq_turned"], 1)
                    pe.wait_ge(S["xqT_ready"], b + 1)
                    for f in range(HID_TILES):
                        if f < 2:
                            pe.wait_ge(S["h_ready"], b * HID_TILES)
                        else:
                            pe.wait_ge(S["h_ready"], b * HID_TILES + f - 1)
                        for k in range(DK):
                            mm = pe.matmul(wide_ps[f % 2][:, :], w1T[:, k, f * P:(f + 1) * P], xqT[:, k, :], start=k == 0, stop=k == DK - 1)
                        mm.then_inc(S["h_mm"], 1)
                    pe.wait_ge(S["top_done"], b + 1)
                    for q in range(TOK_TILES):
                        mm = pe.transpose(wide_ps[2][:, q * P:(q + 1) * P], top[:, q * P:(q + 1) * P], ident[:, :])
                    mm.then_inc(S["top_turned"], 1)
                    pe.wait_ge(S["spread2_ready"], b + 1)
                    for q in range(TOK_TILES):
                        mm = pe.transpose(wide_ps[3][:, q * P:(q + 1) * P], spread2[:, q, :], ident[:, :])
                    mm.then_inc(S["up_turned"], 1)
                    pe.wait_ge(S["hq_ready"], (b + 1) * HID_TILES)
                    for q in range(TOK_TILES):
                        for f in range(HID_TILES):
                            mm = pe.matmul(wide_ps[4 + q // 2][:, (q % 2) * DIM:(q % 2 + 1) * DIM], hq[:, f, q * P:(q + 1) * P], w2T[:, f, :],
                                           start=f == 0, stop=f == HID_TILES - 1)
                        if q % 2:
                            mm.then_inc(S["y_mm"], 1)

            @block.scalar
            def _(act):
                act.wait_ge(S["stats_ready"], 1)
                act.activation(rstd[:, 0, :], moments[:, :, 1], ACT.Sqrt, bias=T["eps"][:, :]).then_inc(S["std_ready"], 1)
                for b in range(BATCH):
                    act.wait_ge(S["undo_turned"], b + 1)
                    s = act.copy(undo[:, b * SEQ:(b + 1) * SEQ], wide_ps[2 + b][:, :])
                s.then_inc(S["undo_ready"], 1)
                act.wait_ge(S["w_turned"], 1)
                for k in range(DK):
                    s = act.copy(w1T[:, k, :], bf_ps[k][:, :])
                s.then_inc(S["wT_ready"], 1)
                act.wait_ge(S["w_turned"], 2)
                for o in range(DK):
                    s = act.copy(w2T[:, :, o * P:(o + 1) * P], bf_ps[o][:, :].rearrange("p (f n) -> p f n", n=P))
                s.then_inc(S["wT_ready"], 1)
                act.wait_ge(S["taps_ready"], 1)
                with act.Fori(0, BATCH) as b:
                    act.wait_ge(S["xq_turned"], b + 1)
                    act.copy(xqT[:, :, :].rearrange("p k n -> p (k n)"), bf_ps[0][:, :]).then_inc(S["xqT_ready"], 1)
                    for f in range(HID_TILES + 2):
                        if f < HID_TILES:
                            act.wait_ge(S["h_ready"], b * HID_TILES + f + 1)
                            if f >= RING:
                                act.wait_ge(S["silu"], b * HID_TILES + f - RING + 1)
                            act.activation(conv[:, f % RING, :], h_pad[:, f % RING, 1:SEQ + 1], ACT.Identity, scale=taps[:, 1, f:f + 1],
                                           bias=taps[:, 3, f:f + 1]).then_inc(S["centre"], 1)
                        if f >= 2:
                            act.wait_ge(S["conv_done"], b * HID_TILES + f - 1)
                            act.activation(act_h[:, f - 2, :], conv[:, (f - 2) % RING, :], ACT.Silu).then_inc(S["silu"], 1)

            @block.vector
            def _(dve):
                own = Steps(dve, S["dve_own"])

                def do(instruction):
                    own.done(instruction)
                    own.wait()

                dve.tensor_copy(ident_b[:, :], ident[:, :]).then_inc(S["identb_ready"], 1)
                dve.wait_ge(S["taps_in"], 32)
                for j in range(3):
                    s = dve.tensor_copy(tap_rows[:, j, :], tap_raw[:, :].rearrange("f (p j) -> f j p", j=3)[:, j, :])
                s.then_inc(S["taps_turned"], 1)
                dve.wait_ge(S["w_in"], 32)
                for i in range(2):
                    s = dve.tensor_reduce(w_sum[:, i:i + 1], w_raw[:, i, :], AX.X, ALU.add, apply_absolute_value=True)
                s.then_inc(S["w_summed"], 1)
                s = layernorm_all(dve, own, S["stats_ready"], S["std_ready"], 1, x_res, stats, moments, rstd, z)
                do(s)
                do(dve.tensor_reduce(tok[:, 0, :], z[:, :, :], AX.X, ALU.max, apply_absolute_value=True))
                do(dve.tensor_scalar(tok[:, 0, :], tok[:, 0, :], 1e-5, None, ALU.max))
                dve.tensor_scalar(tok[:, 3, :], tok[:, 0, :], 1.0 / QMAX, None, ALU.mult)
                do(dve.reciprocal(tok[:, 1, :], tok[:, 0, :]))
                do(dve.tensor_scalar(tok[:, 2, :], tok[:, 1, :], QMAX, None, ALU.mult))
                dve.wait_ge(S["ones_ready"], 1)
                dve.tensor_tensor(spread[:, :, :], ones[:, :].rearrange("p (a n) -> p a n", a=1).broadcast_to([P, ALL_TILES, P]),
                                  tok[:, 3, :].rearrange("p (t a) -> p t a", a=1).broadcast_to([P, ALL_TILES, P]), ALU.mult).then_inc(S["spread_ready"], 1)
                for t in range(ALL_TILES):
                    s = dve.tensor_scalar(z[:, t, :], z[:, t, :], tok[:, 2, t:t + 1], ROUND, ALU.mult, ALU.add)
                dve.wait_ge(S["w_total"], 1)
                do(dve.tensor_scalar(w_inv[:, :], wide_ps[1][:, 0:2], 1.0 / (HID * DIM), 1e-5, ALU.mult, ALU.max))
                do(dve.reciprocal(w_scale[:, :], w_inv[:, :]))
                for i in range(2):
                    do(dve.tensor_scalar(w_raw[:, i, :], w_raw[:, i, :], w_scale[:, i:i + 1], ROUND, ALU.mult, ALU.add))
                    do(dve.tensor_scalar(w_raw[:, i, :], w_raw[:, i, :], ROUND + 1.0, ROUND - 1.0, ALU.min, ALU.max))
                    dve.tensor_scalar(w_tern[:, i, :], w_raw[:, i, :], ROUND, None, ALU.subtract).then_inc(S["tern_ready"], 1)
                dve.wait_ge(S["taps_turned"], 2)
                do(dve.tensor_scalar(taps[:, 0:3, :].rearrange("p j f -> p (j f)"), wide_ps[0][:, 0:3 * HID_TILES], w_inv[:, 0:1], None, ALU.mult))
                dve.tensor_copy(taps[:, 3, :], wide_ps[0][:, 3 * HID_TILES:4 * HID_TILES]).then_inc(S["taps_ready"], 1)
                dve.wait_ge(S["taps_ready"], 1)
                dve.wait_ge(S["pads_zero"], 1)
                dve.wait_ge(S["undo_ready"], 1)
                with dve.Fori(0, BATCH) as b:
                    own.loop(b, DVE_D)
                    zv = z[:, :, :].rearrange("p (b q) d -> p b (q d)", b=BATCH)
                    dve.tensor_scalar(xq_b[:, :, :].rearrange("p q d -> p (q d)"), flat(zv[:, bass.ds(b, 1), :]), ROUND, None, ALU.subtract).then_inc(S["xq_ready"], 1)

                    for f in range(HID_TILES + 1):
                        if f < HID_TILES:
                            dve.wait_ge(S["h_mm"], b * HID_TILES + f + 1)
                            if f >= RING:
                                dve.wait_ge(S["conv_done"], b * HID_TILES + f - RING + 1)
                            dve.tensor_tensor(h_pad[:, f % RING, 1:SEQ + 1], wide_ps[f % 2][:, :], undo[:, bass.ds(b * SEQ, SEQ)], ALU.mult).then_inc(S["h_ready"], 1)
                        if 1 <= f <= HID_TILES:
                            g = f - 1
                            c = conv[:, g % RING, :]
                            dve.wait_ge(S["centre"], b * HID_TILES + g + 1)
                            own.done(dve.scalar_tensor_tensor(out=c, in0=h_pad[:, g % RING, 0:SEQ], scalar=taps[:, 0, g:g + 1], in1=c, op0=ALU.mult, op1=ALU.add))
                            own.wait()
                            dve.scalar_tensor_tensor(out=c, in0=h_pad[:, g % RING, 2:SEQ + 2], scalar=taps[:, 2, g:g + 1], in1=c,
                                                     op0=ALU.mult, op1=ALU.add).then_inc(S["conv_done"], 1)
                    dve.wait_ge(S["silu"], (b + 1) * HID_TILES)
                    dve.tensor_reduce(top[:, :], act_h[:, :, :].rearrange("p f n -> p n f"), AX.X, ALU.max, apply_absolute_value=True).then_inc(S["top_done"], 1)
                    dve.wait_ge(S["top_turned"], b + 1)
                    do(dve.tensor_reduce(tok2[:, 0, :], wide_ps[2][:, :].rearrange("p (q n) -> p q n", n=P), AX.X, ALU.max))
                    do(dve.tensor_scalar(tok2[:, 0, :], tok2[:, 0, :], 1e-5, None, ALU.max))
                    do(dve.tensor_scalar(tok2[:, 3, :], tok2[:, 0, :], w_inv[:, 1:2], 1.0 / QMAX, ALU.mult, ALU.mult))
                    do(dve.reciprocal(tok2[:, 1, :], tok2[:, 0, :]))
                    do(dve.tensor_scalar(tok2[:, 2, :], tok2[:, 1, :], QMAX, None, ALU.mult))
                    dve.tensor_tensor(spread2[:, :, :], ones[:, :].rearrange("p (a n) -> p a n", a=1).broadcast_to([P, TOK_TILES, P]),
                                      tok2[:, 2, :].rearrange("p (t a) -> p t a", a=1).broadcast_to([P, TOK_TILES, P]), ALU.mult).then_inc(S["spread2_ready"], 1)
                    dve.wait_ge(S["up_turned"], b + 1)
                    for f in range(HID_TILES):
                        if f >= 2:
                            dve.wait_ge(S["hq_ready"], b * HID_TILES + f - 1)
                        else:
                            dve.wait_ge(S["hq_ready"], b * HID_TILES)
                        do(dve.tensor_tensor(scaled[:, f % 2, :], wide_ps[3][:, :], act_h[:, f, :], ALU.mult))
                        dve.tensor_scalar(hq[:, f, :], scaled[:, f % 2, :], ROUND, ROUND, ALU.add, ALU.subtract).then_inc(S["hq_ready"], 1)
                    xv = x_res[:, :, :].rearrange("p (b q) d -> p b (q d)", b=BATCH)
                    for q in range(TOK_TILES):
                        dve.wait_ge(S["y_mm"], 2 * b + q // 2 + 1)
                        xq = flat(xv[:, bass.ds(b, 1), q * DIM:(q + 1) * DIM])
                        dve.scalar_tensor_tensor(out=xq, in0=wide_ps[4 + q // 2][:, (q % 2) * DIM:(q % 2 + 1) * DIM], scalar=tok2[:, 3, q:q + 1], in1=xq,
                                                 op0=ALU.mult, op1=ALU.add).then_inc(S["y_added"], 1)
                    dve.wait_ge(S["y_added"], (b + 1) * TOK_TILES)
                    own.end_loop(BATCH)


DVE_D = HID_TILES + 5 + HID_TILES


def program(nc, A, out):
    with ExitStack() as ctx:
        T = {}
        T["x_res"] = ctx.enter_context(nc.sbuf_tensor("x_res", [P, ALL_TILES, DIM], F32))
        T["ident"] = ctx.enter_context(nc.sbuf_tensor("ident", [P, P], F32))
        T["eps"] = ctx.enter_context(nc.sbuf_tensor("eps", [P, 1], F32))
        T["ident_ready"] = ctx.enter_context(nc.semaphore("ident_ready"))
        T["stored"] = ctx.enter_context(nc.semaphore("stored"))
        T["ident_count"] = 2
        with nc.Block() as block:
            @block.gpsimd
            def _(pool):
                pool.memset(T["ident"][:, :], 0.0).then_inc(T["ident_ready"], 1)
                pool.memset(T["eps"][:, :], EPS)
                pool.wait_ge(T["ident_ready"], 1)
                pool.affine_select(out=T["ident"][:, :], in_=T["ident"][:, :], compare_op=ALU.not_equal, fill=1.0, base=0,
                                   pattern=[[-1, P]], channel_multiplier=1).then_inc(T["ident_ready"], 1)
        diff_attention(nc, ctx, T, A)
        experts(nc, ctx, T, A)
        cross_attention(nc, ctx, T, A)
        ternary_ffn(nc, ctx, T, A)
        with nc.Block() as block:
            @block.sync
            def _(sp):
                sp.dma_start(out.rearrange("b (q p) d -> p (b q) d", p=P), T["x_res"][:, :, :]).then_inc(T["stored"], 16)
                sp.wait_ge(T["stored"], 16)


_OUT = (BATCH, SEQ, DIM)


def kernel(**inputs):
    import concourse.bacc as bacc
    from concourse.bass_utils import run_bass_kernel_spmd

    nc = bacc.Bacc("TRN2", target_bir_lowering=False, num_devices=1)
    arrays, args = {}, {}
    for name, value in inputs.items():
        a = np.ascontiguousarray(value)
        arrays[f"in_{name}_dram"] = a
        args[name] = nc.dram_tensor(f"in_{name}_dram", a.shape, mybir.dt.from_np(a.dtype), kind="ExternalInput").ap()
    out = nc.dram_tensor("out_0_dram", _OUT, F32, kind="ExternalOutput").ap()
    program(nc, args, out)
    r = run_bass_kernel_spmd(nc, [arrays], core_ids=[0])
    return r.results[0]["out_0_dram"]
```

```python
from contextlib import ExitStack

import numpy as np

import concourse.bass as bass
from concourse import mybir

F32 = mybir.dt.float32
BF16 = mybir.dt.bfloat16
I32 = mybir.dt.int32
ALU = mybir.AluOpType
ACT = mybir.ActivationFunctionType
AX = mybir.AxisListType

P = 128
BATCH, SEQ, DIM = 4, 512, 256
TOK_TILES = SEQ // P
ALL_TILES = BATCH * TOK_TILES
DK = DIM // P
EPS = 1e-5

DH = 16
HEADS = 16
MAPS = 2
FEATS = HEADS * MAPS * DH
FEAT_TILES = FEATS // P
MAPS_PER_TILE = P // DH
LAMBDA_INIT = 0.8


class Steps:

    def __init__(self, eng, sem):
        self.eng, self.sem, self.base, self.n = eng, sem, 0, 0
        self.turn = self.per_turn = None

    def loop(self, turn, per_turn, start=0):
        self.base, self.n, self.turn, self.per_turn = self.base + self.n - start * per_turn, 0, turn, per_turn
        self.start = start

    def end_loop(self, turns):
        assert self.n == self.per_turn, f"{self.sem} counts {self.n} per turn, not {self.per_turn}"
        self.base, self.n, self.turn = self.base + (self.start + turns) * self.per_turn, 0, None

    def over_turns(self, turns, per_turn, body):
        def counted(b, first, last):
            if first or last:
                body(b, first, last)
            else:
                self.loop(b, per_turn, 1)
                body(b, first, last)
                self.end_loop(turns)
        return counted

    def done(self, instruction):
        instruction.then_inc(self.sem, 1)
        self.n += 1
        return self.n

    def wait(self, n=None):
        n = self.n if n is None else n
        at = self.base + n
        self.eng.wait_ge(self.sem, at if self.turn is None else self.turn * self.per_turn + at)


def flat(ap):
    return ap.rearrange("p a n -> p (a n)")


def diff_attention(nc, ctx_outer, T, A):
    with ExitStack() as ctx:
        def sb(name, shape, dt=F32):
            return ctx.enter_context(nc.sbuf_tensor("a_" + name, shape, dt))

        def sem(name):
            return ctx_outer.enter_context(nc.semaphore("a_" + name))

        psum = [ctx.enter_context(nc.psum_tensor(f"a_bank{i}", [P, 512], F32)) for i in range(8)]
        score_ps, turn_ps, value_ps, job_ps = psum[0:4], psum[4:6], psum[6], psum[7]
        x_res, ident = T["x_res"], T["ident"]
        HALF = TOK_TILES // 2
        SCALE = 1.0 / float(np.sqrt(DH))
        PARTS = 3

        wq = sb("wq", [P, DK, FEATS])
        wk = sb("wk", [P, DK, FEATS])
        wv = sb("wv", [P, DK, DIM])
        wo = sb("wo", [P, DK, DIM])
        xnT = sb("xnT", [P, DK, SEQ])
        ctxT = sb("ctxT", [P, DK, SEQ])
        part = sb("part", [P, 2, PARTS, SEQ], BF16)
        rest = sb("rest", [P, SEQ])
        q_packed = sb("q_packed", [6 * DH, HEADS * MAPS, SEQ], BF16)
        k_packed = sb("k_packed", [6 * DH, HEADS * MAPS, SEQ], BF16)
        mask = sb("mask", [P, 2, TOK_TILES, SEQ])
        prob = sb("prob", [P, 2, TOK_TILES, MAPS, SEQ])
        attn = sb("attn", [P, 2, TOK_TILES, SEQ])
        attnT = sb("attnT", [P, TOK_TILES + 2, SEQ])
        value_part = sb("value_part", [P, SEQ])
        v = sb("v", [P, TOK_TILES, DIM + DH])
        o_heads = sb("o_heads", [P, HEADS, TOK_TILES, DH])
        o_norm = sb("o_norm", [P, TOK_TILES, HEADS, DH])
        xn_b = o_norm[:, :, :, :].rearrange("p q h d -> p q (h d)")
        oT = sb("oT", [P, DK, SEQ])
        ctx_b = oT[:, :, :].rearrange("p k n -> p (k n)").rearrange("p (q d) -> p q d", d=DIM)
        neg_max = sb("neg_max", [P, 2, TOK_TILES, MAPS])
        row_sum = sb("row_sum", [P, 2, MAPS, TOK_TILES])
        row_inv = sb("row_inv", [P, HEADS, MAPS, TOK_TILES])
        coef = sb("coef", [P, 2, TOK_TILES])
        o_sum = sb("o_sum", [P, TOK_TILES, DH])
        small = sb("small", [P, 3, HEADS * TOK_TILES])
        norm_now = sb("norm_now", [P, 3 * TOK_TILES])
        stats = sb("stats", [P, ALL_TILES, 6])
        moments = sb("moments", [P, ALL_TILES, 2])
        rstd = sb("rstd", [P, 2, ALL_TILES])
        lam_in = attnT[:, 0:TOK_TILES, 0:HEADS * DH]
        neg_lam = sb("neg_lam", [P, HEADS])
        rms_col = sb("rms_col", [P, 2])
        q_parts_d = nc.dram_tensor("a_q_parts", (BATCH, PARTS, FEATS, SEQ), BF16, kind="Internal").ap()
        k_parts_d = nc.dram_tensor("a_k_parts", (BATCH, PARTS, FEATS, SEQ), BF16, kind="Internal").ap()

        names = ("x_in w_in rest_in small_in dve_setup act_setup zero_ready ctx_in mask_in0 mask_in1 "
                 "xn_ready in_turned in_copied qk_mm part1 part2 part3 parts_written0 parts_written1 v_mm v_copied "
                 "scores masked exp combined combined_pool coef_ready rest_ready pool_own turned attnT_ready values value_copied out_turned gathered "
                 "ms_ready rms_ready on_ready on_turned oT_ready wo_mm x_added dve_own").split()
        S = {n: sem(n) for n in names}
        pack_in = [sem(f"pack_in{f}") for f in range(FEAT_TILES)]

        START_BANKS = score_ps + turn_ps
        UNITS = HEADS * TOK_TILES
        COEF, COMBINE, TURN, COPY, VALUES, COPY_VALUES, TURN_OUT, GATHER = 5, 6, 11, 11, 16, 16, 18, 18
        OUT_SQUARES, OUT_ROOT, OUT_NORM, NEXT_XN = 14, 15, 16, 28
        PLAN = [(2, "qk", 6, 0), (5, "qk", 7, 0), (12, "v", 0, 0), (14, "v", 1, 0),
                (21, "turn_o", 0, -1), (24, "turn_o", 1, -1), (27, "out", 0, -1), (30, "out", 1, -1),
                (33, "in", 0, 1), (36, "in", 1, 1), (39, "in", 2, 1), (42, "in", 3, 1), (45, "qk", 0, 1), (48, "qk", 1, 1),
                (51, "qk", 2, 1), (54, "qk", 3, 1), (57, "qk", 4, 1), (60, "qk", 5, 1)]
        START = [("in", 0), ("in", 1), ("qk", 0), ("in", 2), ("in", 3), ("qk", 1)]
        FIRST_PLAN = [(0, "qk", 2, 0), (3, "qk", 3, 0), (6, "qk", 4, 0), (9, "qk", 5, 0), (12, "v", 0, 0), (14, "v", 1, 0),
                      (18, "qk", 6, 0), (21, "qk", 7, 0)] + [p for p in PLAN if p[3] > 0]
        ZERO_SLOTS = 26
        COPY_JOB, SPLIT_JOB, THIRD_JOB, WRITE_JOB, TAIL = 0, 1, 2, 3, 32

        def released(kind, i, c):
            return {"qk": (S["rest_ready"], c * 8 + i + 1), "v": (S["v_copied"], c * 2 + i + 1), "turn_o": (S["oT_ready"], c * 2 + i + 1),
                    "out": (S["x_added"], c * 2 + i + 1), "in": (S["in_copied"], c * 4 + i + 1)}[kind]

        def plan(first, last):
            return FIRST_PLAN if first else [p for p in PLAN if not (last and p[3] > 0)]

        def planned(u, first, last, delay=0):
            return [p[1:] for p in plan(first, last) if p[0] + delay == u]

        def head(u):
            return (u // TOK_TILES) % HEADS

        def stage(u, lag, first, tail):
            w = u - lag
            if (first and w < 0) or (tail and w >= UNITS):
                return None
            return head(w), w % TOK_TILES, w

        def over_batches(eng, body):
            for u in range(UNITS):
                body(0, u, True, False, False)
            with eng.Fori(1, BATCH - 1) as b:
                for u in range(UNITS):
                    body(b, u, False, False, False)
            for u in range(UNITS):
                body(BATCH - 1, u, False, True, False)
            for u in range(UNITS, UNITS + TAIL):
                body(BATCH - 1, u, False, True, True)

        scratch = sb("scratch", [P, COPY_VALUES])

        def place(h, k):
            return k + TOK_TILES if k < 2 and h % 2 else k

        def one(b):
            return bass.ds(b, 1)

        with nc.Block() as block:
            @block.sync
            def _(sp):
                def load_ctx(c):
                    sp.dma_start(ctx_b, A["ctx_1024"][one(c)].rearrange("a (q p) d -> p (a q) d", p=P)).then_inc(S["ctx_in"], 16)

                def load_mask(c, h):
                    sp.dma_start(mask[:, h % 2, :, :], A["mask_Bx16xSxS2_ff0"][one(c), h].rearrange("a (q p) n -> p (a q) n", p=P)
                                 ).then_inc(S[f"mask_in{h % 2}"], 16)

                def write_parts(c, i):
                    sp.wait_ge(S["part3"], c * 8 + i + 1)
                    dst = (q_parts_d if i % 2 else k_parts_d)[one(c), :, (i // 2) * P:(i // 2 + 1) * P, :]
                    sp.dma_start(dst.rearrange("a j p n -> p (a j) n"), part[:, i % 2, :, :]).then_inc(S[f"parts_written{i % 2}"], 16)

                def read_packed(c, f):
                    sp.wait_ge(S["parts_written0"], (c * 4 + f + 1) * 16)
                    sp.wait_ge(S["parts_written1"], (c * 4 + f + 1) * 16)
                    row = 0
                    maps = slice(f * MAPS_PER_TILE, (f + 1) * MAPS_PER_TILE)
                    for j in range(PARTS):
                        for r in range(PARTS - j):
                            rows = slice(row, row + DH)
                            for dst, src, n in ((q_packed, q_parts_d, r), (k_packed, k_parts_d, j)):
                                sp.dma_start(dst[rows, maps, :], src[one(c), n, f * P:(f + 1) * P, :].rearrange("a (s d) n -> d (a s) n", d=DH)
                                             ).then_inc(pack_in[f], 16)
                            row += DH

                def load_x(tiles, signal):
                    sp.dma_start(x_res[:, tiles, :], A["x"].rearrange("b (q p) d -> p (b q) d", p=P)[:, tiles, :]).then_inc(signal, 16)

                def load_weights(names, signal):
                    for w, name in names:
                        sp.dma_start(w[:, :, :], A["L0_xattn_" + name].rearrange("(k p) n -> p k n", p=P)).then_inc(signal, 16)

                load_x(slice(0, TOK_TILES), S["x_in"])
                load_ctx(0)
                load_weights(((wk, "W_k"), (wq, "W_q")), S["w_in"])
                load_mask(0, 0)
                load_x(slice(TOK_TILES, ALL_TILES), S["rest_in"])
                load_weights(((wv, "W_v"), (wo, "W_o")), S["rest_in"])
                write_parts(0, 0)
                write_parts(0, 1)
                read_packed(0, 0)
                load_mask(0, 1)

                def body(b, u, first, last, tail):
                    if tail:
                        return
                    if u % TOK_TILES == TOK_TILES - 1:
                        h = u // TOK_TILES + 2
                        if not (last and h >= HEADS):
                            sp.wait_ge(S["masked"], (b * UNITS + u + 1) * MAPS)
                            load_mask(b + h // HEADS, h % HEADS)
                    if ZERO_SLOTS <= u < ZERO_SLOTS + FETCHED_TILES and first:
                        sp.dma_start(T["x_sorted"][(u - ZERO_SLOTS) * P:(u - ZERO_SLOTS + 1) * P, :], T["zeros"][:, :]).then_inc(T["slots_zeroed"], 16)
                    if u == NEXT_XN - 1 and not last:
                        if not first:
                            sp.wait_ge(S["wo_mm"], b * 2)
                        load_ctx(b + 1)
                    for kind, i, o in planned(u, first, last, WRITE_JOB):
                        if kind == "qk":
                            c = b + o
                            write_parts(c, i)
                            if i % 2:
                                read_packed(c, i // 2)

                over_batches(sp, body)

            @block.gpsimd
            def _(pool):
                pool.memset(v[:, :, DIM:], 0.0).then_inc(S["zero_ready"], 1)
                for i, n in enumerate(("q1", "k1", "q2", "k2")):
                    pool.dma_start(lam_in[:, i, :], A["L0_xattn_lambda_" + n].rearrange("h d -> (h d)").rearrange("(a n) -> a n", a=1)
                                   .broadcast_to([P, HEADS * DH])).then_inc(S["small_in"], 16)
                for g in range(P // DH):
                    pool.dma_start(rms_col[g * DH:(g + 1) * DH, 0:1], A["L0_xattn_rms_scale"].rearrange("(d a) -> d a", a=1)).then_inc(S["small_in"], 16)

                no_change = v[:, 0, DIM:DIM + 1].broadcast_to([P, SEQ])
                pool.wait_ge(S["zero_ready"], 1)

                def third_part(c, i):
                    pool.wait_ge(S["rest_ready"], c * 8 + i + 1)
                    pool.tensor_tensor(part[:, i % 2, 1, :], rest[:, :], no_change, ALU.add).then_inc(S["part2"], 1)
                    pool.wait_ge(S["part2"], c * 8 + i + 1)
                    pool.tensor_tensor(part[:, i % 2, 2, :], rest[:, :], part[:, i % 2, 1, :], ALU.subtract).then_inc(S["part3"], 1)

                for kind, i in START:
                    if kind == "qk":
                        third_part(0, i)

                def combine(b, h, w):
                    pool.wait_ge(S["coef_ready"], b * HEADS + w // TOK_TILES + 1)
                    if not (isinstance(b, int) and b == 0 and w < 2 * TOK_TILES):
                        pool.wait_ge(S["turned"], b * UNITS + w - TOK_TILES)
                    for q in range(HALF, TOK_TILES):
                        pool.tensor_tensor(prob[:, h % 2, q, 1, :], prob[:, h % 2, q, 1, :],
                                           coef[:, h % 2, q:q + 1].broadcast_to([P, SEQ]), ALU.mult).then_inc(S["pool_own"], 1)
                    for q in range(HALF, TOK_TILES):
                        pool.wait_ge(S["pool_own"], (b * HEADS + w // TOK_TILES) * HALF + q - HALF + 1)
                        pool.tensor_tensor(attn[:, h % 2, q, :], prob[:, h % 2, q, 1, :], prob[:, h % 2, q, 0, :], ALU.add).then_inc(S["combined_pool"], 1)

                def body(b, u, first, last, tail):
                    if (s := stage(u, COEF, first, tail)) and s[1] == 0:
                        combine(b, s[0], s[2])
                    for kind, i, o in [] if tail else planned(u, first, last, THIRD_JOB):
                        if kind == "qk":
                            third_part(b + o, i)

                over_batches(pool, body)

            @block.tensor
            def _(pe):
                def product(kind, i, c, bank=job_ps):
                    if kind == "in":
                        src, k = (xn_b, i - 2) if i >= 2 else (ctx_b, i)
                        if i == 2:
                            pe.wait_ge(S["xn_ready"], c + 1)
                        if i == 0:
                            pe.wait_ge(S["ctx_in"], (c + 1) * 16)
                        for q in range(TOK_TILES):
                            mm = pe.transpose(bank[:, q * P:(q + 1) * P], src[:, q, k * P:(k + 1) * P], ident[:, :])
                        mm.then_inc(S["in_turned"], 1)
                    elif kind == "qk":
                        w, src, f = (wq, xnT, i // 2) if i % 2 else (wk, ctxT, i // 2)
                        for k in range(DK):
                            mm = pe.matmul(bank[:, :], w[:, k, f * P:(f + 1) * P], src[:, k, :], start=k == 0, stop=k == DK - 1)
                        mm.then_inc(S["qk_mm"], 1)
                    elif kind == "v":
                        for t in range(2):
                            for k in range(DK):
                                mm = pe.matmul(bank[:, t * DIM:(t + 1) * DIM], ctxT[:, k, (2 * i + t) * P:(2 * i + t + 1) * P],
                                               wv[:, k, :], start=k == 0, stop=k == DK - 1)
                        mm.then_inc(S["v_mm"], 1)
                    elif kind == "turn_o":
                        pe.wait_ge(S["on_ready"], c + 1)
                        for q in range(TOK_TILES):
                            mm = pe.transpose(bank[:, q * P:(q + 1) * P], o_norm[:, q, 8 * i:8 * (i + 1), :].rearrange("p h d -> p (h d)"), ident[:, :])
                        mm.then_inc(S["on_turned"], 1)
                    else:
                        for t in range(2):
                            q = 2 * i + t
                            for k in range(DK):
                                mm = pe.matmul(bank[:, t * DIM:(t + 1) * DIM], oT[:, k, q * P:(q + 1) * P], wo[:, k, :], start=k == 0, stop=k == DK - 1)
                        mm.then_inc(S["wo_mm"], 1)

                pe.wait_ge(T["ident_ready"], T["ident_count"])
                for n, (kind, i) in enumerate(START):
                    if kind == "qk":
                        pe.wait_ge(S["in_copied"], 2 * i + 2)
                    if (kind, i) == ("qk", 0):
                        pe.wait_ge(S["w_in"], 32)
                    product(kind, i, 0, START_BANKS[n])

                def scores(b, u):
                    h, q = head(u), u % TOK_TILES
                    if h % 4 == 0 and q == 0:
                        pe.wait_ge(pack_in[h // 4], (b + 1) * 192)
                    for m in range(MAPS):
                        n = u * MAPS + m
                        if not (isinstance(b, int) and b == 0 and n < 4):
                            pe.wait_ge(S["masked"], b * UNITS * MAPS + n - 3)
                        hm = h * MAPS + m
                        pe.matmul(score_ps[n % 4][:, :], q_packed[:, hm, q * P:(q + 1) * P], k_packed[:, hm, :], start=True, stop=True).then_inc(S["scores"], 1)

                def turn(b, h, k, w):
                    if k == 0:
                        pe.wait_ge(S["combined"], (b * HEADS + w // TOK_TILES + 1) * HALF)
                        pe.wait_ge(S["combined_pool"], (b * HEADS + w // TOK_TILES + 1) * HALF)
                    if not (isinstance(b, int) and b == 0 and w < 2):
                        pe.wait_ge(S["attnT_ready"], b * UNITS + w - 1)
                    for q in range(TOK_TILES):
                        mm = pe.transpose(turn_ps[w % 2][:, q * P:(q + 1) * P], attn[:, h % 2, q, k * P:(k + 1) * P], ident[:, :])
                    mm.then_inc(S["turned"], 1)

                def values(b, h, w):
                    pe.wait_ge(S["attnT_ready"], b * UNITS + w + TOK_TILES)
                    if h == 0:
                        pe.wait_ge(S["v_copied"], b * 2 + w // UNITS * 2 + 2)
                    if not (isinstance(b, int) and b == 0 and w == 0):
                        pe.wait_ge(S["gathered"], b * HEADS + w // TOK_TILES)
                    for k in range(TOK_TILES):
                        mm = pe.matmul(value_ps[32 * k:32 * (k + 1), :], v[:, k, h * DH:h * DH + 32], attnT[:, place(h, k), :], start=True, stop=True)
                    mm.then_inc(S["values"], 1)

                def turn_out(b, w):
                    pe.wait_ge(S["value_copied"], b * HEADS + w // TOK_TILES + 1)
                    for q in range(TOK_TILES):
                        mm = pe.transpose(value_ps[:, q * P:(q + 1) * P], value_part[:, q * P:(q + 1) * P], ident[:, :])
                    mm.then_inc(S["out_turned"], 1)

                pe.wait_ge(S["zero_ready"], 1)

                def body(b, u, first, last, tail):
                    if not tail:
                        scores(b, u)
                    if (s := stage(u, VALUES, first, tail)) and s[1] == 0:
                        values(b, s[0], s[2])
                    if (s := stage(u, TURN, first, tail)):
                        turn(b, *s)
                    if (s := stage(u, TURN_OUT, first, tail)) and s[1] == 0:
                        turn_out(b, s[2])
                    for kind, i, o in planned(u, first, last) if not tail else []:
                        order = [p[1:] for p in plan(first, last)]
                        n = order.index((kind, i, o))
                        if n or not first:
                            before = order[n - 1] if n else ("qk", 5, 0)
                            pe.wait_ge(*released(*before[:2], b + before[2]))
                        product(kind, i, b + o)
                    if tail:
                        for at, kind, i, _ in PLAN:
                            if kind in ("turn_o", "out") and at + UNITS == u:
                                if (kind, i) == ("turn_o", 0):
                                    pe.wait_ge(*released("v", 1, b))
                                else:
                                    pe.wait_ge(*released(*{("turn_o", 1): ("turn_o", 0), ("out", 0): ("turn_o", 1), ("out", 1): ("out", 0)}[kind, i], b))
                                if (kind, i) == ("out", 0):
                                    pe.wait_ge(S["oT_ready"], b * 2 + 2)
                                product(kind, i, b)

                pe.wait_ge(S["rest_in"], 48)
                over_batches(pe, body)

            @block.scalar
            def _(act):
                def copy_product(kind, i, c, bank=job_ps):
                    if kind == "in":
                        act.wait_ge(S["in_turned"], c * 4 + i + 1)
                        act.copy((xnT if i >= 2 else ctxT)[:, i % 2, :], bank[:, :]).then_inc(S["in_copied"], 1)
                    elif kind == "qk":
                        act.wait_ge(S["qk_mm"], c * 8 + i + 1)
                        if not (isinstance(c, int) and c == 0 and i < 2):
                            act.wait_ge(S[f"parts_written{i % 2}"], (c * 4 + i // 2) * 16)
                        act.activation(part[:, i % 2, 0, :], bank[:, :], ACT.Copy, scale=SCALE if i % 2 else 1.0).then_inc(S["part1"], 1)
                    elif kind == "v":
                        act.wait_ge(S["v_mm"], c * 2 + i + 1)
                        act.copy(v[:, 2 * i:2 * i + 2, 0:DIM], bank[:, :].rearrange("p (t n) -> p t n", n=DIM)).then_inc(S["v_copied"], 1)
                    elif kind == "turn_o":
                        act.wait_ge(S["on_turned"], c * 2 + i + 1)
                        act.activation(oT[:, i, :], bank[:, :], ACT.Copy, scale=rms_col[:, 1:2]).then_inc(S["oT_ready"], 1)

                def root(batches):
                    act.activation(rstd[:, 0, batches], moments[:, batches, 1], ACT.Sqrt, bias=T["eps"][:, :]).then_inc(S["act_setup"], 1)

                act.wait_ge(S["dve_setup"], 1)
                root(slice(0, TOK_TILES))
                for n, (kind, i) in enumerate(START):
                    copy_product(kind, i, 0, START_BANKS[n])
                act.wait_ge(S["dve_setup"], 2)
                root(slice(TOK_TILES, ALL_TILES))
                act.wait_ge(S["dve_setup"], 3)
                act.activation(small[:, 1, 0:2 * HEADS], small[:, 0, 0:2 * HEADS], ACT.Exp).then_inc(S["act_setup"], 1)
                act.wait_ge(S["dve_setup"], 4)

                def exps(b, u):
                    h, q = head(u), u % TOK_TILES
                    for m in range(MAPS):
                        act.wait_ge(S["masked"], (b * UNITS + u) * MAPS + m + 1)
                        tile = prob[:, h % 2, q, m, :]
                        act.activation(tile, tile, ACT.Exp, bias=neg_max[:, h % 2, q, m:m + 1], scale=-1.0,
                                       accum_out=row_sum[:, h % 2, m, q:q + 1]).then_inc(S["exp"], 1)

                def copy_turned(b, h, k, w):
                    if k == 2 and not (isinstance(b, int) and b == 0 and w < TOK_TILES):
                        act.wait_ge(S["values"], b * HEADS + w // TOK_TILES)
                    act.wait_ge(S["turned"], b * UNITS + w + 1)
                    act.copy(attnT[:, place(h, k), :], turn_ps[w % 2][:, :]).then_inc(S["attnT_ready"], 1)

                def body(b, u, first, last, tail):
                    if (s := stage(u, COPY, first, tail)):
                        copy_turned(b, *s)
                    for kind, i, o in [] if tail else planned(u, first, last, COPY_JOB):
                        copy_product(kind, i, b + o)
                    if not tail:
                        exps(b, u)
                    if u % UNITS == OUT_ROOT and not first and (tail or not u >= UNITS):
                        c = b if tail else b - 1
                        act.wait_ge(S["ms_ready"], c + 1)
                        act.activation(small[:, 2, :], small[:, 1, :], ACT.Sqrt, bias=T["eps"][:, :], scale=1.0 / DH).then_inc(S["rms_ready"], 1)
                    if tail:
                        for at, kind, i, _ in PLAN:
                            if kind == "turn_o" and at + COPY_JOB + UNITS == u:
                                copy_product(kind, i, b)

                over_batches(act, body)

            @block.vector
            def _(dve):
                own = Steps(dve, S["dve_own"])

                def statistics(batches):
                    for t in batches:
                        s = dve.bn_stats(stats[:, t, :], x_res[:, t, :])
                    own.done(s)
                    own.wait()
                    for t in batches:
                        s = dve.bn_aggr(moments[:, t, :], stats[:, t, :])
                    s.then_inc(S["dve_setup"], 1)

                def invert_deviation(tiles, at):
                    dve.wait_ge(S["act_setup"], at)
                    own.done(dve.reciprocal(rstd[:, 1, tiles], rstd[:, 0, tiles]))
                    own.wait()

                dve.wait_ge(S["x_in"], 16)
                statistics(range(TOK_TILES))
                invert_deviation(slice(0, TOK_TILES), 1)
                xv = x_res[:, :, :].rearrange("p (b q) d -> p b (q d)", b=BATCH)

                def normalise_x(c):
                    mom = moments[:, :, :].rearrange("p (b q) c -> p b (q c)", b=BATCH)
                    rs = rstd[:, 1, :].rearrange("p (b q) -> p b q", b=BATCH)
                    own.done(dve.tensor_copy(norm_now[:, 0:8], flat(mom[:, one(c), :])))
                    own.done(dve.tensor_copy(norm_now[:, 8:12], flat(rs[:, one(c), :])))
                    own.wait()
                    for q in range(TOK_TILES):
                        s = dve.tensor_scalar(xn_b[:, q, :], flat(xv[:, one(c), q * DIM:(q + 1) * DIM]),
                                              norm_now[:, 2 * q:2 * q + 1], norm_now[:, 8 + q:9 + q], ALU.subtract, ALU.mult)
                    s.then_inc(S["xn_ready"], 1)

                def split(i, c, bank=job_ps):
                    dve.wait_ge(S["part1"], c * 8 + i + 1)
                    if not (isinstance(c, int) and c == 0 and i < 1):
                        dve.wait_ge(S["part3"], c * 8 + i)
                    dve.scalar_tensor_tensor(out=rest[:, :], in0=bank[:, :], scalar=SCALE if i % 2 else 1.0,
                                             in1=part[:, i % 2, 0, :], op0=ALU.mult, op1=ALU.subtract).then_inc(S["rest_ready"], 1)

                normalise_x(0)
                for n, (kind, i) in enumerate(START):
                    if kind == "qk":
                        split(i, 0, START_BANKS[n])
                dve.wait_ge(S["rest_in"], 48)
                statistics(range(TOK_TILES, ALL_TILES))
                dve.wait_ge(S["small_in"], (4 + P // DH) * 16)
                for i in range(2):
                    own.done(dve.tensor_tensor(lam_in[:, 2 * i, :], lam_in[:, 2 * i, :], lam_in[:, 2 * i + 1, :], ALU.mult))
                own.wait()
                for i in range(2):
                    s = dve.tensor_reduce(small[:, 0, i * HEADS:(i + 1) * HEADS], lam_in[:, 2 * i, :].rearrange("p (h d) -> p h d", d=DH), AX.X, ALU.add)
                s.then_inc(S["dve_setup"], 1)
                dve.tensor_scalar(rms_col[:, 1:2], rms_col[:, 0:1], 1.0 - LAMBDA_INIT, None, ALU.mult).then_inc(S["dve_setup"], 1)
                invert_deviation(slice(TOK_TILES, ALL_TILES), 2)
                dve.wait_ge(S["act_setup"], 3)
                own.done(dve.scalar_tensor_tensor(out=neg_lam[:, :], in0=small[:, 1, HEADS:2 * HEADS], scalar=-LAMBDA_INIT, in1=small[:, 1, 0:HEADS],
                                                  op0=ALU.add, op1=ALU.subtract))
                own.wait()

                def ready(b, u):
                    h = head(u)
                    if u % TOK_TILES == 0:
                        dve.wait_ge(S[f"mask_in{h % 2}"], (b * (HEADS // 2) + h // 2 + 1) * 16)
                    if not (isinstance(b, int) and b == 0 and u < 2 * TOK_TILES):
                        done = S["combined_pool" if u % TOK_TILES >= HALF else "combined"]
                        dve.wait_ge(done, (b * HEADS + u // TOK_TILES - 2) * HALF + u % HALF + 1)
                    dve.wait_ge(S["scores"], (b * UNITS + u + 1) * MAPS)

                def add_mask(u, m):
                    h, q = head(u), u % TOK_TILES
                    dve.tensor_tensor_reduce(prob[:, h % 2, q, m, :], score_ps[(u * MAPS + m) % 4][:, :], mask[:, h % 2, q, :], -1.0, 3.0e38,
                                             ALU.add, ALU.min, neg_max[:, h % 2, q, m:m + 1]).then_inc(S["masked"], 1)

                def invert_sums(h):
                    own.done(dve.reciprocal(row_inv[:, h, :, :], row_sum[:, h % 2, :, :]))

                def coefficients(h):
                    own.wait()
                    dve.scalar_tensor_tensor(out=coef[:, h % 2, :], in0=row_sum[:, h % 2, 0, :], scalar=neg_lam[:, h:h + 1],
                                             in1=row_inv[:, h, 1, :], op0=ALU.mult, op1=ALU.mult).then_inc(S["coef_ready"], 1)

                def combine(b, h, q, w):
                    if q == 0:
                        dve.wait_ge(S["coef_ready"], b * HEADS + w // TOK_TILES + 1)
                    if q == 0 and not (isinstance(b, int) and b == 0 and w < 2 * TOK_TILES):
                        dve.wait_ge(S["turned"], b * UNITS + w - TOK_TILES)
                    dve.scalar_tensor_tensor(out=attn[:, h % 2, q, :], in0=prob[:, h % 2, q, 1, :], scalar=coef[:, h % 2, q:q + 1],
                                             in1=prob[:, h % 2, q, 0, :], op0=ALU.mult, op1=ALU.add).then_inc(S["combined"], 1)

                def copy_values(b, w):
                    dve.wait_ge(S["values"], b * HEADS + w // TOK_TILES + 1)
                    dve.tensor_copy(value_part[:, :], value_ps[:, :]).then_inc(S["value_copied"], 1)

                def gather(b, w):
                    own.wait()
                    dve.wait_ge(S["out_turned"], b * HEADS + w // TOK_TILES + 1)
                    dve.tensor_reduce(o_sum[:, :, :], value_ps[:, :].rearrange("p (q g d) -> p q d g", q=TOK_TILES, g=4)[:, :, 0:DH, :],
                                      AX.X, ALU.add).then_inc(S["gathered"], 1)

                def scale_gathered(b, h, w):
                    dve.wait_ge(S["gathered"], b * HEADS + w // TOK_TILES + 1)
                    own.done(dve.tensor_tensor(o_heads[:, h, :, :], o_sum[:, :, :],
                                               row_inv[:, h, 0, :].rearrange("p (q a) -> p q a", a=1).broadcast_to([P, TOK_TILES, DH]), ALU.mult))

                oh = o_heads[:, :, :, :].rearrange("p h q d -> p (h q) d")

                def squares():
                    own.wait()
                    own.done(dve.tensor_tensor(o_norm[:, :, :, :].rearrange("p q h d -> p (q h) d"), oh, oh, ALU.mult))
                    own.wait()
                    dve.tensor_reduce(small[:, 1, :], o_norm[:, :, :, :].rearrange("p q h d -> p (q h) d"), AX.X, ALU.add).then_inc(S["ms_ready"], 1)

                def rms_norm(c):
                    dve.wait_ge(S["rms_ready"], c + 1)
                    own.done(dve.reciprocal(small[:, 0, :], small[:, 2, :]))
                    own.wait()
                    dve.tensor_tensor(o_norm[:, :, :, :].rearrange("p q h d -> p h q d"), o_heads[:, :, :, :],
                                      small[:, 0, :].rearrange("p (h q a) -> p h q a", q=TOK_TILES, a=1).broadcast_to([P, HEADS, TOK_TILES, DH]),
                                      ALU.mult).then_inc(S["on_ready"], 1)

                def add_out(i, c):
                    dve.wait_ge(S["wo_mm"], c * 2 + i + 1)
                    xq = flat(xv[:, one(c), i * 2 * DIM:(i + 1) * 2 * DIM])
                    dve.tensor_tensor(xq, job_ps[:, :], xq, ALU.add).then_inc(S["x_added"], 1)

                def body(b, u, first, last, tail):
                    mixed, sums, copied, out = (stage(u, lag, first, tail) for lag in (COMBINE, COEF, COPY_VALUES, GATHER))
                    mixed = mixed if mixed and mixed[1] < HALF else None
                    copied = copied if copied and copied[1] == 0 else None
                    sums = sums if sums and sums[1] == 0 else None
                    out = out if out and out[1] == 0 else None
                    if sums:
                        dve.wait_ge(S["exp"], (b * UNITS + sums[2] + TOK_TILES) * MAPS)
                    if not tail:
                        ready(b, u)
                    if mixed:
                        combine(b, *mixed)
                    elif copied:
                        copy_values(b, copied[2])
                    elif sums:
                        invert_sums(sums[0])
                    elif not tail:
                        dve.memset(scratch[:, u:u + 1], 0.0)
                    if not tail:
                        add_mask(u, 0)
                    if sums:
                        coefficients(sums[0])
                    if out:
                        gather(b, out[2])
                    if not tail:
                        add_mask(u, 1)
                    if out:
                        scale_gathered(b, out[0], out[2])
                    if not first and (tail or u < UNITS):
                        c = b if tail else b - 1
                        at = u - UNITS if tail else u
                        if at == OUT_SQUARES:
                            squares()
                        if at == OUT_NORM:
                            rms_norm(c)
                        for when, kind, i, _ in PLAN:
                            if kind == "out" and at == when + 1:
                                add_out(i, c)
                    if not tail:
                        if u == NEXT_XN and not last:
                            if not first:
                                dve.wait_ge(S["on_turned"], b * 2)
                            normalise_x(b + 1)
                        for kind, i, o in planned(u, first, last, SPLIT_JOB):
                            if kind == "qk":
                                split(i, b + o)

                for u in range(UNITS):
                    body(0, u, True, False, False)
                with dve.Fori(1, BATCH - 1) as b:
                    own.loop(b, DVE_A, 1)
                    for u in range(UNITS):
                        body(b, u, False, False, False)
                own.end_loop(BATCH - 2)
                for u in range(UNITS):
                    body(BATCH - 1, u, False, True, False)
                for u in range(UNITS, UNITS + TAIL):
                    body(BATCH - 1, u, False, True, True)
                dve.wait_ge(S["x_added"], BATCH * 2)


DVE_A = HEADS + HEADS + 1 + 1 + 2



EXPERTS = 8
FF = 1024
FF_TILES = FF // P
SLOT_TILES = 24
FETCHED_TILES = SLOT_TILES + 2
W2_AHEAD = 5


def layernorm_all(dve, own, sem_stats, sem_std, std_at, x_res, stats, moments, rstd, out, sem_batch=None):
    for t in range(ALL_TILES):
        s = dve.bn_stats(stats[:, t, :], x_res[:, t, :])
    own.done(s)
    own.wait()
    for t in range(ALL_TILES):
        s = dve.bn_aggr(moments[:, t, :], stats[:, t, :])
    s.then_inc(sem_stats, 1)
    dve.wait_ge(sem_std, std_at)
    own.done(dve.reciprocal(rstd[:, 1, :], rstd[:, 0, :]))
    own.wait()
    for t in range(ALL_TILES):
        s = dve.tensor_scalar(out[:, t, :], x_res[:, t, :], moments[:, t, 0:1], rstd[:, 1, t:t + 1], ALU.subtract, ALU.mult)
        if sem_batch is not None and t % TOK_TILES == TOK_TILES - 1:
            s.then_inc(sem_batch, 1)
    return s


def experts(nc, ctx_outer, T, A):
    with ExitStack() as ctx:
        def sb(name, shape, dt=F32):
            return ctx.enter_context(nc.sbuf_tensor("b_" + name, shape, dt))

        def sem(name):
            return ctx_outer.enter_context(nc.semaphore("b_" + name))

        psum = [ctx.enter_context(nc.psum_tensor(f"b_bank{i}", [P, 512], F32)) for i in range(8)]
        x_res, ident = T["x_res"], T["ident"]
        stats = sb("stats", [P, ALL_TILES, 6])
        moments = sb("moments", [P, ALL_TILES, 2])
        rstd = sb("rstd", [P, 2, ALL_TILES])
        xn = sb("xn", [P, ALL_TILES, DIM])
        router = sb("router", [P, DK, EXPERTS])
        router_b = sb("router_b", [P, EXPERTS])
        logits = sb("logits", [P, ALL_TILES, EXPERTS])
        expd = sb("expd", [P, ALL_TILES, EXPERTS])
        pick = sb("pick", [P, ALL_TILES, EXPERTS])
        onehot = sb("onehot", [P, ALL_TILES, EXPERTS])
        onehot_b = sb("onehot_b", [P, ALL_TILES, EXPERTS], BF16)
        col = sb("col", [P, 6, ALL_TILES])
        first_w = sb("first_w", [P, EXPERTS])
        before = sb("before", [P, P], BF16)
        ones_b = sb("ones_b", [P, P], BF16)
        totals = expd
        cum = sb("cum", [P, 2, ALL_TILES, EXPERTS])
        where = pick
        count_i = sb("count_i", [P, 2, EXPERTS], I32)
        need = sb("need", [P, 4, EXPERTS])
        slot_f = sb("slot_f", [P, ALL_TILES])
        slot, gate = T["slot"], T["gate"]
        tile_no = sb("tile_no", [P, FETCHED_TILES])
        past = sb("past", [P, FETCHED_TILES, EXPERTS])
        owner_f = sb("owner_f", [P, FETCHED_TILES])
        owner = sb("owner", [P, FETCHED_TILES], I32)
        b1_rows = sb("b1_rows", [EXPERTS * FF_TILES, P])
        b1T = sb("b1T", [P, EXPERTS * FF_TILES])
        b2_all = sb("b2_all", [P, EXPERTS, DIM])
        w1_all = sb("w1_all", [P, EXPERTS * DK, FF])
        w2_all = sb("w2_all", [P, EXPERTS * FF_TILES, DIM])
        ctx_all = flat(w2_all[:, EXPERTS * FF_TILES - ALL_TILES:, :]).rearrange("p (t d) -> p t d", d=DIM)
        w1 = sb("w1", [P, 2, DK * FF])
        xnT = w1[:, :, :].rearrange("p r n -> p (r n)").rearrange("p (b k n) -> p b k n", b=BATCH, k=DK)
        x_slots = sb("x_slots", [P, 2, DIM])
        x_slotsT = sb("x_slotsT", [P, 2, DK, P])
        hiddenT = sb("hiddenT", [P, 2, FF_TILES, P])
        b1_t = sb("b1_t", [P, 2, FF_TILES])
        y_slots = sb("y_slots", [P, 2, DIM])
        x_slots_d = T["x_sorted"]
        y_slots_d = T["y_sorted"] = nc.dram_tensor("b_y_sorted", (SLOT_TILES * P, DIM), F32, kind="Internal").ap()

        names = ("w_in b1_in b1_turned b1_ready all_w1_in all_w2_in ctx_in stats_ready std_ready xn_ready turned xnT_ready "
                 "logit_mm shifted exp_done onehot_ready masks_ready count_mm slot_ready owner_ready scattered "
                 "w1_ready0 w1_ready1 xs_in0 xs_in1 xs_turned xsT_ready b1_picked h_mm0 h_mm1 "
                 "relu_act relu_dve y_mm y_ready y_out0 y_out1 dve_own pool_own iota_done").split()
        S = {n: sem(n) for n in names}
        EB, NTILE = EXPERTS, ALL_TILES

        with nc.Block() as block:
            @block.sync
            def _(sp):
                sp.dma_start(router[:, :, :], A["L0_ffn_router_W"].rearrange("(k p) e -> p k e", p=P)).then_inc(S["w_in"], 16)
                sp.dma_start(router_b[:, :], A["L0_ffn_router_b"].rearrange("(a e) -> a e", a=1).broadcast_to([P, EXPERTS])).then_inc(S["w_in"], 16)
                sp.dma_start(b1_rows[:, :], A["L0_ffn_b1"].rearrange("e (f p) -> (e f) p", p=P)).then_inc(S["b1_in"], 16)
                sp.dma_start(b2_all[:, :, :], A["L0_ffn_b2"].rearrange("(a e) d -> a e d", a=1).broadcast_to([P, EXPERTS, DIM])).then_inc(S["b1_in"], 16)
                sp.dma_start(ctx_all, A["ctx_1024"].rearrange("b (q p) d -> p (b q) d", p=P)).then_inc(S["ctx_in"], 16)

                def load_w2(e):
                    sp.dma_start(w2_all[:, e * FF_TILES:(e + 1) * FF_TILES, :], A["L0_ffn_W2"][e].rearrange("(k p) d -> p k d", p=P)).then_inc(S["all_w2_in"], 16)

                for e in range(EXPERTS):
                    sp.dma_start(w1_all[:, e * DK:(e + 1) * DK, :], A["L0_ffn_W1"][e].rearrange("(k p) f -> p k f", p=P)).then_inc(S["all_w1_in"], 16)
                for e in range(W2_AHEAD):
                    load_w2(e)
                sorted_x = x_slots_d.rearrange("(i r p) d -> i r p d", r=2, p=P)
                sp.wait_ge(S["scattered"], 16 * ALL_TILES)
                for r in range(2):
                    sp.dma_start(x_slots[:, r, :], sorted_x[0, r]).then_inc(S[f"xs_in{r}"], 16)
                sp.wait_ge(S["stats_ready"], 2)
                for e in range(W2_AHEAD, EXPERTS):
                    load_w2(e)
                with sp.Fori(0, SLOT_TILES // 2) as i:
                    for r in range(2):
                        sp.wait_ge(S["xs_turned"], 2 * i + r + 1)
                        sp.dma_start(x_slots[:, r, :], sorted_x[bass.ds(i + 1, 1), r].rearrange("a p d -> p (a d)")).then_inc(S[f"xs_in{r}"], 16)

            @block.gpsimd
            def _(pool):
                own = Steps(pool, S["pool_own"])
                for r in range(2):
                    pool.memset(y_slots[:, r, :], 0.0).then_inc(S[f"y_out{r}"], 16)
                pool.memset(ones_b[:, :], 1.0)
                own.done(pool.memset(before[:, :], 1.0))
                own.wait()
                pool.affine_select(out=before[:, :], in_=before[:, :], compare_op=ALU.is_gt, fill=0.0, base=0,
                                   pattern=[[1, P]], channel_multiplier=-1).then_inc(S["masks_ready"], 1)
                pool.iota(first_w[:, :], pattern=[[-1, EXPERTS]], base=EXPERTS, channel_multiplier=0,
                          allow_small_or_imprecise_dtypes=True).then_inc(S["iota_done"], 1)
                pool.iota(tile_no[:, :], pattern=[[1, FETCHED_TILES]], base=0, channel_multiplier=0,
                          allow_small_or_imprecise_dtypes=True).then_inc(S["iota_done"], 1)
                pool.wait_ge(S["slot_ready"], 1)
                pool.wait_ge(S["xn_ready"], BATCH)
                pool.wait_ge(T["slots_zeroed"], T["zero_count"])
                for t in range(ALL_TILES):
                    pool.indirect_dma_start(x_slots_d, bass.IndirectOffsetOnAxis(slot[:, t:t + 1], 0), xn[:, t, :], None).then_inc(S["scattered"], 16)
                pool.wait_ge(S["y_out0"], 16 * (SLOT_TILES // 2 + 1))
                pool.wait_ge(S["y_out1"], 16 * (SLOT_TILES // 2 + 1))

            @block.tensor
            def _(pe):
                pe.wait_ge(S["w_in"], 32)

                def router_logits(b):
                    pe.wait_ge(S["xnT_ready"], (b + 1) * DK)
                    for q in range(TOK_TILES):
                        for k in range(DK):
                            t = b * TOK_TILES + q
                            mm = pe.matmul(psum[4][:, t * EB:(t + 1) * EB], xnT[:, b, k, q * P:(q + 1) * P], router[:, k, :], start=k == 0, stop=k == DK - 1)
                    return mm

                for b in range(BATCH):
                    pe.wait_ge(S["xn_ready"], b + 1)
                    for k in range(DK):
                        n = b * DK + k
                        if n >= 4:
                            pe.wait_ge(S["xnT_ready"], n - 3)
                        for q in range(TOK_TILES):
                            mm = pe.transpose(psum[n % 4][:, q * P:(q + 1) * P], xn[:, b * TOK_TILES + q, k * P:(k + 1) * P], ident[:, :])
                        mm.then_inc(S["turned"], 1)
                    if b:
                        router_logits(b - 1)
                mm = router_logits(BATCH - 1)
                mm.then_inc(S["logit_mm"], 1)
                pe.wait_ge(S["b1_in"], 32)
                pe.transpose(psum[7][:, 0:EXPERTS * FF_TILES], b1_rows[:, :], ident[0:EXPERTS * FF_TILES, 0:EXPERTS * FF_TILES]).then_inc(S["b1_turned"], 1)
                pe.wait_ge(S["masks_ready"], 1)
                pe.wait_ge(S["onehot_ready"], 1)
                pe.matmul(psum[5][:, 0:NTILE * EB], ones_b[:, :], onehot_b[:, :, :].rearrange("p t e -> p (t e)"), start=True, stop=True).then_inc(S["count_mm"], 1)
                pe.matmul(psum[6][:, 0:NTILE * EB], before[:, :], onehot_b[:, :, :].rearrange("p t e -> p (t e)"), start=True, stop=True).then_inc(S["count_mm"], 1)

                def turn(r, at):
                    pe.wait_ge(S[f"xs_in{r}"], at)
                    for k in range(DK):
                        mm = pe.transpose(psum[r][:, k * P:(k + 1) * P], x_slots[:, r, k * P:(k + 1) * P], ident[:, :])
                    mm.then_inc(S["xs_turned"], 1)

                turn(0, 16)
                turn(1, 16)
                with pe.Fori(0, SLOT_TILES // 2) as i:
                    def hidden(r):
                        pe.wait_ge(S["xsT_ready"], 2 * i + r + 1)
                        pe.wait_ge(S[f"w1_ready{r}"], i + 1)
                        for f in range(FF_TILES):
                            for k in range(DK):
                                mm = pe.matmul(psum[2 + 2 * r + f // 4][:, (f % 4) * P:(f % 4 + 1) * P], w1[:, r, k * FF + f * P:k * FF + (f + 1) * P],
                                               x_slotsT[:, r, k, :], start=k == 0, stop=k == DK - 1)
                        mm.then_inc(S[f"h_mm{r}"], 1)

                    def down(r):
                        pe.wait_ge(S["relu_act"], 2 * i + r + 1)
                        pe.wait_ge(S["relu_dve"], 2 * i + r + 1)
                        pe.wait_ge(S["all_w2_in"], 16 * EXPERTS)
                        for f in range(FF_TILES):
                            mm = pe.matmul(psum[6 + r][:, 0:DIM], hiddenT[:, r, f, :], flat(w2_all[:, bass.ds(experts_now[r] * FF_TILES + f, 1), :]),
                                           start=f == 0, stop=f == FF_TILES - 1)
                        mm.then_inc(S["y_mm"], 1)

                    experts_now = [pe.value_load(owner[0:1, bass.ds(2 * i + r, 1)], min_val=0, max_val=EXPERTS - 1) for r in range(2)]
                    hidden(0)
                    hidden(1)
                    turn(0, (i + 2) * 16)
                    turn(1, (i + 2) * 16)
                    down(0)
                    down(1)

            @block.scalar
            def _(act):
                act.wait_ge(S["stats_ready"], 1)
                act.activation(rstd[:, 0, :], moments[:, :, 1], ACT.Sqrt, bias=T["eps"][:, :]).then_inc(S["std_ready"], 1)
                for n in range(BATCH * DK):
                    act.wait_ge(S["turned"], n + 1)
                    act.copy(xnT[:, n // DK, n % DK, :], psum[n % 4][:, :]).then_inc(S["xnT_ready"], 1)
                act.wait_ge(S["shifted"], 1)
                act.activation(expd[:, :, :], logits[:, :, :], ACT.Exp).then_inc(S["exp_done"], 1)
                act.wait_ge(S["b1_turned"], 1)
                act.copy(b1T[:, :], psum[7][:, 0:EXPERTS * FF_TILES]).then_inc(S["b1_ready"], 1)
                act.wait_ge(S["stats_ready"], 2)
                act.activation(T["rstd"][:, 2, 0, :], T["moments"][:, 2, :, 1], ACT.Sqrt, bias=T["eps"][:, :]).then_inc(S["std_ready"], 1)

                def turned(r, at):
                    act.wait_ge(S["xs_turned"], at)
                    act.copy(x_slotsT[:, r, :, :].rearrange("p k n -> p (k n)"), psum[r][:, 0:2 * P]).then_inc(S["xsT_ready"], 1)

                turned(0, 1)
                turned(1, 2)
                with act.Fori(0, SLOT_TILES // 2) as i:
                    def relu(r):
                        act.wait_ge(S["b1_picked"], 2 * i + r + 1)
                        act.wait_ge(S[f"h_mm{r}"], i + 1)
                        for f in range(4):
                            s = act.activation(hiddenT[:, r, f, :], psum[2 + 2 * r][:, f * P:(f + 1) * P], ACT.Relu, bias=b1_t[:, r, f:f + 1])
                        s.then_inc(S["relu_act"], 1)

                    relu(0)
                    relu(1)
                    turned(0, 2 * i + 3)
                    turned(1, 2 * i + 4)
                    for r in range(2):
                        act.wait_ge(S["y_ready"], 2 * i + r + 1)
                        act.dma_start(y_slots_d.rearrange("(i r p) d -> i r p d", r=2, p=P)[bass.ds(i, 1), r].rearrange("a p d -> p (a d)"),
                                      y_slots[:, r, :]).then_inc(S[f"y_out{r}"], 16)

            @block.vector
            def _(dve):
                own = Steps(dve, S["dve_own"])

                def do(instruction):
                    own.done(instruction)
                    own.wait()

                layernorm_all(dve, own, S["stats_ready"], S["std_ready"], 1, x_res, stats, moments, rstd, xn, S["xn_ready"])
                wide = lambda ap: ap.rearrange("p (t a) -> p t a", a=1).broadcast_to([P, NTILE, EB])
                every = lambda ap: ap.rearrange("p (a e) -> p a e", a=1).broadcast_to([P, NTILE, EB])
                dve.wait_ge(S["logit_mm"], 1)
                do(dve.tensor_tensor(logits[:, :, :], psum[4][:, 0:NTILE * EB].rearrange("p (t e) -> p t e", e=EB), every(router_b[:, :]), ALU.add))
                do(dve.tensor_reduce(col[:, 0, :], logits[:, :, :], AX.X, ALU.max))
                dve.tensor_tensor(logits[:, :, :], logits[:, :, :], wide(col[:, 0, :]), ALU.subtract).then_inc(S["shifted"], 1)
                dve.wait_ge(S["exp_done"], 1)
                dve.wait_ge(S["iota_done"], 2)
                dve.tensor_reduce(col[:, 1, :], expd[:, :, :], AX.X, ALU.add)
                do(dve.tensor_reduce(col[:, 2, :], expd[:, :, :], AX.X, ALU.max))
                dve.reciprocal(col[:, 3, :], col[:, 1, :])
                do(dve.tensor_tensor(pick[:, :, :], expd[:, :, :], wide(col[:, 2, :]), ALU.is_ge))
                dve.tensor_tensor(gate[:, :], col[:, 2, :], col[:, 3, :], ALU.mult)
                do(dve.tensor_tensor(pick[:, :, :], pick[:, :, :], every(first_w[:, :]), ALU.mult))
                do(dve.tensor_reduce(col[:, 4, :], pick[:, :, :], AX.X, ALU.max))
                do(dve.tensor_tensor(onehot[:, :, :], pick[:, :, :], wide(col[:, 4, :]), ALU.is_equal))
                dve.tensor_copy(onehot_b[:, :, :], onehot[:, :, :]).then_inc(S["onehot_ready"], 1)
                dve.wait_ge(S["count_mm"], 1)
                flat_ps = psum[5][:, 0:NTILE * EB].rearrange("p (t e) -> p t e", e=EB)
                dve.tensor_copy(totals[:, :, :], flat_ps)
                do(dve.tensor_copy(cum[:, 0, :, :], flat_ps))
                at, step = 0, 1
                while step < NTILE:
                    dve.tensor_copy(cum[:, 1 - at, 0:step, :], cum[:, at, 0:step, :])
                    do(dve.tensor_tensor(cum[:, 1 - at, step:, :], cum[:, at, step:, :], cum[:, at, 0:NTILE - step, :], ALU.add))
                    at, step = 1 - at, 2 * step
                do(dve.tensor_scalar(count_i[:, 0, :], cum[:, at, NTILE - 1, :], float(P - 1), None, ALU.add))
                do(dve.tensor_scalar(count_i[:, 1, :], count_i[:, 0, :], P.bit_length() - 1, None, ALU.arith_shift_right))
                dve.tensor_copy(need[:, 0, :], count_i[:, 1, :])
                do(dve.tensor_copy(need[:, 1, :], count_i[:, 1, :]))
                here, step = 1, 1
                while step < EB:
                    dve.tensor_copy(need[:, 3 - here, 0:step], need[:, here, 0:step])
                    do(dve.tensor_tensor(need[:, 3 - here, step:], need[:, here, step:], need[:, here, 0:EB - step], ALU.add))
                    here, step = 3 - here, 2 * step
                ends = need[:, here, :].rearrange("p (a e) -> p a e", a=1).broadcast_to([P, FETCHED_TILES, EB])
                do(dve.tensor_tensor(past[:, :, :], tile_no[:, :].rearrange("p (t a) -> p t a", a=1).broadcast_to([P, FETCHED_TILES, EB]), ends, ALU.is_ge))
                do(dve.tensor_reduce(owner_f[:, :], past[:, :, :], AX.X, ALU.add))
                dve.tensor_scalar(owner[:, :], owner_f[:, :], float(EB - 1), None, ALU.min).then_inc(S["owner_ready"], 1)
                do(dve.tensor_tensor(need[:, 3, :], need[:, here, :], need[:, 0, :], ALU.subtract))
                do(dve.tensor_scalar(need[:, 3, :], need[:, 3, :], float(P), None, ALU.mult))
                do(dve.tensor_tensor(where[:, :, :], cum[:, at, :, :], totals[:, :, :], ALU.subtract))
                dve.wait_ge(S["count_mm"], 2)
                do(dve.tensor_tensor(where[:, :, :], where[:, :, :], psum[6][:, 0:NTILE * EB].rearrange("p (t e) -> p t e", e=EB), ALU.add))
                do(dve.tensor_tensor(where[:, :, :], where[:, :, :], every(need[:, 3, :]), ALU.add))
                do(dve.tensor_tensor(where[:, :, :], where[:, :, :], onehot[:, :, :], ALU.mult))
                do(dve.tensor_reduce(slot_f[:, :], where[:, :, :], AX.X, ALU.add))
                dve.tensor_copy(slot[:, :], slot_f[:, :]).then_inc(S["slot_ready"], 1)
                dve.wait_ge(S["ctx_in"], 16)
                for t in range(ALL_TILES):
                    s = dve.bn_stats(stats[:, t, :], ctx_all[:, t, :])
                do(s)
                for t in range(ALL_TILES):
                    s = dve.bn_aggr(T["moments"][:, 2, t, :], stats[:, t, :])
                s.then_inc(S["stats_ready"], 1)
                dve.wait_ge(S["b1_ready"], 1)
                dve.wait_ge(S["owner_ready"], 1)
                dve.wait_ge(S["all_w1_in"], 16 * EXPERTS)

                def load_owner(tile):
                    return dve.value_load(owner[0:1, tile], min_val=0, max_val=EXPERTS - 1)

                def place_w1(r, e):
                    dve.tensor_copy(w1[:, r, :], w1_all[:, bass.ds(e * DK, DK), :].rearrange("p k n -> p (k n)")).then_inc(S[f"w1_ready{r}"], 1)

                def pick_b1(r, e):
                    dve.tensor_copy(b1_t[:, r, :], b1T[:, bass.ds(e * FF_TILES, FF_TILES)]).then_inc(S["b1_picked"], 1)

                for r in range(2):
                    e = load_owner(slice(r, r + 1))
                    place_w1(r, e)
                    pick_b1(r, e)
                dve.wait_ge(S["std_ready"], 2)
                dve.reciprocal(T["rstd"][:, 2, 1, :], T["rstd"][:, 2, 0, :])
                with dve.Fori(0, SLOT_TILES // 2) as i:
                    now = [load_owner(bass.ds(2 * i + r, 1)) for r in range(2)]
                    for r in range(2):
                        dve.wait_ge(S["b1_picked"], 2 * i + r + 1)
                        dve.wait_ge(S[f"h_mm{r}"], i + 1)
                        for f in range(4, 8):
                            s = dve.tensor_scalar(hiddenT[:, r, f, :], psum[3 + 2 * r][:, (f - 4) * P:(f - 3) * P], b1_t[:, r, f:f + 1], 0.0, ALU.add, ALU.max)
                        s.then_inc(S["relu_dve"], 1)
                        following = load_owner(bass.ds(2 * i + 2 + r, 1))
                        place_w1(r, following)
                        dve.wait_ge(S["relu_act"], 2 * i + r + 1)
                        dve.wait_ge(S["relu_dve"], 2 * i + r + 1)
                        pick_b1(r, following)
                    for r in range(2):
                        dve.wait_ge(S[f"y_out{r}"], (i + 1) * 16)
                        dve.wait_ge(S["y_mm"], 2 * i + r + 1)
                        dve.tensor_tensor(y_slots[:, r, :], psum[6 + r][:, 0:DIM], flat(b2_all[:, bass.ds(now[r], 1), :]), ALU.add).then_inc(S["y_ready"], 1)


HD = 64
INNER = HEADS * HD
PAIRS = HEADS // 2
CLIP = 11.0


def cross_attention(nc, ctx_outer, T, A):
    with ExitStack() as ctx:
        def sb(name, shape, dt=F32):
            return ctx.enter_context(nc.sbuf_tensor("c_" + name, shape, dt))

        def sem(name):
            return ctx_outer.enter_context(nc.semaphore("c_" + name))

        score_ps = ctx.enter_context(nc.psum_tensor("c_scores", [P, 4, 512], F32))
        value_ps = ctx.enter_context(nc.psum_tensor("c_values", [P, 2, 512], F32))
        sum_ps = ctx.enter_context(nc.psum_tensor("c_sums", [P, 2, 512], F32))
        x_res, ident = T["x_res"], T["ident"]
        SCALE = HD ** -0.5
        LOW, HIGH = float(np.exp(-CLIP)), float(np.exp(CLIP))

        wq = sb("wq", [P, DK, INNER])
        wkv = sb("wkv", [P, DK, 2 * INNER])
        wo = sb("wo", [P, PAIRS, DIM])
        bo = sb("bo", [P, DIM])
        ln_col = sb("ln_col", [P, 4, DK])
        z1 = sb("z1", [P, ALL_TILES, DIM])
        stats = sb("stats", [P, ALL_TILES, 6])
        moments, rstd = T["moments"], T["rstd"]
        now = sb("now", [P, 2, 12])
        lat_b = sb("lat_b", [P, TOK_TILES, DIM])
        ctx_raw = sb("ctx_raw", [P, TOK_TILES, DIM])
        latT = sb("latT", [P, DK, SEQ])
        ctxT = sb("ctxT", [P, DK, SEQ])
        q_half = sb("q_half", [P, HEADS, SEQ])
        kT = sb("kT", [P, PAIRS, SEQ])
        v = sb("v", [P, TOK_TILES, INNER])
        prob = sb("prob", [P, 2, TOK_TILES, 2, SEQ])
        y_tok = prob[:, 0, :, :, :].rearrange("p k m n -> p (k m n)").rearrange("p (t d) -> p t d", d=DIM)
        key_sum = sb("key_sum", [P, 2, 2, SEQ])
        rinv = key_sum
        oT = sb("oT", [P, PAIRS, SEQ])
        recip = sb("recip", [P, SEQ])
        ones = sb("ones", [P, HD])

        names = ("w_in wkv_in ln_in bo_in stats_ready std_ready half_zero ones_ready ctx_in lat_ready ctx_ready "
                 "pro_mm pro_act pro_dve scores exp clipped summed values sums normed wo_mm dve_own pool_own").split()
        S = {n: sem(n) for n in names}

        gathered = [sem(f"gathered{g}") for g in range(BATCH)]
        EARLY_JOBS = [("ctx", 0, "a"), ("ctx", 1, "a")] + [("k", f, "a") for f in range(PAIRS)]
        JOBS = EARLY_JOBS + [("v", f, "a") for f in range(8)] + [("lat", 0, "d"), ("lat", 1, "d")] + [("q", f, "ad") for f in range(PAIRS)]
        JOB_AT = {(kind, f): j for j, (kind, f, _) in enumerate(JOBS)}

        def copied(engine, upto):
            return sum(engine in e for _, _, e in JOBS[:upto])

        ACT_JOBS, DVE_JOBS, N_JOBS = copied("a", len(JOBS)), copied("d", len(JOBS)), len(JOBS)
        STEPS = PAIRS * TOK_TILES
        NORMED = PAIRS + 2

        def one(b):
            return bass.ds(b, 1)

        def over_batches(eng, body):
            body(0, True, False)
            with eng.Fori(1, BATCH - 1) as b:
                body(b, False, False)
            body(BATCH - 1, False, True)

        with nc.Block() as block:
            @block.sync
            def _(sp):
                def load_ctx(b):
                    sp.dma_start(ctx_raw[:, :, :], A["ctx_1024"][one(b)].rearrange("a (q p) d -> p (a q) d", p=P)).then_inc(S["ctx_in"], 16)

                load_ctx(0)
                for i, n in enumerate(("ln_l_w", "ln_l_b", "ln_c_w", "ln_c_b")):
                    for k in range(DK):
                        sp.dma_start(ln_col[:, i, k:k + 1], A["L1_xattn_" + n][k * P:(k + 1) * P].rearrange("(p a) -> p a", a=1)).then_inc(S["ln_in"], 16)
                sp.dma_start(wkv[:, :, :], A["L1_xattn_Wkv"].rearrange("(k p) n -> p k n", p=P)).then_inc(S["wkv_in"], 16)
                sp.dma_start(bo[:, :], A["L1_xattn_bo"].rearrange("(a n) -> a n", a=1).broadcast_to([P, DIM])).then_inc(S["bo_in"], 16)
                sp.wait_ge(gathered[BATCH - 1], 16 * TOK_TILES)
                sp.dma_start(wq[:, :, :], A["L1_xattn_Wq"].rearrange("(k p) n -> p k n", p=P)).then_inc(S["w_in"], 16)
                sp.dma_start(wo[:, :, :], A["L1_xattn_Wo"].rearrange("(k p) n -> p k n", p=P)).then_inc(S["w_in"], 16)

                def body(b, first, last):
                    if not last:
                        sp.wait_ge(S["pro_mm"], b * N_JOBS + DK)
                        load_ctx(b + 1)

                over_batches(sp, body)

            @block.gpsimd
            def _(pool):
                own = Steps(pool, S["pool_own"])
                pool.memset(ones[:, :], 1.0).then_inc(S["ones_ready"], 1)
                for t in range(ALL_TILES):
                    pool.indirect_dma_start(y_tok[:, t, :], None, T["y_sorted"], bass.IndirectOffsetOnAxis(T["slot"][:, t:t + 1], 0)
                                            ).then_inc(gathered[t // TOK_TILES], 16)
                pool.memset(q_half[:, :, :], 0.0).then_inc(S["half_zero"], 1)

                def body(b, first, last):
                    for p in range(PAIRS):
                        acc = key_sum[:, p % 2, :, :]
                        for k in range(1, TOK_TILES):
                            if k > 1:
                                own.wait()
                            elif not (first and p < 2):
                                pool.wait_ge(S["sums"], b * PAIRS + p - 1)
                            pool.wait_ge(S["clipped"], b * STEPS + p * TOK_TILES + k + 1)
                            begin = prob[:, p % 2, 0, :, :] if k == 1 else acc
                            s = pool.tensor_tensor(acc, begin, prob[:, p % 2, k, :, :], ALU.add)
                            if k < TOK_TILES - 1:
                                own.done(s)
                        s.then_inc(S["summed"], 1)

                over_batches(pool, own.over_turns(BATCH - 2, PAIRS * 2, body))

            @block.tensor
            def _(pe):
                pe.wait_ge(S["ones_ready"], 1)

                def job(b, first, j):
                    kind, f, _ = JOBS[j]
                    bank = score_ps[:, j % 4, :]
                    upto = max(j - 3, {"ctx": 0, "k": 2, "v": 2, "lat": 0, "q": JOB_AT["lat", 1] + 1}[kind])
                    if upto > 0:
                        for engine, done, total in (("a", S["pro_act"], ACT_JOBS), ("d", S["pro_dve"], DVE_JOBS)):
                            if copied(engine, upto):
                                pe.wait_ge(done, b * total + copied(engine, upto))
                    if j < 4 and not first:
                        pe.wait_ge(S["exp"], b * STEPS)
                    if (kind, f) == ("ctx", 0):
                        pe.wait_ge(S["ctx_ready"], b + 1)
                    if (kind, f) == ("lat", 0):
                        pe.wait_ge(S["lat_ready"], b + 1)
                    if kind in ("lat", "ctx"):
                        src = lat_b if kind == "lat" else ctx_raw
                        for q in range(TOK_TILES):
                            mm = pe.transpose(bank[:, q * P:(q + 1) * P], src[:, q, f * P:(f + 1) * P], ident[:, :])
                    elif kind == "q":
                        for k in range(DK):
                            mm = pe.matmul(bank, wq[:, k, f * P:(f + 1) * P], latT[:, k, :], start=k == 0, stop=k == DK - 1)
                    elif kind == "k":
                        for k in range(DK):
                            mm = pe.matmul(bank, wkv[:, k, f * P:(f + 1) * P], ctxT[:, k, :], start=k == 0, stop=k == DK - 1)
                    else:
                        t, half = f // 2, f % 2
                        for k in range(DK):
                            mm = pe.matmul(bank, ctxT[:, k, t * P:(t + 1) * P], wkv[:, k, INNER + half * 512:INNER + (half + 1) * 512],
                                           start=k == 0, stop=k == DK - 1)
                    mm.then_inc(S["pro_mm"], 1)

                def scores(b, n):
                    p, k = n // TOK_TILES, n % TOK_TILES
                    if n >= 2:
                        pe.wait_ge(S["exp"], b * STEPS + n - 1)
                    for m in range(2):
                        mm = pe.matmul(score_ps[:, 2 * (k % 2) + m, :], kT[:, p, k * P:(k + 1) * P], q_half[:, 2 * p + m, :], start=True, stop=True)
                    mm.then_inc(S["scores"], 1)

                def values(b, first, g, k):
                    pe.wait_ge(S["clipped"], b * STEPS + g * TOK_TILES + k + 1)
                    if k == 0 and not (first and g < 2):
                        pe.wait_ge(S["normed"], b * NORMED + g - 1 if g >= 2 else b * NORMED)
                    for m in range(2):
                        mm = pe.matmul(value_ps[m * HD:(m + 1) * HD, g % 2, :], v[:, k, (2 * g + m) * HD:(2 * g + m + 1) * HD],
                                       prob[:, g % 2, k, m, :], start=k == 0, stop=k == TOK_TILES - 1)
                    mm.then_inc(S["values"], 1)

                for j in range(len(EARLY_JOBS)):
                    if j == DK:
                        pe.wait_ge(S["wkv_in"], 16)
                    job(0, True, j)
                pe.wait_ge(S["w_in"], 32)

                def body(b, first, last):
                    for j in range(len(EARLY_JOBS), N_JOBS):
                        job(b, first, j)
                    pe.wait_ge(S["pro_act"], (b + 1) * ACT_JOBS)
                    pe.wait_ge(S["pro_dve"], (b + 1) * DVE_JOBS)
                    for p in range(PAIRS + 1):
                        for k in range(TOK_TILES):
                            if p < PAIRS:
                                scores(b, p * TOK_TILES + k)
                            if p:
                                values(b, first, p - 1, k)
                        if p:
                            pe.wait_ge(S["summed"], b * PAIRS + p)
                            for m in range(2):
                                mm = pe.matmul(sum_ps[m * HD:(m + 1) * HD, (p - 1) % 2, :], ones[:, :], key_sum[:, (p - 1) % 2, m, :], start=True, stop=True)
                            mm.then_inc(S["sums"], 1)
                    if not last:
                        for j in range(len(EARLY_JOBS)):
                            job(b + 1, False, j)
                    pe.wait_ge(S["normed"], b * NORMED + PAIRS)
                    for q in range(TOK_TILES):
                        for k in range(PAIRS):
                            mm = pe.matmul(value_ps[:, q // 2, (q % 2) * DIM:(q % 2 + 1) * DIM], oT[:, k, q * P:(q + 1) * P], wo[:, k, :],
                                           start=k == 0, stop=k == PAIRS - 1)
                        if q % 2:
                            mm.then_inc(S["wo_mm"], 1)

                over_batches(pe, body)

            @block.scalar
            def _(act):
                def root(i):
                    act.wait_ge(S["stats_ready"], i + 1)
                    act.activation(rstd[:, i, 0, :], moments[:, i, :, 1], ACT.Sqrt, bias=T["eps"][:, :]).then_inc(S["std_ready"], 1)

                act.wait_ge(S["ln_in"], 64 * DK)

                def copy_job(b, j):
                    kind, f, engines = JOBS[j]
                    if "a" not in engines:
                        return
                    if (kind, f) == ("q", 0):
                        act.wait_ge(S["half_zero"], 1)
                    bank = score_ps[:, j % 4, :]
                    act.wait_ge(S["pro_mm"], b * N_JOBS + j + 1)
                    if kind == "ctx":
                        s = act.activation(ctxT[:, f, :], bank, ACT.Identity, scale=ln_col[:, 2, f:f + 1], bias=ln_col[:, 3, f:f + 1])
                    elif kind == "q":
                        s = act.activation(q_half[0:HD, 2 * f, :], bank[0:HD, :], ACT.Copy, scale=SCALE)
                    elif kind == "k":
                        s = act.copy(kT[:, f, :], bank)
                    else:
                        s = act.copy(v[:, f // 2, (f % 2) * 512:(f % 2 + 1) * 512], bank)
                    s.then_inc(S["pro_act"], 1)

                for j in range(len(EARLY_JOBS)):
                    copy_job(0, j)
                root(0)

                def body(b, first, last):
                    for j in range(len(EARLY_JOBS), N_JOBS):
                        copy_job(b, j)
                        if first and (JOBS[j][0], JOBS[j][1]) == ("v", 2):
                            root(1)
                    for p in range(PAIRS):
                        for k in range(TOK_TILES):
                            n = p * TOK_TILES + k
                            if p >= 2:
                                act.wait_ge(S["values"], b * STEPS + n - 2 * TOK_TILES + 1)
                                if k == 0:
                                    act.wait_ge(S["summed"], b * PAIRS + p - 1)
                            act.wait_ge(S["scores"], b * STEPS + n + 1)
                            act.activation(prob[:, p % 2, k, :, :], score_ps[:, 2 * (k % 2):2 * (k % 2) + 2, :], ACT.Exp).then_inc(S["exp"], 1)
                    if not last:
                        for j in range(len(EARLY_JOBS)):
                            copy_job(b + 1, j)

                over_batches(act, body)

            @block.vector
            def _(dve):
                own = Steps(dve, S["dve_own"])

                def stats_of(i, src):
                    for t in range(ALL_TILES):
                        s = dve.bn_stats(stats[:, t, :], src[:, t, :])
                    own.done(s)
                    own.wait()
                    for t in range(ALL_TILES):
                        s = dve.bn_aggr(moments[:, i, t, :], stats[:, t, :])
                    own.done(s)
                    own.wait()
                    dve.tensor_copy(now[:, 0, i:i + 1], moments[:, i, 0, 0:1]).then_inc(S["stats_ready"], 1)

                def root_of(i):
                    dve.wait_ge(S["std_ready"], i + 1)
                    own.done(dve.reciprocal(rstd[:, i, 1, :], rstd[:, i, 0, :]))
                    own.wait()

                def normalise_input(i, b, out, src):
                    mom = moments[:, i + 1, :, :].rearrange("p (b q) c -> p b (q c)", b=BATCH)
                    rs = rstd[:, i + 1, 1, :].rearrange("p (b q) -> p b q", b=BATCH)
                    own.done(dve.tensor_copy(now[:, i, 0:8], flat(mom[:, one(b), :])))
                    own.done(dve.tensor_copy(now[:, i, 8:12], flat(rs[:, one(b), :])))
                    own.wait()
                    for q in range(TOK_TILES):
                        s = dve.tensor_scalar(out[:, q, :], src(q), now[:, i, 2 * q:2 * q + 1], now[:, i, 8 + q:9 + q], ALU.subtract, ALU.mult)
                    return s

                def ready_ctx(b):
                    dve.wait_ge(S["ctx_in"], b * 16 + 16)
                    normalise_input(1, b, ctx_raw, lambda q: ctx_raw[:, q, :]).then_inc(S["ctx_ready"], 1)

                zv = z1[:, :, :].rearrange("p (b q) d -> p b (q d)", b=BATCH)

                def ready_lat(b):
                    normalise_input(0, b, lat_b, lambda q: flat(zv[:, one(b), q * DIM:(q + 1) * DIM])).then_inc(S["lat_ready"], 1)

                ready_ctx(0)
                for t in range(ALL_TILES):
                    if t % TOK_TILES == 0:
                        dve.wait_ge(gathered[t // TOK_TILES], 16 * TOK_TILES)
                    s = dve.scalar_tensor_tensor(out=x_res[:, t, :], in0=y_tok[:, t, :], scalar=T["gate"][:, t:t + 1], in1=x_res[:, t, :],
                                                 op0=ALU.mult, op1=ALU.add)
                own.done(s)
                own.wait()
                stats_of(0, x_res)
                root_of(0)
                for t in range(ALL_TILES):
                    s = dve.tensor_scalar(z1[:, t, :], x_res[:, t, :], moments[:, 0, t, 0:1], rstd[:, 0, 1, t:t + 1], ALU.subtract, ALU.mult)
                own.done(s)
                own.wait()
                stats_of(1, z1)
                root_of(1)
                ready_lat(0)
                dve.wait_ge(S["ln_in"], 64 * DK)
                dve.wait_ge(S["half_zero"], 1)

                def copy_job(b, j):
                    kind, f, engines = JOBS[j]
                    if "d" not in engines:
                        return
                    bank = score_ps[:, j % 4, :]
                    dve.wait_ge(S["pro_mm"], b * N_JOBS + j + 1)
                    if kind == "lat":
                        s = dve.tensor_scalar(latT[:, f, :], bank, ln_col[:, 0, f:f + 1], ln_col[:, 1, f:f + 1], ALU.mult, ALU.add)
                    else:
                        s = dve.tensor_scalar(q_half[HD:P, 2 * f + 1, :], bank[HD:P, :], SCALE, None, ALU.mult)
                    s.then_inc(S["pro_dve"], 1)

                def normalise(b, g):
                    dve.wait_ge(S["sums"], b * PAIRS + g + 1)
                    own.done(dve.reciprocal(recip[:, :], sum_ps[:, g % 2, :]))
                    own.wait()
                    dve.tensor_tensor(oT[:, g, :], value_ps[:, g % 2, :], recip[:, :], ALU.mult).then_inc(S["normed"], 1)
                    dve.wait_ge(S["normed"], b * NORMED + g + 1)

                xv = x_res[:, :, :].rearrange("p (b q) d -> p b (q d)", b=BATCH)

                def body(b, first, last):
                    for j in range(N_JOBS):
                        copy_job(b, j)
                    if first:
                        dve.wait_ge(S["bo_in"], 16)
                        own.done(dve.tensor_tensor(x_res[:, :, :], x_res[:, :, :], bo[:, :].rearrange("p (a n) -> p a n", a=1)
                                                   .broadcast_to([P, ALL_TILES, DIM]), ALU.add))
                        own.wait()
                    for p in range(PAIRS + 2):
                        for k in range(TOK_TILES):
                            if p < PAIRS:
                                dve.wait_ge(S["exp"], b * STEPS + p * TOK_TILES + k + 1)
                                tile = prob[:, p % 2, k, :, :]
                                dve.tensor_scalar(tile, tile, LOW, HIGH, ALU.max, ALU.min).then_inc(S["clipped"], 1)
                            if k == 1 and p >= 2:
                                normalise(b, p - 2)
                        if p == 1 and not last:
                            ready_ctx(b + 1)
                            ready_lat(b + 1)
                    for h in range(2):
                        dve.wait_ge(S["wo_mm"], 2 * b + h + 1)
                        xq = flat(xv[:, one(b), h * 512:(h + 1) * 512])
                        dve.tensor_tensor(xq, value_ps[:, h, :], xq, ALU.add).then_inc(S["normed"], 1)

                over_batches(dve, own.over_turns(BATCH - 2, 2 + 2 + PAIRS, body))


HID = 1024
HID_TILES = HID // P
ROUND = 1.5 * 2.0 ** 23
QMAX = 127.0
RING = 8
SCALED_RING = 4


def ternary_ffn(nc, ctx_outer, T, A):
    with ExitStack() as ctx:
        def sb(name, shape, dt=F32):
            return ctx.enter_context(nc.sbuf_tensor("d_" + name, shape, dt))

        def sem(name):
            return ctx_outer.enter_context(nc.semaphore("d_" + name))

        wide_ps = [ctx.enter_context(nc.psum_tensor(f"d_wide{i}", [P, 512], F32)) for i in range(6)]
        bf_ps = [ctx.enter_context(nc.psum_tensor(f"d_bf{i}", [P, 1024], BF16)) for i in range(2)]
        x_res, ident = T["x_res"], T["ident"]

        w_tern = sb("w_tern", [P, 2, 2048], BF16)
        w1T = sb("w1T", [P, DK, HID], BF16)
        w2T = sb("w2T", [P, HID_TILES, DIM], BF16)
        ident_b = sb("ident_b", [P, P], BF16)
        ones = sb("ones", [P, P])
        tap_rows = sb("tap_rows", [HID_TILES, 4, P])
        tap_raw = sb("tap_raw", [HID_TILES, P * 3])
        taps = sb("taps", [P, 4, HID_TILES])
        w_sum = sb("w_sum", [P, 2])
        w_inv = sb("w_inv", [P, 2])
        w_scale = sb("w_scale", [P, 2])
        stats = sb("stats", [P, ALL_TILES, 6])
        moments = sb("moments", [P, ALL_TILES, 2])
        rstd = sb("rstd", [P, 2, ALL_TILES])
        tok = sb("tok", [P, 4, ALL_TILES])
        undo = sb("undo", [P, ALL_TILES * P])
        xq_b = sb("xq_b", [P, ALL_TILES, DIM], BF16)
        xqT = sb("xqT", [P, BATCH * DK, SEQ], BF16)
        h_pad = sb("h_pad", [P, RING, SEQ + 2])
        conv = sb("conv", [P, RING, SEQ])
        side = sb("side", [P, RING, SEQ])
        act_h = sb("act_h", [P, BATCH * HID_TILES, SEQ])
        up = sb("up", [P, SEQ])
        w_raw = flat(act_h[:, 24:32, :]).rearrange("p (i n) -> p i n", i=2)
        z = flat(act_h[:, 16:24, :]).rearrange("p (t d) -> p t d", d=DIM)
        spread = flat(act_h[:, 12:16, :]).rearrange("p (t n) -> p t n", n=P)
        top = sb("top", [P, SEQ])
        tok2 = sb("tok2", [P, 4, TOK_TILES])
        spread2 = sb("spread2", [P, TOK_TILES, P])
        scaled = sb("scaled", [P, SCALED_RING, SEQ])
        hq = sb("hq", [P, HID_TILES, SEQ], BF16)

        names = ("w_in taps_in ones_ready pads_zero w_summed w_total tern_ready w_turned wT_ready taps_turned taps_ready "
                 "stats_ready std_ready scales_ready half_scaled spread_ready undo_turned undo_ready xq_ready xq_turned xqT_ready h_mm h_ready centre side_added up_ready scaled_ready "
                 "conv_done silu top_done top_turned spread2_ready up_turned hq_ready y_mm y_added dve_own identb_ready").split()
        S = {n: sem(n) for n in names}
        HALF = ALL_TILES // 2

        AHEAD = 7
        TAP, TOP, TOP_TURN, TOKEN, UP_TURN, UP, SCALE, QUANT, DOWN, ADD = 4, 12, 13, 13, 14, 14, 14, 16, 20, 21

        def over_slots(eng, body):
            for s in range(-AHEAD, HID_TILES):
                body(0, s)
            with eng.Fori(1, BATCH - 1) as t:
                for s in range(HID_TILES):
                    body(t, s)
            for s in range(ADD + 1 - AHEAD):
                body(BATCH - 1, s)

        def due(t, s, lag, every=True):
            n = AHEAD + s - lag
            c, f = t + n // HID_TILES, n % HID_TILES
            if (isinstance(t, int) and not 0 <= c < BATCH) or (f and not every):
                return None, None
            return c, f

        def wait_after(eng, name, count):
            if not isinstance(count, int) or count > 0:
                eng.wait_ge(S[name], count)

        with nc.Block() as block:
            @block.sync
            def _(sp):
                sp.dma_start(w_raw[:, 0, :].rearrange("p (f d) -> p f d", d=DIM), A["L1_ffn_w1"].rearrange("(f p) d -> p f d", p=P)).then_inc(S["w_in"], 16)
                sp.dma_start(w_raw[:, 1, :].rearrange("p (o h) -> p o h", h=HID), A["L1_ffn_w2"].rearrange("(o p) h -> p o h", p=P)).then_inc(S["w_in"], 16)
                sp.dma_start(tap_raw[:, :], A["L1_ffn_conv_w"].rearrange("(f p) a j -> f (p a j)", p=P)).then_inc(S["taps_in"], 16)
                sp.dma_start(tap_rows[:, 3, :], A["L1_ffn_conv_b"].rearrange("(f p) -> f p", p=P)).then_inc(S["taps_in"], 16)

            @block.gpsimd
            def _(pool):
                pool.memset(ones[:, :], 1.0).then_inc(S["ones_ready"], 1)
                pool.memset(h_pad[:, :, :], 0.0).then_inc(S["pads_zero"], 1)
                pool.wait_ge(S["scales_ready"], 1)
                for t in range(HALF, ALL_TILES):
                    m = pool.tensor_scalar(z[:, t, :], z[:, t, :], tok[:, 2, t:t + 1], ROUND, ALU.mult, ALU.add)
                m.then_inc(S["half_scaled"], 1)

                def body(t, s):
                    c, f = due(t, s, 0)
                    if f is not None:
                        tile = conv[:, f % RING, :]
                        pool.wait_ge(S["centre"], c * HID_TILES + f + 1)
                        pool.tensor_tensor(tile, tile, side[:, f % RING, :], ALU.add).then_inc(S["side_added"], 1)
                    c, f = due(t, s, SCALE)
                    if f is not None and f < HID_TILES // 2:
                        if f == 0:
                            pool.wait_ge(S["up_ready"], c + 1)
                        g = 2 * f
                        if g >= SCALED_RING:
                            pool.wait_ge(S["hq_ready"], c * HID_TILES + g - SCALED_RING + 1)
                        pool.tensor_tensor(scaled[:, g % SCALED_RING, :], up[:, :], flat(act_h[:, bass.ds(c * HID_TILES + g, 1), :]), ALU.mult
                                           ).then_inc(S["scaled_ready"], 1)

                over_slots(pool, body)

            @block.tensor
            def _(pe):
                pe.wait_ge(S["taps_in"], 32)
                pe.wait_ge(S["taps_turned"], 1)
                for j in range(4):
                    mm = pe.transpose(wide_ps[0][:, j * HID_TILES:(j + 1) * HID_TILES], tap_rows[:, j, :], ident[0:HID_TILES, 0:HID_TILES])
                mm.then_inc(S["taps_turned"], 1)
                pe.wait_ge(S["ones_ready"], 1)
                pe.wait_ge(S["w_summed"], 2)
                pe.matmul(wide_ps[1][:, 0:2], ones[:, :], w_sum[:, :], start=True, stop=True).then_inc(S["w_total"], 1)
                pe.wait_ge(S["spread_ready"], 1)
                for b in range(BATCH):
                    for q in range(TOK_TILES):
                        mm = pe.transpose(wide_ps[2 + b][:, q * P:(q + 1) * P], spread[:, b * TOK_TILES + q, :], ident[:, :])
                    mm.then_inc(S["undo_turned"], 1)
                pe.wait_ge(S["xq_ready"], 1)
                for b in range(BATCH):
                    if b >= 2:
                        pe.wait_ge(S["xqT_ready"], b - 1)
                    for k in range(DK):
                        for q in range(TOK_TILES):
                            mm = pe.transpose(bf_ps[b % 2][:, (k * TOK_TILES + q) * P:(k * TOK_TILES + q + 1) * P],
                                              xq_b[:, b * TOK_TILES + q, k * P:(k + 1) * P], ident_b[:, :])
                    mm.then_inc(S["xq_turned"], 1)
                pe.wait_ge(S["xqT_ready"], BATCH)
                pe.wait_ge(S["tern_ready"], 1)
                for o in range(DK):
                    for f in range(HID_TILES):
                        mm = pe.transpose(bf_ps[o][:, f * P:(f + 1) * P], w_tern[:, 1, o * HID + f * P:o * HID + (f + 1) * P], ident_b[:, :])
                mm.then_inc(S["w_turned"], 1)
                pe.wait_ge(S["tern_ready"], 2)
                pe.wait_ge(S["wT_ready"], 1)
                for k in range(DK):
                    for f in range(HID_TILES):
                        mm = pe.transpose(bf_ps[k][:, f * P:(f + 1) * P], w_tern[:, 0, f * DIM + k * P:f * DIM + (k + 1) * P], ident_b[:, :])
                mm.then_inc(S["w_turned"], 1)
                pe.wait_ge(S["wT_ready"], 2)
                pe.wait_ge(S["undo_ready"], 1)
                pe.wait_ge(S["taps_ready"], 1)

                def body(t, s):
                    c, f = due(t, s, 0)
                    if f is not None:
                        wait_after(pe, "h_ready", c * HID_TILES + f - 1)
                        for k in range(DK):
                            mm = pe.matmul(wide_ps[f % 2][:, :], w1T[:, k, f * P:(f + 1) * P], flat(xqT[:, bass.ds(c * DK + k, 1), :]), start=k == 0, stop=k == DK - 1)
                        mm.then_inc(S["h_mm"], 1)
                    c, _ = due(t, s, TOP_TURN, False)
                    if c is not None:
                        pe.wait_ge(S["top_done"], c + 1)
                        for q in range(TOK_TILES):
                            mm = pe.transpose(wide_ps[2][:, q * P:(q + 1) * P], top[:, q * P:(q + 1) * P], ident[:, :])
                        mm.then_inc(S["top_turned"], 1)
                    c, _ = due(t, s, UP_TURN, False)
                    if c is not None:
                        pe.wait_ge(S["spread2_ready"], c + 1)
                        for q in range(TOK_TILES):
                            mm = pe.transpose(wide_ps[3][:, q * P:(q + 1) * P], spread2[:, q, :], ident[:, :])
                        mm.then_inc(S["up_turned"], 1)
                    c, _ = due(t, s, DOWN, False)
                    if c is not None:
                        pe.wait_ge(S["hq_ready"], (c + 1) * HID_TILES)
                        for q in range(TOK_TILES):
                            for f in range(HID_TILES):
                                mm = pe.matmul(wide_ps[4 + q // 2][:, (q % 2) * DIM:(q % 2 + 1) * DIM], hq[:, f, q * P:(q + 1) * P], w2T[:, f, :],
                                               start=f == 0, stop=f == HID_TILES - 1)
                            if q % 2:
                                mm.then_inc(S["y_mm"], 1)

                over_slots(pe, body)

            @block.scalar
            def _(act):
                act.wait_ge(S["stats_ready"], 1)
                act.activation(rstd[:, 0, :], moments[:, :, 1], ACT.Sqrt, bias=T["eps"][:, :]).then_inc(S["std_ready"], 1)
                act.wait_ge(S["w_in"], 32)
                for i in range(2):
                    act.activation(flat(act_h[:, 0:4, :]), w_raw[:, i, :], ACT.Abs, accum_out=w_sum[:, i:i + 1]).then_inc(S["w_summed"], 1)
                    act.wait_ge(S["w_summed"], i + 1)
                for b in range(BATCH):
                    act.wait_ge(S["undo_turned"], b + 1)
                    s = act.copy(undo[:, b * SEQ:(b + 1) * SEQ], wide_ps[2 + b][:, :])
                s.then_inc(S["undo_ready"], 1)
                for b in range(BATCH):
                    act.wait_ge(S["xq_turned"], b + 1)
                    act.copy(flat(xqT[:, b * DK:(b + 1) * DK, :]), bf_ps[b % 2][:, :]).then_inc(S["xqT_ready"], 1)
                act.wait_ge(S["w_turned"], 1)
                for o in range(DK):
                    s = act.copy(w2T[:, :, o * P:(o + 1) * P], bf_ps[o][:, :].rearrange("p (f n) -> p f n", n=P))
                s.then_inc(S["wT_ready"], 1)
                act.wait_ge(S["w_turned"], 2)
                for k in range(DK):
                    s = act.copy(w1T[:, k, :], bf_ps[k][:, :])
                s.then_inc(S["wT_ready"], 1)
                act.wait_ge(S["taps_ready"], 1)
                act.wait_ge(S["pads_zero"], 1)

                def body(t, s):
                    c, f = due(t, s, 0)
                    if f is not None:
                        n = c * HID_TILES + f
                        act.wait_ge(S["h_ready"], n + 1)
                        wait_after(act, "silu", n - RING + 1)
                        act.activation(conv[:, f % RING, :], h_pad[:, f % RING, 1:SEQ + 1], ACT.Identity, scale=taps[:, 1, f:f + 1], bias=taps[:, 3, f:f + 1])
                        act.activation(side[:, f % RING, :], h_pad[:, f % RING, 0:SEQ], ACT.Copy, scale=taps[:, 0, f:f + 1]).then_inc(S["centre"], 1)
                    c, _ = due(t, s, UP, False)
                    if c is not None:
                        act.wait_ge(S["up_turned"], c + 1)
                        act.copy(up[:, :], wide_ps[3][:, :]).then_inc(S["up_ready"], 1)
                    c, f = due(t, s, TAP)
                    if f is not None:
                        act.wait_ge(S["conv_done"], c * HID_TILES + f + 1)
                        act.activation(flat(act_h[:, bass.ds(c * HID_TILES + f, 1), :]), conv[:, f % RING, :], ACT.Silu).then_inc(S["silu"], 1)

                over_slots(act, body)

            @block.vector
            def _(dve):
                own = Steps(dve, S["dve_own"])

                def do(instruction):
                    own.done(instruction)
                    own.wait()

                dve.tensor_copy(ident_b[:, :], ident[:, :]).then_inc(S["identb_ready"], 1)
                s = layernorm_all(dve, own, S["stats_ready"], S["std_ready"], 1, x_res, stats, moments, rstd, z)
                do(s)
                dve.wait_ge(S["taps_in"], 32)
                for j in range(3):
                    s = dve.tensor_copy(tap_rows[:, j, :], tap_raw[:, :].rearrange("f (p j) -> f j p", j=3)[:, j, :])
                s.then_inc(S["taps_turned"], 1)
                do(dve.tensor_reduce(tok[:, 0, :], z[:, :, :], AX.X, ALU.max, apply_absolute_value=True))
                do(dve.tensor_scalar(tok[:, 0, :], tok[:, 0, :], 1e-5, None, ALU.max))
                dve.tensor_scalar(tok[:, 3, :], tok[:, 0, :], 1.0 / QMAX, None, ALU.mult)
                do(dve.reciprocal(tok[:, 1, :], tok[:, 0, :]))
                dve.tensor_scalar(tok[:, 2, :], tok[:, 1, :], QMAX, None, ALU.mult).then_inc(S["scales_ready"], 1)
                dve.wait_ge(S["scales_ready"], 1)
                dve.wait_ge(S["ones_ready"], 1)
                dve.tensor_tensor(spread[:, :, :], ones[:, :].rearrange("p (a n) -> p a n", a=1).broadcast_to([P, ALL_TILES, P]),
                                  tok[:, 3, :].rearrange("p (t a) -> p t a", a=1).broadcast_to([P, ALL_TILES, P]), ALU.mult).then_inc(S["spread_ready"], 1)
                for t in range(HALF):
                    s = dve.tensor_scalar(z[:, t, :], z[:, t, :], tok[:, 2, t:t + 1], ROUND, ALU.mult, ALU.add)
                own.done(s)
                own.wait()
                dve.wait_ge(S["half_scaled"], 1)
                dve.tensor_scalar(xq_b[:, :, :], z[:, :, :], ROUND, None, ALU.subtract).then_inc(S["xq_ready"], 1)
                dve.wait_ge(S["w_total"], 1)
                do(dve.tensor_scalar(w_inv[:, :], wide_ps[1][:, 0:2], 1.0 / (HID * DIM), 1e-5, ALU.mult, ALU.max))
                do(dve.reciprocal(w_scale[:, :], w_inv[:, :]))
                for i in (1, 0):
                    do(dve.tensor_scalar(w_raw[:, i, :], w_raw[:, i, :], w_scale[:, i:i + 1], ROUND, ALU.mult, ALU.add))
                    do(dve.tensor_scalar(w_raw[:, i, :], w_raw[:, i, :], ROUND + 1.0, ROUND - 1.0, ALU.min, ALU.max))
                    dve.tensor_scalar(w_tern[:, i, :], w_raw[:, i, :], ROUND, None, ALU.subtract).then_inc(S["tern_ready"], 1)
                dve.wait_ge(S["taps_turned"], 2)
                do(dve.tensor_scalar(taps[:, 0:3, :].rearrange("p j f -> p (j f)"), wide_ps[0][:, 0:3 * HID_TILES], w_inv[:, 0:1], None, ALU.mult))
                dve.tensor_copy(taps[:, 3, :], wide_ps[0][:, 3 * HID_TILES:4 * HID_TILES]).then_inc(S["taps_ready"], 1)
                dve.wait_ge(S["taps_ready"], 1)
                dve.wait_ge(S["pads_zero"], 1)
                dve.wait_ge(S["undo_ready"], 1)
                xv = x_res[:, :, :].rearrange("p (b q) d -> p b (q d)", b=BATCH)

                def token_scales(c):
                    dve.wait_ge(S["top_turned"], c + 1)
                    do(dve.tensor_reduce(tok2[:, 0, :], wide_ps[2][:, :].rearrange("p (q n) -> p q n", n=P), AX.X, ALU.max))
                    do(dve.tensor_scalar(tok2[:, 0, :], tok2[:, 0, :], 1e-5, None, ALU.max))
                    dve.tensor_scalar(tok2[:, 3, :], tok2[:, 0, :], w_inv[:, 1:2], 1.0 / QMAX, ALU.mult, ALU.mult)
                    do(dve.reciprocal(tok2[:, 1, :], tok2[:, 0, :]))
                    do(dve.tensor_scalar(tok2[:, 2, :], tok2[:, 1, :], QMAX, None, ALU.mult))
                    dve.tensor_tensor(spread2[:, :, :], ones[:, :].rearrange("p (a n) -> p a n", a=1).broadcast_to([P, TOK_TILES, P]),
                                      tok2[:, 2, :].rearrange("p (t a) -> p t a", a=1).broadcast_to([P, TOK_TILES, P]), ALU.mult).then_inc(S["spread2_ready"], 1)

                def body(t, s):
                    c, f = due(t, s, 0)
                    if f is not None:
                        n = c * HID_TILES + f
                        dve.wait_ge(S["h_mm"], n + 1)
                        wait_after(dve, "conv_done", n - RING + 1)
                        dve.tensor_tensor(h_pad[:, f % RING, 1:SEQ + 1], wide_ps[f % 2][:, :], undo[:, bass.ds(c * SEQ, SEQ)], ALU.mult).then_inc(S["h_ready"], 1)
                    c, f = due(t, s, TAP)
                    if f is not None:
                        tile = conv[:, f % RING, :]
                        dve.wait_ge(S["side_added"], c * HID_TILES + f + 1)
                        dve.scalar_tensor_tensor(out=tile, in0=h_pad[:, f % RING, 2:SEQ + 2], scalar=taps[:, 2, f:f + 1], in1=tile,
                                                 op0=ALU.mult, op1=ALU.add).then_inc(S["conv_done"], 1)
                    c, _ = due(t, s, ADD, False)
                    if c is not None:
                        for q in range(TOK_TILES):
                            dve.wait_ge(S["y_mm"], 2 * c + q // 2 + 1)
                            xq = flat(xv[:, bass.ds(c, 1), q * DIM:(q + 1) * DIM])
                            dve.scalar_tensor_tensor(out=xq, in0=wide_ps[4 + q // 2][:, (q % 2) * DIM:(q % 2 + 1) * DIM], scalar=tok2[:, 3, q:q + 1], in1=xq,
                                                     op0=ALU.mult, op1=ALU.add).then_inc(S["y_added"], 1)
                    c, _ = due(t, s, TOP, False)
                    if c is not None:
                        dve.wait_ge(S["silu"], (c + 1) * HID_TILES)
                        dve.tensor_reduce(top[:, :], act_h[:, bass.ds(c * HID_TILES, HID_TILES), :].rearrange("p f n -> p n f"), AX.X, ALU.max,
                                          apply_absolute_value=True).then_inc(S["top_done"], 1)
                    c, _ = due(t, s, TOKEN, False)
                    if c is not None:
                        token_scales(c)
                    c, f = due(t, s, QUANT)
                    if f is not None and f < HID_TILES // 2:
                        g = 2 * f
                        if g == 0:
                            dve.wait_ge(S["up_ready"], c + 1)
                        if g >= SCALED_RING:
                            dve.wait_ge(S["hq_ready"], c * HID_TILES + g - SCALED_RING + 2)
                        own.done(dve.tensor_tensor(scaled[:, (g + 1) % SCALED_RING, :], up[:, :], flat(act_h[:, bass.ds(c * HID_TILES + g + 1, 1), :]), ALU.mult))
                        dve.wait_ge(S["scaled_ready"], c * (HID_TILES // 2) + f + 1)
                        dve.tensor_scalar(hq[:, g, :], scaled[:, g % SCALED_RING, :], ROUND, ROUND, ALU.add, ALU.subtract).then_inc(S["hq_ready"], 1)
                        own.wait()
                        dve.tensor_scalar(hq[:, g + 1, :], scaled[:, (g + 1) % SCALED_RING, :], ROUND, ROUND, ALU.add, ALU.subtract).then_inc(S["hq_ready"], 1)

                def counted(t, s):
                    if isinstance(t, int):
                        body(t, s)
                    else:
                        if s == 0:
                            own.loop(t, STEPS_D, 1)
                        body(t, s)
                        if s == HID_TILES - 1:
                            own.end_loop(BATCH - 2)

                over_slots(dve, counted)
                dve.wait_ge(S["y_added"], BATCH * TOK_TILES)


STEPS_D = 8


def program(nc, A, out):
    with ExitStack() as ctx:
        T = {}
        T["x_res"] = ctx.enter_context(nc.sbuf_tensor("x_res", [P, ALL_TILES, DIM], F32))
        T["ident"] = ctx.enter_context(nc.sbuf_tensor("ident", [P, P], F32))
        T["eps"] = ctx.enter_context(nc.sbuf_tensor("eps", [P, 1], F32))
        T["slot"] = ctx.enter_context(nc.sbuf_tensor("slot", [P, ALL_TILES], I32))
        T["gate"] = ctx.enter_context(nc.sbuf_tensor("gate", [P, ALL_TILES], F32))
        T["moments"] = ctx.enter_context(nc.sbuf_tensor("moments", [P, 3, ALL_TILES, 2], F32))
        T["rstd"] = ctx.enter_context(nc.sbuf_tensor("rstd", [P, 3, 2, ALL_TILES], F32))
        T["zeros"] = ctx.enter_context(nc.sbuf_tensor("zeros", [P, DIM], F32))
        T["slots_zeroed"] = ctx.enter_context(nc.semaphore("slots_zeroed"))
        T["x_sorted"] = nc.dram_tensor("x_sorted", (FETCHED_TILES * P, DIM), F32, kind="Internal").ap()
        T["zero_count"] = 16 * FETCHED_TILES
        T["ident_ready"] = ctx.enter_context(nc.semaphore("ident_ready"))
        T["stored"] = ctx.enter_context(nc.semaphore("stored"))
        T["ident_count"] = 2
        with nc.Block() as block:
            @block.gpsimd
            def _(pool):
                pool.memset(T["ident"][:, :], 0.0).then_inc(T["ident_ready"], 1)
                pool.memset(T["eps"][:, :], EPS)
                pool.memset(T["zeros"][:, :], 0.0)
                pool.wait_ge(T["ident_ready"], 1)
                pool.affine_select(out=T["ident"][:, :], in_=T["ident"][:, :], compare_op=ALU.not_equal, fill=1.0, base=0,
                                   pattern=[[-1, P]], channel_multiplier=1).then_inc(T["ident_ready"], 1)
        diff_attention(nc, ctx, T, A)
        experts(nc, ctx, T, A)
        cross_attention(nc, ctx, T, A)
        ternary_ffn(nc, ctx, T, A)
        with nc.Block() as block:
            @block.sync
            def _(sp):
                sp.dma_start(out.rearrange("b (q p) d -> p (b q) d", p=P), T["x_res"][:, :, :]).then_inc(T["stored"], 16)
                sp.wait_ge(T["stored"], 16)


_OUT = (BATCH, SEQ, DIM)


def kernel(**inputs):
    import concourse.bacc as bacc
    from concourse.bass_utils import run_bass_kernel_spmd

    nc = bacc.Bacc("TRN2", target_bir_lowering=False, num_devices=1)
    arrays, args = {}, {}
    for name, value in inputs.items():
        a = np.ascontiguousarray(value)
        arrays[f"in_{name}_dram"] = a
        args[name] = nc.dram_tensor(f"in_{name}_dram", a.shape, mybir.dt.from_np(a.dtype), kind="ExternalInput").ap()
    out = nc.dram_tensor("out_0_dram", _OUT, F32, kind="ExternalOutput").ap()
    program(nc, args, out)
    r = run_bass_kernel_spmd(nc, [arrays], core_ids=[0])
    return r.results[0]["out_0_dram"]
```
